# Optimizing a Trainium2 kernel written in Bass

```python
import numpy as np
import jax
import jax.numpy as jnp

def _softmax(x, axis=-1):
    return jax.nn.softmax(x, axis=axis)

def _gelu(x):
    return jax.nn.gelu(x, approximate=True)

def _silu(x):
    return jax.nn.silu(x)

def _sigmoid(x):
    return jax.nn.sigmoid(x)

def _layernorm(x, axis=-1, eps=1e-05):
    m = jnp.mean(x, axis=axis, keepdims=True)
    v = jnp.var(x, axis=axis, keepdims=True)
    return (x - m) / jnp.sqrt(v + eps)

def _scatter_add(tgt, idx, src, axis=0):
    return tgt.at[idx].add(src)

def _segment_sum(src, seg, n):
    return jax.ops.segment_sum(src, seg, n)
kernel_name = 'mk_xattn_ffn_d2_seqx_r4_bbebcb'

def setup_inputs(seed: int=0):
    np.random.seed(seed)
    _w = jnp.asarray

    def _rec_inputs():
        import jax
        import jax.numpy as jnp
        _rk = jax.random.key(seed)
        x = 0.002226 + 0.9996 * jax.random.normal(jax.random.fold_in(_rk, 1), (2, 1024, 256), jnp.float32)
        _lenS = 1024 - jax.random.randint(jax.random.fold_in(_rk, 7), (2,), 0, max(1, 1024 // 4) + 1, jnp.int32)
        _lenS2 = 77 - jax.random.randint(jax.random.fold_in(_rk, 8), (2,), 0, max(1, 77 // 4) + 1, jnp.int32)
        _ctx_1024P = jax.random.normal(jax.random.fold_in(_rk, 11), (2, 16, 256), jnp.float32)
        _ctx_1024c = jax.random.dirichlet(jax.random.fold_in(_rk, 511), 0.3 * jnp.ones((16,), jnp.float32), (2, 77))
        _ctx_1024t = jnp.einsum('bsk,bkd->bsd', _ctx_1024c, _ctx_1024P)
        _ctx_1024t = _ctx_1024t * jax.lax.rsqrt(jnp.mean(jnp.square(_ctx_1024t)) + 1e-12) * 0.953939
        ctx_1024 = -0.000125008 + 0.999885 * (_ctx_1024t + 0.3 * jax.random.normal(jax.random.fold_in(_rk, 611), (2, 77, 256), jnp.float32))
        return (x, ctx_1024)
    x, ctx_1024 = _rec_inputs()

    def _L0_xattn_setup():
        import jax, jax.numpy as jnp
        import numpy as np
        DIM = 256
        HEADS = 16
        DIM_HEAD = 64
        INNER = HEADS * DIM_HEAD
        EPS = 1e-05

        def _layernorm(t, w, b):
            mu = jnp.mean(t, axis=-1, keepdims=True)
            var = jnp.mean(jnp.square(t - mu), axis=-1, keepdims=True)
            return (t - mu) * jax.lax.rsqrt(var + EPS) * w + b
        key = jax.random.key(seed)
        ks = jax.random.split(key, 8)
        b, n, l = (8, 1024, 64)
        x = jax.random.normal(ks[0], (b, n, DIM), dtype=jnp.float32)
        latents = jax.random.normal(ks[1], (b, l, DIM), dtype=jnp.float32)
        ln1_w = jnp.ones((DIM,), jnp.float32)
        ln1_b = jnp.zeros((DIM,), jnp.float32)
        ln2_w = jnp.ones((DIM,), jnp.float32)
        ln2_b = jnp.zeros((DIM,), jnp.float32)
        Wq = jax.random.normal(ks[2], (DIM, INNER), dtype=jnp.float32) / np.sqrt(DIM)
        Wkv = jax.random.normal(ks[3], (DIM, 2 * INNER), dtype=jnp.float32) / np.sqrt(DIM)
        Wo = jax.random.normal(ks[4], (INNER, DIM), dtype=jnp.float32) / np.sqrt(INNER)
        return {'x': x, 'latents': latents, 'ln1_w': ln1_w, 'ln1_b': ln1_b, 'ln2_w': ln2_w, 'ln2_b': ln2_b, 'Wq': Wq, 'Wkv': Wkv, 'Wo': Wo}
    _L0_xattn_all = _L0_xattn_setup()
    _L0_xattn_in = {k: v for k, v in _L0_xattn_all.items() if k in ('ln1_w', 'ln1_b', 'ln2_w', 'ln2_b', 'Wq', 'Wkv', 'Wo')}
    del _L0_xattn_all

    def _L0_ffn_setup():
        import jax, jax.numpy as jnp
        import numpy as np
        B, S, D, F, E = (2, 512, 256, 1024, 8)
        LN_EPS = 1e-05

        def _layer_norm(x, gamma, beta):
            mu = jnp.mean(x, axis=-1, keepdims=True)
            var = jnp.mean(jnp.square(x - mu), axis=-1, keepdims=True)
            return (x - mu) * jax.lax.rsqrt(var + LN_EPS) * gamma + beta
        key = jax.random.key(seed)
        ks = jax.random.split(key, 8)

        def xavier(k, shape):
            fan_in, fan_out = (shape[-1], shape[-2])
            a = jnp.sqrt(6.0 / (fan_in + fan_out))
            return jax.random.uniform(k, shape, jnp.float32, -a, a)
        return {'tgt': jax.random.normal(ks[0], (B, S, D), jnp.float32), 'Wr': xavier(ks[1], (E, D)), 'br': jnp.zeros((E,), jnp.float32), 'W1': xavier(ks[2], (E, F, D)), 'b1': jnp.zeros((E, F), jnp.float32), 'W2': xavier(ks[3], (E, D, F)), 'b2': jnp.zeros((E, D), jnp.float32), 'gamma': jnp.ones((D,), jnp.float32), 'beta': jnp.zeros((D,), jnp.float32)}
    _L0_ffn_all = _L0_ffn_setup()
    _L0_ffn_in = {k: v for k, v in _L0_ffn_all.items() if k in ('Wr', 'br', 'W1', 'b1', 'W2', 'b2', 'gamma', 'beta')}
    del _L0_ffn_all

    def _L1_xattn_setup():
        import jax, jax.numpy as jnp
        import numpy as np
        import math
        D_MODEL = 256
        N_HEADS = 16
        key = jax.random.key(seed)
        ks = jax.random.split(key, 11)
        N, L, S = (2, 512, 512)
        d = D_MODEL
        s = 1.0 / math.sqrt(d)
        return {'queries': jax.random.normal(ks[0], (N, L, d), dtype=jnp.float32), 'keys': jax.random.normal(ks[1], (N, S, d), dtype=jnp.float32), 'values': jax.random.normal(ks[2], (N, S, d), dtype=jnp.float32), 'Wq': jax.random.normal(ks[3], (d, d), dtype=jnp.float32) * s, 'bq': jax.random.normal(ks[4], (d,), dtype=jnp.float32) * s, 'Wk': jax.random.normal(ks[5], (d, d), dtype=jnp.float32) * s, 'bk': jax.random.normal(ks[6], (d,), dtype=jnp.float32) * s, 'Wv': jax.random.normal(ks[7], (d, d), dtype=jnp.float32) * s, 'bv': jax.random.normal(ks[8], (d,), dtype=jnp.float32) * s, 'Wo': jax.random.normal(ks[9], (d, d), dtype=jnp.float32) * s, 'bo': jax.random.normal(ks[10], (d,), dtype=jnp.float32) * s}
    _L1_xattn_all = _L1_xattn_setup()
    _L1_xattn_in = {k: v for k, v in _L1_xattn_all.items() if k in ('Wq', 'bq', 'Wk', 'bk', 'Wv', 'bv', 'Wo', 'bo')}
    del _L1_xattn_all

    def _L1_ffn_setup():
        import jax, jax.numpy as jnp
        import numpy as np
        from jax import lax
        H = 256
        E = 8
        E_MLP = E - 4
        TOP_K = 2
        I = 128
        KC = 4
        SHARED_SCALE = 1.0
        key = jax.random.key(seed)
        ks = jax.random.split(key, 8)
        B, S = (4, 1024)
        s_h = 1.0 / np.sqrt(H)
        s_i = 1.0 / np.sqrt(I)
        return {'hidden_states': jax.random.normal(ks[0], (B, S, H), dtype=jnp.float32), 'Wr': jax.random.normal(ks[1], (H, E), dtype=jnp.float32) * s_h, 'router_bias': jnp.zeros((E,), dtype=jnp.float32), 'Wg': jax.random.normal(ks[2], (E_MLP, H, I), dtype=jnp.float32) * s_h, 'Wu': jax.random.normal(ks[3], (E_MLP, H, I), dtype=jnp.float32) * s_h, 'Wd': jax.random.normal(ks[4], (E_MLP, I, H), dtype=jnp.float32) * s_i, 'conv_w': jax.random.normal(ks[5], (KC, 1, H), dtype=jnp.float32) * (1.0 / np.sqrt(KC)), 'conv_b': jnp.zeros((H,), dtype=jnp.float32)}
    _L1_ffn_all = _L1_ffn_setup()
    _L1_ffn_in = {k: v for k, v in _L1_ffn_all.items() if k in ('Wr', 'router_bias', 'Wg', 'Wu', 'Wd', 'conv_w', 'conv_b')}
    del _L1_ffn_all
    return {'x': x, 'ctx_1024': ctx_1024, 'L0_xattn_ln1_w': _L0_xattn_in['ln1_w'], 'L0_xattn_ln1_b': _L0_xattn_in['ln1_b'], 'L0_xattn_ln2_w': _L0_xattn_in['ln2_w'], 'L0_xattn_ln2_b': _L0_xattn_in['ln2_b'], 'L0_xattn_Wq': _L0_xattn_in['Wq'], 'L0_xattn_Wkv': _L0_xattn_in['Wkv'], 'L0_xattn_Wo': _L0_xattn_in['Wo'], 'L0_ffn_Wr': _L0_ffn_in['Wr'], 'L0_ffn_br': _L0_ffn_in['br'], 'L0_ffn_W1': _L0_ffn_in['W1'], 'L0_ffn_b1': _L0_ffn_in['b1'], 'L0_ffn_W2': _L0_ffn_in['W2'], 'L0_ffn_b2': _L0_ffn_in['b2'], 'L0_ffn_gamma': _L0_ffn_in['gamma'], 'L0_ffn_beta': _L0_ffn_in['beta'], 'L1_xattn_Wq': _L1_xattn_in['Wq'], 'L1_xattn_bq': _L1_xattn_in['bq'], 'L1_xattn_Wk': _L1_xattn_in['Wk'], 'L1_xattn_bk': _L1_xattn_in['bk'], 'L1_xattn_Wv': _L1_xattn_in['Wv'], 'L1_xattn_bv': _L1_xattn_in['bv'], 'L1_xattn_Wo': _L1_xattn_in['Wo'], 'L1_xattn_bo': _L1_xattn_in['bo'], 'L1_ffn_Wr': _L1_ffn_in['Wr'], 'L1_ffn_router_bias': _L1_ffn_in['router_bias'], 'L1_ffn_Wg': _L1_ffn_in['Wg'], 'L1_ffn_Wu': _L1_ffn_in['Wu'], 'L1_ffn_Wd': _L1_ffn_in['Wd'], 'L1_ffn_conv_w': _L1_ffn_in['conv_w'], 'L1_ffn_conv_b': _L1_ffn_in['conv_b']}

def reference(x, ctx_1024, L0_xattn_ln1_w, L0_xattn_ln1_b, L0_xattn_ln2_w, L0_xattn_ln2_b, L0_xattn_Wq, L0_xattn_Wkv, L0_xattn_Wo, L0_ffn_Wr, L0_ffn_br, L0_ffn_W1, L0_ffn_b1, L0_ffn_W2, L0_ffn_b2, L0_ffn_gamma, L0_ffn_beta, L1_xattn_Wq, L1_xattn_bq, L1_xattn_Wk, L1_xattn_bk, L1_xattn_Wv, L1_xattn_bv, L1_xattn_Wo, L1_xattn_bo, L1_ffn_Wr, L1_ffn_router_bias, L1_ffn_Wg, L1_ffn_Wu, L1_ffn_Wd, L1_ffn_conv_w, L1_ffn_conv_b):
    import jax
    import jax.numpy as jnp

    def _L0_xattn_ref(x, latents, ln1_w, ln1_b, ln2_w, ln2_b, Wq, Wkv, Wo):
        import jax, jax.numpy as jnp
        import numpy as np
        DIM = 256
        HEADS = 16
        DIM_HEAD = 64
        INNER = HEADS * DIM_HEAD
        EPS = 1e-05

        def _layernorm(t, w, b):
            mu = jnp.mean(t, axis=-1, keepdims=True)
            var = jnp.mean(jnp.square(t - mu), axis=-1, keepdims=True)
            return (t - mu) * jax.lax.rsqrt(var + EPS) * w + b
        xn = _layernorm(x, ln1_w, ln1_b)
        latn = _layernorm(latents, ln2_w, ln2_b)
        b, l, _ = latn.shape
        q = latn @ Wq
        kv_input = jnp.concatenate([xn, latn], axis=1)
        kv = kv_input @ Wkv
        k, v = jnp.split(kv, 2, axis=-1)

        def heads(t):
            return t.reshape(t.shape[0], t.shape[1], HEADS, DIM_HEAD).transpose(0, 2, 1, 3)
        q, k, v = (heads(q), heads(k), heads(v))
        scale = 1.0 / np.sqrt(np.sqrt(DIM_HEAD))
        weight = jnp.einsum('bhld,bhnd->bhln', q * scale, k * scale)
        weight = jax.nn.softmax(weight.astype(jnp.float32), axis=-1).astype(weight.dtype)
        out = jnp.einsum('bhln,bhnd->bhld', weight, v)
        out = out.transpose(0, 2, 1, 3).reshape(b, l, INNER)
        return out @ Wo

    def _L0_ffn_ref(tgt, Wr, br, W1, b1, W2, b2, gamma, beta):
        import jax, jax.numpy as jnp
        import numpy as np
        B, S, D, F, E = (2, 512, 256, 1024, 8)
        LN_EPS = 1e-05

        def _layer_norm(x, gamma, beta):
            mu = jnp.mean(x, axis=-1, keepdims=True)
            var = jnp.mean(jnp.square(x - mu), axis=-1, keepdims=True)
            return (x - mu) * jax.lax.rsqrt(var + LN_EPS) * gamma + beta
        logits = jnp.einsum('bsd,ed->bse', tgt, Wr) + br
        top_v, top_i = jax.lax.top_k(logits, 2)
        top_w = jax.nn.softmax(top_v, axis=-1)
        n_exp = logits.shape[-1]
        router_w = jnp.sum(jax.nn.one_hot(top_i, n_exp, dtype=top_w.dtype) * top_w[..., None], axis=-2)
        h = jnp.einsum('bsd,efd->bsef', tgt, W1) + b1
        h = jax.nn.relu(h)
        o = jnp.einsum('bsef,edf->bsed', h, W2) + b2
        tgt2 = jnp.einsum('bsed,bse->bsd', o, router_w)
        return _layer_norm(tgt + tgt2, gamma, beta)

    def _L1_xattn_ref(queries, keys, values, Wq, bq, Wk, bk, Wv, bv, Wo, bo):
        import jax, jax.numpy as jnp
        import numpy as np
        import math
        D_MODEL = 256
        N_HEADS = 16
        N, L, _ = queries.shape
        S = keys.shape[1]
        H = N_HEADS
        q = (queries @ Wq.T + bq).reshape(N, L, H, -1)
        k = (keys @ Wk.T + bk).reshape(N, S, H, -1)
        v = (values @ Wv.T + bv).reshape(N, S, H, -1)
        D = k.shape[-1]
        sm = jnp.einsum('nlhd,nshd->nlhs', q, k) / math.sqrt(D)
        causal_mask = jnp.triu(jnp.ones((L, S), dtype=bool), k=1)
        sm = jnp.where(causal_mask[None, :, None, :], -jnp.inf, sm)
        sm = jax.nn.softmax(sm, axis=-1)
        attn = jnp.einsum('nlhs,nshd->nlhd', sm, v)
        new_values = attn.reshape(N, L, H * D)
        return new_values @ Wo.T + bo

    def _L1_ffn_ref(hidden_states, Wr, router_bias, Wg, Wu, Wd, conv_w, conv_b):
        import jax, jax.numpy as jnp
        import numpy as np
        from jax import lax
        H = 256
        E = 8
        E_MLP = E - 4
        TOP_K = 2
        I = 128
        KC = 4
        SHARED_SCALE = 1.0
        B, S, Hd = hidden_states.shape
        T = B * S
        x = hidden_states.reshape(T, Hd)
        scores = jax.nn.sigmoid(x @ Wr)
        _, idx = lax.top_k(scores + router_bias, TOP_K)
        w = jnp.take_along_axis(scores, idx, axis=-1)
        w = w / (jnp.sum(w, axis=-1, keepdims=True) + 1e-09)
        cw = jnp.zeros((T, E), dtype=x.dtype).at[jnp.arange(T)[:, None], idx].add(w)
        g = jnp.einsum('th,ehi->tei', x, Wg)
        u = jnp.einsum('th,ehi->tei', x, Wu)
        hid = jax.nn.silu(g) * u
        mlp_out = jnp.einsum('tei,eih->teh', hid, Wd)
        routed = jnp.einsum('te,teh->th', cw[:, :E_MLP], mlp_out)
        routed = routed + cw[:, E_MLP:E_MLP + 1] * x
        routed = routed + cw[:, E_MLP + 2:E_MLP + 3] * x
        routed = routed + cw[:, E_MLP + 3:E_MLP + 4] * jax.nn.relu(x)
        routed = routed.reshape(B, S, Hd)
        shared = lax.conv_general_dilated(hidden_states, conv_w, window_strides=(1,), padding=[(KC - 1, 0)], dimension_numbers=('NHC', 'HIO', 'NHC'), feature_group_count=Hd) + conv_b
        return routed + SHARED_SCALE * shared
    x = x + _L0_xattn_ref(ctx_1024, _layernorm(x, axis=-1), L0_xattn_ln1_w, L0_xattn_ln1_b, L0_xattn_ln2_w, L0_xattn_ln2_b, L0_xattn_Wq, L0_xattn_Wkv, L0_xattn_Wo)
    x = x + _L0_ffn_ref(_layernorm(x, axis=-1), L0_ffn_Wr, L0_ffn_br, L0_ffn_W1, L0_ffn_b1, L0_ffn_W2, L0_ffn_b2, L0_ffn_gamma, L0_ffn_beta)
    x = x + _L1_xattn_ref(_layernorm(x, axis=-1), ctx_1024, ctx_1024, L1_xattn_Wq, L1_xattn_bq, L1_xattn_Wk, L1_xattn_bk, L1_xattn_Wv, L1_xattn_bv, L1_xattn_Wo, L1_xattn_bo)
    x = x + _L1_ffn_ref(_layernorm(x, axis=-1), L1_ffn_Wr, L1_ffn_router_bias, L1_ffn_Wg, L1_ffn_Wu, L1_ffn_Wd, L1_ffn_conv_w, L1_ffn_conv_b)
    return x

_drawn_inputs = setup_inputs


def setup_inputs(seed=0):
    import zlib

    import numpy as np

    out = dict(_drawn_inputs(seed))
    spreads = {'L0_xattn_ln1_w': (1.0, 0.55),
     'L0_xattn_ln1_b': (0.0, 0.347),
     'L0_xattn_ln2_w': (1.0, 0.2),
     'L0_xattn_ln2_b': (0.0, 0.1),
     'L0_ffn_br': (0.0, 0.1),
     'L0_ffn_b1': (0.0, 0.1),
     'L0_ffn_b2': (0.0, 0.1),
     'L0_ffn_gamma': (1.0, 0.2),
     'L0_ffn_beta': (0.0, 0.1),
     'L1_ffn_router_bias': (0.0, 0.1),
     'L1_ffn_conv_b': (0.0, 0.1)}
    factors = {'L1_xattn_bq': 2.91, 'L1_xattn_bk': 8.0}
    for name, (base, spread) in spreads.items():
        noise = np.random.default_rng([zlib.crc32(name.encode()), seed]).standard_normal(out[name].shape)
        drawn = base * np.exp(spread * noise) if base else spread * noise
        out[name] = jnp.asarray(drawn.astype(out[name].dtype))
    for name, factor in factors.items():
        out[name] = (out[name] * factor).astype(out[name].dtype)
    return out
```

```python
from contextlib import ExitStack

import concourse.bass as bass
from concourse import mybir

P = 128
ALU = mybir.AluOpType
ACT = mybir.ActivationFunctionType
AX = mybir.AxisListType
F32 = mybir.dt.float32
F32R = mybir.dt.float32r
U32 = mybir.dt.uint32

B, T, D = 2, 1024, 256
S = 77
SP = S + 1
NC = D // P
NT = B * T // P
TB = T // P
HD = 64
PAIRS = 1024 // P
KT = TB + 1
NK = T + SP
NKP = NK + 2
HALF = 512
EPS = 1e-5
STEPS = 4 * KT
JOBS = 14
CASTS = 7
E0, F0 = 8, 1024
FC = F0 // P
GR = B * T // HALF
E1, EM = 8, 4
TAPS = 4
PAD = 4
H1, D1 = 16, 16
XJ = 2 * GR
RANDL = (("h", "h"), ("h", "l"), ("l", "h"))


def program(nc, x, ctx, ln1w, ln1b, ln2w, ln2b, wqk0, wv0, wo0, wr, rbias, w1, b1, w2, b2, gb,
            watt, bqk1, bvo1, wgu, wd, convw, convb, out):
    stack = ExitStack()
    with stack:
        def sb(name, shape, dt=F32):
            return stack.enter_context(nc.sbuf_tensor(name, shape, dt))

        def sem(name):
            return stack.enter_context(nc.semaphore(name))

        ps = stack.enter_context(nc.psum_tensor("ps", [P, 8, HALF], F32))
        score_banks = [ps[:, 0, :], ps[:, 1, :]]
        max_banks = ps[:, 2:4, :].rearrange("p a n -> p (a n)")
        small_bank = ps[:, 4, :]
        shared = [ps[:, 5, :], ps[:, 6, :]]
        pv_bank = ps[:, 7, 0:4 * (HD + 1)].rearrange("p (q d) -> p q d", q=4)

        X = sb("X", [P, NT, D])
        Y = sb("Y", [P, NT, D])
        ident = sb("ident", [P, P])
        stats = sb("stats", [P, NT, 6])
        ln_tmp = sb("ln_tmp", [P, 6, NT])
        nhalf = sb("nhalf", [P, NT])
        zeros = sb("zeros", [P, 1])
        st0 = ExitStack()

        def sb0(name, shape, dt=F32):
            return st0.enter_context(nc.sbuf_tensor(name, shape, dt))

        C = sb0("C", [P, B, D])
        lnp = sb0("lnp", [P, 4, NC])
        lat = {k: sb0("lat_" + k, [P, B, NC, NKP], F32R) for k in "hl"}
        latf = sb0("latf", [P, HALF])
        wqk_raw = sb0("wqk_raw", [P, NC, 2, P])
        wv_raw = sb0("wv_raw", [P, NC, P])
        wo_raw = sb0("wo_raw", [P, D])
        wqk = {k: sb0("wqk_" + k, [P, NC, 2, P], F32R) for k in "hl"}
        wv = {k: sb0("wv_" + k, [P, NC, P], F32R) for k in "hl"}
        wo = {k: sb0("wo_" + k, [P, D], F32R) for k in "hl"}
        Q = {k: sb0("Q_" + k, [P, T], F32R) for k in "hl"}
        K = {k: sb0("K_" + k, [P, NKP], F32R) for k in "hl"}
        QA = [sb0(f"QA{h}", [P, T], F32R) for h in range(2)]
        QB = [sb0(f"QB{h}", [P, T], F32R) for h in range(2)]
        KA = [sb0(f"KA{h}", [P, NKP], F32R) for h in range(2)]
        KB = [sb0(f"KB{h}", [P, NKP], F32R) for h in range(2)]
        V = sb0("V", [P, KT, 2, HD + 1])
        PT = sb0("PT", [P, 3, HALF])
        AT = sb0("AT", [P, TB, P])
        ATT = {k: sb0("ATT_" + k, [P, T], F32R) for k in "hl"}
        rsum = sb0("rsum", [P, 4])
        mxs = sb0("mxs", [P, TB])
        mcs = sb0("mcs", [P, TB])
        maxs = sb0("maxs", [P, TB])
        maxT = [sb0(f"maxT{h}", [TB, P], F32R) for h in range(2)]
        st0.close()

        XT = {k: sb("XT_" + k, [P, NC, B, PAD + T], F32R) for k in "hl"}
        wr_raw = sb("wr_raw", [P, 2, NC, E0])
        wrs = {k: sb("wr_" + k, [P, 2, NC, E0], F32R) for k in "hl"}
        rb = sb("rb", [P, 2, E0])
        iota8 = sb("iota8", [P, E0])
        logits = sb("logits", [P, NT, E0])
        top = sb("top", [P, NT, 8])
        topi = sb("topi", [P, NT, 8], U32)
        topf = sb("topf", [P, NT, 2])
        rw = sb("rw", [P, 4, NT])
        oh = sb("oh", [P, 2, NT, E0])
        R = sb("R", [P, NT, E0])
        st1 = ExitStack()

        def sb1(name, shape, dt=F32):
            return st1.enter_context(nc.sbuf_tensor(name, shape, dt))

        RT = sb1("RT", [E0, NT, P])
        b2s = sb1("b2s", [E0, D])
        b1e = sb1("b1e", [P, FC])
        gbs = sb1("gbs", [P, 2, D])
        w1_raw = sb1("w1_raw", [P, FC, NC * P])
        w2_raw = sb1("w2_raw", [P, FC, D])
        w1s = {k: sb1("w1_" + k, [P, FC, NC * P], F32R) for k in "hl"}
        w2s = {k: sb1("w2_" + k, [P, FC, D], F32R) for k in "hl"}
        hf = sb1("hf", [P, 2, HALF])
        hs = {k: sb1("h_" + k, [P, 3, HALF], F32R) for k in "hl"}
        st1.close()
        st2 = ExitStack()

        def sb2(name, shape, dt=F32):
            return st2.enter_context(nc.sbuf_tensor(name, shape, dt))

        C1 = sb2("C1", [P, B, D])
        CT = {k: sb2("CT_" + k, [P, NC, B, SP], F32R) for k in "hl"}
        wa_raw = sb2("wa_raw", [P, 4, NC, D])
        wa = {k: sb2("wa_" + k, [P, 4, NC, D], F32R) for k in "hl"}
        bqk = sb2("bqk", [P, 2, NC])
        bvo_raw = sb2("bvo_raw", [1, 2, D])
        bvo = {k: sb2("bvo_" + k, [1, 2, D], F32R) for k in "hl"}
        ones_row = sb2("ones_row", [1, P], F32R)
        ident_r = sb2("ident_r", [P, P], F32R)
        mask_f = sb2("mask_f", [P, 2, P])
        mask = sb2("mask", [P, 2, P], F32R)
        kf = sb2("kf", [P, NC, B * SP])
        K1 = {k: sb2("K1_" + k, [P, NC, B * SP], F32R) for k in "hl"}
        V1 = sb2("V1", [P, B, H1, D1 + 1])
        qf = sb2("qf", [P, HALF])
        Q1 = {k: sb2("Q1_" + k, [P, NC, T], F32R) for k in "hl"}
        QS = sb2("QS", [P, 4, T], F32R)
        KS = sb2("KS", [P, 4, SP], F32R)
        PT1 = sb2("PT1", [P, 3, HALF])
        m8 = sb2("m8", [P, 2, TB])
        m8T = sb2("m8T", [TB, 2, P], F32R)
        rs8 = sb2("rs8", [P, TB])
        A1T = {k: sb2("A1T_" + k, [P, NC, HALF], F32R) for k in "hl"}
        st2.close()
        st3 = ExitStack()

        def sb3(name, shape, dt=F32):
            return st3.enter_context(nc.sbuf_tensor(name, shape, dt))

        wgu_raw = sb3("wgu_raw", [P, EM, 2, NC, P])
        wgus = {k: sb3("wgu_" + k, [P, EM, 2, NC, P], F32R) for k in "hl"}
        wd_raw = sb3("wd_raw", [P, EM, D])
        wds = {k: sb3("wd_" + k, [P, EM, D], F32R) for k in "hl"}
        cw = sb3("cw", [P, 2, TAPS * NC])
        cwh = sb3("cwh", [P, TAPS * NC], F32R)
        diag = {k: sb3("diag_" + k, [P, TAPS * NC, P], F32R) for k in "hl"}
        cb = sb3("cb", [1, D])
        ones_f = sb3("ones_f", [1, P])
        silu = sb3("silu", [P, 2, HALF])
        gated = sb3("gated", [P, 2, HALF])
        gs = {k: sb3("g_" + k, [P, 3, HALF], F32R) for k in "hl"}
        reluY = sb3("reluY", [P, 4, D])
        st3.close()

        s_in = sem("inputs_loaded")
        s_zero = sem("context_cleared")
        s_const = sem("constants_ready")
        s_dve = sem("vector_chain")
        s_var = sem("variances_ready")
        s_rstd = sem("rstds_ready")
        s_lnc = sem("context_normalised")
        s_ln = sem("latents_normalised")
        s_lat_full = sem("latent_bank_full")
        s_lat_hi = sem("latent_hi_ready")
        s_lat_f = sem("latent_full_ready")
        s_lat_lo = sem("latent_lo_ready")
        s_wqk_raw, s_wv_raw, s_wo_raw = sem("wqk_loaded"), sem("wv_loaded"), sem("wo_loaded")
        s_wqk, s_wv, s_wo = sem("wqk_split"), sem("wv_split"), sem("wo_split")
        s_job = sem("shared_bank_full")
        s_cast = sem("shared_bank_rounded")
        s_jobfree = sem("shared_bank_free")
        s_mx = sem("max_bank_full")
        s_mxfree = sem("max_bank_free")
        s_max = sem("head_max_ready")
        s_maxT = sem("head_max_transposed")
        s_maxrow = sem("head_max_row_ready")
        s_stack = [sem("stack0_loaded"), sem("stack1_loaded")]
        s_row = [sem("max_row0_loaded"), sem("max_row1_loaded")]
        s_score = sem("scores_ready")
        s_exp = sem("exp_done")
        s_pv = sem("pv_done")
        s_rec = sem("sums_inverted")
        s_norm = sem("attention_normalised")
        s_out = sem("output_written")
        s_in1 = sem("expert_inputs_loaded")
        s_xn = sem("tokens_normalised")
        s_tj = sem("transposed_bank_full")
        s_thi = sem("transposed_hi_ready")
        s_tfree = sem("transposed_bank_free")
        s_wr = sem("router_weights_split")
        s_route = sem("router_logits_ready")
        s_rexp_in = sem("router_exponents_ready")
        s_rexp = sem("router_exp_done")
        s_R = sem("routing_weights_ready")
        s_RT = sem("routing_weights_transposed")
        s_w1_raw, s_w2_raw = sem("w1_loaded"), sem("w2_loaded")
        s_w1, s_w2 = sem("w1_split"), sem("w2_split")
        s_b1e = sem("expert_biases_placed")
        s_up = sem("hidden_bank_full")
        s_hhi = sem("hidden_hi_ready")
        s_hf = sem("hidden_bank_free")
        s_hlo = sem("hidden_lo_ready")
        s_down = sem("hidden_used")
        s_accfree = sem("output_banks_free")
        s_in2 = sem("layer1_attention_loaded")
        s_wa = sem("layer1_weights_split")
        s_a1 = sem("layer1_bank_full")
        s_a1e = sem("layer1_bank_free")
        s_q1f = sem("layer1_q_ready")
        s_q1s = sem("layer1_q_split")
        s_st1 = [sem(f"layer1_stack{i}_loaded") for i in range(4)]
        s_mx1 = sem("layer1_max_banks_full")
        s_m8 = sem("layer1_max_ready")
        s_m8t = sem("layer1_max_transposed")
        s_m8T = sem("layer1_max_row_ready")
        s_row1 = [sem(f"layer1_max_row{i}_loaded") for i in range(4)]
        s_sc1 = sem("layer1_scores_ready")
        s_ex1 = sem("layer1_exp_done")
        s_pv1 = sem("layer1_pv_done")
        s_nm1 = sem("layer1_attention_normalised")
        s_in3 = sem("layer1_experts_loaded")
        s_w3 = sem("layer1_expert_weights_split")
        s_conv = sem("convolution_bank_full")
        s_convfree = sem("convolution_bank_free")
        s_gu = sem("gate_and_up_full")
        s_silu = sem("silu_ready")
        s_gated = sem("gated_ready")
        s_ghi = sem("gated_hi_ready")
        s_glo = sem("gated_lo_ready")
        s_acc1 = sem("layer1_down_added")
        s_dn1h = sem("layer1_down_half_full")
        s_w3d = sem("tap_diagonals_ready")
        s_ones = sem("layer1_constants_ready")

        def flat4(t):
            return t[:].rearrange("p a b c -> p (a b c)")

        def flat(t):
            return t[:] if len(t.shape) == 2 else t[:].rearrange(
                "p a b -> p (a b)" if len(t.shape) == 3 else "p a b c -> p (a b c)")

        chain = [0]

        def link(dve, ins):
            chain[0] += 1
            ins.then_inc(s_dve, 1)
            dve.wait_ge(s_dve, chain[0])

        lns = [0]

        def normalise(dve, src, dst, n, last=None):
            for t in range(n):
                ins = nc.vector.bn_stats(stats[:, t, :], src[:, t, :])
            link(dve, ins)
            me, mo = stats[:, 0:n, 1], stats[:, 0:n, 4]
            mean, dif, m2, var, rstd, sq = (ln_tmp[:, i, 0:n] for i in range(6))
            nc.vector.tensor_tensor(mean, me, mo, ALU.add)
            nc.vector.tensor_tensor(m2, stats[:, 0:n, 2], stats[:, 0:n, 5], ALU.add)
            link(dve, nc.vector.tensor_tensor(dif, me, mo, ALU.subtract))
            link(dve, nc.vector.tensor_tensor(sq, dif, dif, ALU.mult))
            link(dve, nc.vector.scalar_tensor_tensor(out=sq, in0=sq, scalar=D / 4.0, in1=m2,
                                                     op0=ALU.mult, op1=ALU.add))
            nc.vector.tensor_scalar(mean, mean, 0.5, None, ALU.mult)
            nc.vector.tensor_scalar(var, sq, 1.0 / D, EPS, ALU.mult, ALU.add).then_inc(s_var, 1)
            lns[0] += 1
            dve.wait_ge(s_rstd, lns[0])
            for t in range(n):
                ins = nc.vector.tensor_scalar(dst[:, t, :], src[:, t, :], mean[:, t:t + 1], rstd[:, t:t + 1],
                                              ALU.subtract, ALU.mult)
            if last is None:
                link(dve, ins)
            else:
                ins.then_inc(last, 1)

        def rstds(pool, k, n):
            pool.wait_ge(s_var, k)
            nc.gpsimd.tensor_tensor(ln_tmp[:, 4, 0:n], ln_tmp[:, 3, 0:n], nhalf[:, 0:n],
                                    ALU.pow).then_inc(s_rstd, 1)

        LATJOBS = [(b, c, h) for b in range(B) for c in range(NC) for h in range(3)]

        def jobs_before(g):
            return 5 + JOBS * g

        def bank(idx):
            return shared[(5 + idx) % 2]

        def turns(eng, emit):
            for b in range(B):
                with eng.Fori(0, PAIRS - 1) as i:
                    emit(b, i, b * PAIRS + i, b)
                emit(b, PAIRS - 1, b * PAIRS + PAIRS - 1, b + 1 if b + 1 < B else None)

        ATT0_JOBS = 5 + JOBS * B * PAIRS - 5
        tbank = [ps[:, 6, :], ps[:, 7, :]]
        TJOBS = [(c, b, h) for b in range(B) for h in range(2) for c in range(NC)]

        hidden_banks = [ps[:, 0, :], ps[:, 1, :]]
        acc_banks = [ps[:, 2:4, :].rearrange("p a n -> p (a n)"), ps[:, 4:6, :].rearrange("p a n -> p (a n)")]
        score1 = [ps[0:S, 3, :], ps[0:S, 4, :]]
        pv1 = ps[:, 5, 0:TB * (D1 + 1)].rearrange("p (t d) -> p t d", t=TB)
        gate_banks, up_banks = [ps[:, 0, :], ps[:, 1, :]], [ps[:, 2, :], ps[:, 3, :]]
        down_banks = [ps[:, 4, :], ps[:, 5, :]]

        M1_AT, M1_MAX, M1_T = 1, 10, 11
        QK_AT, M0_AT, M0_MAX, M0_T = 18, 24, 33, 34

        block = stack.enter_context(nc.Block())

        @block.sync
        def _(sp):
            sp.wait_ge(s_zero, 1)
            sp.dma_start(C[0:S], ctx.rearrange("b s d -> s b d")).then_inc(s_in, 16)
            sp.dma_start(C[S:SP], ctx[:, S - 1:S, :].rearrange("b s d -> s b d")).then_inc(s_in, 16)
            for i, w in enumerate((ln1w, ln1b, ln2w, ln2b)):
                sp.dma_start(lnp[:, i, :], w).then_inc(s_in, 16)
            sp.dma_start(X[:], x.rearrange("b (t p) d -> p (b t) d", p=P)).then_inc(s_in, 16)
            sp.dma_start(wqk_raw[:], wqk0[0]).then_inc(s_wqk_raw, 16)
            sp.dma_start(wv_raw[:], wv0[0]).then_inc(s_wv_raw, 16)
            sp.dma_start(wo_raw[:], wo0[0]).then_inc(s_wo_raw, 16)

            def stack_head(h):
                r = slice(HD * h, HD * h + HD)
                for dst, src in ((QA[h][0:HD], Q["h"][r]), (QA[h][HD:P], Q["h"][r]), (QB[h][0:HD], Q["l"][r])):
                    sp.dma_start(dst.bitcast(F32), src.bitcast(F32)).then_inc(s_stack[h], 16)
                for dst, src in ((KA[h][0:HD, 0:NK], K["h"][r, 0:NK]), (KA[h][HD:P, 0:NK], K["l"][r, 0:NK]),
                                 (KB[h][0:HD, 0:NK], K["h"][r, 0:NK])):
                    sp.dma_start(dst.bitcast(F32), src.bitcast(F32)).then_inc(s_stack[h], 16)

            def max_row(h):
                sp.dma_start(QB[h][HD:HD + 1, :].bitcast(F32).rearrange("o (t p) -> o t p", t=TB), maxT[h][:].bitcast(F32)) \
                    .then_inc(s_row[h], 16)

            sp.wait_ge(s_jobfree, 2 + 5)
            stack_head(0)
            sp.wait_ge(s_maxrow, 1)
            max_row(0)

            def turn(b, i, g, nb):
                sp.wait_ge(s_jobfree, jobs_before(g) + 2)
                stack_head(1)
                if nb is not None:
                    nxt = (i + 1) % PAIRS if isinstance(i, int) else i + 1
                    for raw, src, split, loaded in ((wqk_raw, wqk0, s_wqk, s_wqk_raw), (wv_raw, wv0, s_wv, s_wv_raw),
                                                    (wo_raw, wo0, s_wo, s_wo_raw)):
                        sp.wait_ge(split, 2 * g + 2)
                        sp.dma_start(raw[:], src[nxt] if isinstance(nxt, int) else src[bass.ds(nxt, 1)].squeeze(0)).then_inc(loaded, 16)
                sp.wait_ge(s_maxrow, 2 * g + 2)
                max_row(1)
                if nb is not None:
                    sp.wait_ge(s_jobfree, jobs_before(g) + 8 + 2)
                    stack_head(0)
                    sp.wait_ge(s_maxrow, 2 * g + 3)
                    max_row(0)

            turns(sp, turn)
            sp.wait_ge(s_jobfree, ATT0_JOBS + 2)
            for dst, src in ((wr_raw, wr), (rb, rbias.partition_broadcast(P)), (b2s, b2),
                             (gbs, gb.partition_broadcast(P))):
                sp.dma_start(dst[:], src).then_inc(s_in1, 16)
            sp.dma_start(b1e[:], b1[0]).then_inc(s_b1e, 16)
            sp.dma_start(w1_raw[:], w1[0]).then_inc(s_w1_raw, 16)
            sp.dma_start(w2_raw[:], w2[0]).then_inc(s_w2_raw, 16)
            with sp.Fori(0, E0 - 1) as e:
                sp.wait_ge(s_w1, 2 * FC * e + 2 * FC)
                sp.dma_start(w1_raw[:], w1[bass.ds(e + 1, 1)].squeeze(0)).then_inc(s_w1_raw, 16)
                sp.wait_ge(s_w2, 2 * FC * e + 2 * FC)
                sp.dma_start(w2_raw[:], w2[bass.ds(e + 1, 1)].squeeze(0)).then_inc(s_w2_raw, 16)
                sp.wait_ge(s_hf, GR * FC * e + GR * FC + 2)
                sp.dma_start(b1e[:], b1[bass.ds(e + 1, 1)].squeeze(0)).then_inc(s_b1e, 16)

            sp.wait_ge(s_xn, 2)
            sp.wait_ge(s_zero, 2)
            sp.dma_start(C1[0:S], ctx.rearrange("b s d -> s b d")).then_inc(s_in2, 16)
            sp.dma_start(C1[S:SP], ctx[:, S - 1:S, :].rearrange("b s d -> s b d")).then_inc(s_in2, 16)
            sp.dma_start(wa_raw[:], watt).then_inc(s_in2, 16)
            sp.dma_start(bqk[:], bqk1).then_inc(s_in2, 16)
            sp.dma_start(bvo_raw[:], bvo1).then_inc(s_in2, 16)

            def stack1(n):
                b, h = divmod(n, H1)
                r, c, k = slice(D1 * (h % 8), D1 * (h % 8) + D1), h // 8, slice(b * SP, b * SP + SP)
                if n >= 4:
                    sp.wait_ge(s_sc1, 2 * (n - 4) + 2)
                for i, (q, kk) in enumerate((("h", "h"), ("l", "h"), ("h", "l"))):
                    o = slice(D1 * i, D1 * i + D1)
                    sp.dma_start(QS[o, n % 4, :].bitcast(F32), Q1[q][r, c, :].bitcast(F32)).then_inc(s_st1[n % 4], 16)
                    sp.dma_start(KS[o, n % 4, :].bitcast(F32), K1[kk][r, c, k].bitcast(F32)).then_inc(s_st1[n % 4], 16)

            def row1(n):
                sp.wait_ge(s_m8T, n + 1)
                sp.dma_start(QS[3 * D1:3 * D1 + 1, n % 4, :].bitcast(F32).rearrange("o (t p) -> o t p", t=TB),
                             m8T[:, n % 2, :].bitcast(F32)).then_inc(s_row1[n % 4], 16)

            for b in range(B):
                sp.wait_ge(s_q1s, 8 * (b + 1))
                for n in range(3):
                    stack1(b * H1 + n)
                for n in range(H1):
                    if n + 3 < H1:
                        stack1(b * H1 + n + 3)
                    row1(b * H1 + n)

            sp.wait_ge(s_xn, 3)
            for dst, src in ((wgu_raw[:], wgu), (wd_raw[:], wd), (cw[:, 0, :], convw), (cb[:], convb)):
                sp.dma_start(dst, src).then_inc(s_in3, 16)
            for g in range(GR):
                sp.wait_ge(s_acc1, 4 * EM * (g + 1))
                sp.dma_start(out[g // 2, HALF * (g % 2):HALF * (g % 2) + HALF].rearrange("(t p) d -> p t d", p=P),
                             X[:, 4 * g:4 * g + 4, :]).then_inc(s_out, 16)
            sp.wait_ge(s_out, 16 * GR)

        @block.gpsimd
        def _(pool):
            nc.gpsimd.memset(C[:], 0.0).then_inc(s_zero, 1)
            nc.gpsimd.memset(nhalf[:], -0.5).then_inc(s_const, 1)
            nc.gpsimd.memset(ident[:], 0.0).then_inc(s_const, 1)
            nc.gpsimd.memset(zeros[:], 0.0).then_inc(s_const, 1)
            nc.gpsimd.memset(V[:, :, :, HD:HD + 1], 1.0).then_inc(s_const, 1)
            pool.wait_ge(s_const, 6)
            nc.gpsimd.affine_select(out=ident[:], in_=ident[:], compare_op=ALU.not_equal, fill=1.0, base=0,
                                    pattern=[[-1, P]], channel_multiplier=1).then_inc(s_const, 1)
            rstds(pool, 1, B)
            rstds(pool, 2, NT)
            rstds(pool, 3, NT)

            def split(raw, parts, loaded, n, done):
                pool.wait_ge(loaded, 16 * n + 16)
                nc.gpsimd.tensor_tensor(flat(parts["h"]), flat(raw), zeros[:, 0:1].to_broadcast([P, flat(raw).shape[1]]),
                                        ALU.add).then_inc(done, 1)
                pool.wait_ge(done, 2 * n + 1)
                nc.gpsimd.tensor_tensor(flat(parts["l"]), flat(raw), flat(parts["h"]).bitcast(F32), ALU.subtract) \
                    .then_inc(done, 1)

            split(wqk_raw, wqk, s_wqk_raw, 0, s_wqk)
            split(wv_raw, wv, s_wv_raw, 0, s_wv)
            split(wo_raw, wo, s_wo_raw, 0, s_wo)

            def latents_lo(k, b, c, h):
                pool.wait_ge(s_lat_f, k + 1)
                pool.wait_ge(s_lat_hi, k + 1)
                n = HALF if h < 2 else SP
                cols = slice(HALF * h, HALF * h + n)
                nc.gpsimd.tensor_tensor(lat["l"][:, b, c, cols], latf[:, 0:n],
                                        lat["h"][:, b, c, cols].bitcast(F32), ALU.subtract).then_inc(s_lat_lo, 1)

            for k, (b, c, h) in enumerate(LATJOBS):
                latents_lo(k, b, c, h)

            def turn(b, i, g, nb):
                if nb is None:
                    return
                pool.wait_ge(s_job, jobs_before(g) + 1)
                split(wqk_raw, wqk, s_wqk_raw, g + 1, s_wqk)
                pool.wait_ge(s_job, jobs_before(g) + 3)
                split(wv_raw, wv, s_wv_raw, g + 1, s_wv)
                pool.wait_ge(s_job, jobs_before(g) + JOBS)
                split(wo_raw, wo, s_wo_raw, g + 1, s_wo)

            turns(pool, turn)

            def split_part(raw, hi, lo, done, n):
                nc.gpsimd.tensor_tensor(hi, raw, zeros[:, 0:1].to_broadcast([P, raw.shape[1]]), ALU.add).then_inc(done, 1)
                pool.wait_ge(done, 2 * n + 1)
                nc.gpsimd.tensor_tensor(lo, raw, hi.bitcast(F32), ALU.subtract).then_inc(done, 1)

            pool.wait_ge(s_jobfree, ATT0_JOBS + 2)
            nc.gpsimd.iota(iota8[:], pattern=[[1, E0]], base=0, channel_multiplier=0,
                           allow_small_or_imprecise_dtypes=True).then_inc(s_const, 1)
            for k in "hl":
                nc.gpsimd.memset(XT[k][:, :, :, 0:PAD].bitcast(F32), 0.0).then_inc(s_const, 1)
            rstds(pool, 4, NT)
            for parts, raw, loaded, done in ((w1s, w1_raw, s_w1_raw, s_w1), (w2s, w2_raw, s_w2_raw, s_w2)):
                pool.wait_ge(loaded, 16)
                for f in range(FC):
                    split_part(raw[:, f], parts["h"][:, f], parts["l"][:, f], done, f)

            def hidden_lo(e, u):
                n = GR * FC * e + u
                pool.wait_ge(s_hf, n + 1 + 2)
                nc.gpsimd.tensor_tensor(hs["l"][:, u % 3], hf[:, u % 2], hs["h"][:, u % 3].bitcast(F32),
                                        ALU.subtract).then_inc(s_hlo, 1)

            def expert(e, more):
                for u in range(GR * FC):
                    hidden_lo(e, u)
                    f = u - (GR - 1) * FC - 1
                    if more and f >= 0:
                        next_chunk(e, f)
                if more:
                    next_chunk(e, FC - 1)

            def next_chunk(e, f):
                n = GR * FC * e + (GR - 1) * FC + f
                if f == 0:
                    pool.wait_ge(s_w1_raw, 16 * e + 32)
                pool.wait_ge(s_up, n + 1)
                split_part(w1_raw[:, f], w1s["h"][:, f], w1s["l"][:, f], s_w1, FC * e + FC + f)
                if f == 0:
                    pool.wait_ge(s_w2_raw, 16 * e + 32)
                pool.wait_ge(s_down, n + 1 + 3)
                split_part(w2_raw[:, f], w2s["h"][:, f], w2s["l"][:, f], s_w2, FC * e + FC + f)

            with pool.Fori(0, E0 - 1) as e:
                expert(e, True)
            expert(E0 - 1, False)
            rstds(pool, 5, NT)

            rstds(pool, 6, NT)
            pool.wait_ge(s_xn, 2)
            nc.gpsimd.memset(C1[:], 0.0).then_inc(s_zero, 1)
            nc.gpsimd.memset(V1[:, :, :, D1:D1 + 1], 1.0).then_inc(s_const, 1)
            nc.gpsimd.memset(mask_f[:], 0.0).then_inc(s_const, 1)
            pool.wait_ge(s_const, 12)
            nc.gpsimd.affine_select(out=mask_f[:, 0, :], in_=mask_f[:, 0, :], compare_op=ALU.is_ge, fill=-1e30, base=0,
                                    pattern=[[-1, P]], channel_multiplier=1).then_inc(s_const, 1)
            nc.gpsimd.affine_select(out=mask_f[:, 1, :], in_=mask_f[:, 1, :], compare_op=ALU.is_ge, fill=-1e30, base=0,
                                    pattern=[[1, P]], channel_multiplier=-1).then_inc(s_const, 1)
            pool.wait_ge(s_in2, 16 * 5)
            split_part(flat4(wa_raw), flat4(wa["h"]), flat4(wa["l"]), s_wa, 0)

            for b in range(B):
                for j in range(4):
                    n = 4 * b + j
                    c, h = divmod(j, 2)
                    cols = slice(HALF * h, HALF * h + HALF)
                    pool.wait_ge(s_q1f, n + 1)
                    if j == 0 and b > 0:
                        for stacked in s_st1:
                            pool.wait_ge(stacked, 96 * H1 // 4 * b)
                    nc.gpsimd.tensor_tensor(Q1["h"][:, c, cols], qf[:], zeros[:, 0:1].to_broadcast([P, HALF]),
                                            ALU.add).then_inc(s_q1s, 1)
                    pool.wait_ge(s_q1s, 2 * n + 1)
                    nc.gpsimd.tensor_tensor(Q1["l"][:, c, cols], qf[:], Q1["h"][:, c, cols].bitcast(F32),
                                            ALU.subtract).then_inc(s_q1s, 1)

            rstds(pool, 7, NT)
            pool.wait_ge(s_xn, 3)
            pool.wait_ge(s_in3, 16 * 4)
            split_part(wgu_raw[:].rearrange("p e a c n -> p (e a c n)"),
                       wgus["h"][:].rearrange("p e a c n -> p (e a c n)"),
                       wgus["l"][:].rearrange("p e a c n -> p (e a c n)"), s_w3, 0)
            split_part(flat(wd_raw), flat(wds["h"]), flat(wds["l"]), s_w3, 1)
            for n in range(GR * EM):
                pool.wait_ge(s_ghi, n + 1)
                nc.gpsimd.tensor_tensor(gs["l"][:, n % 3], gated[:, n % 2], gs["h"][:, n % 3].bitcast(F32),
                                        ALU.subtract).then_inc(s_glo, 1)

        @block.scalar
        def _(act):
            act.wait_ge(s_in, 16 * 7)
            for k, (b, c, h) in enumerate(LATJOBS):
                act.wait_ge(s_lat_full, k + 1)
                n = HALF if h < 2 else SP
                w = 2 if h < 2 else 0
                nc.scalar.activation(lat["h"][:, b, c, HALF * h:HALF * h + n], shared[k % 2][:, 0:n], ACT.Identity,
                                     bias=lnp[:, w + 1, c:c + 1], scale=lnp[:, w, c:c + 1]).then_inc(s_lat_hi, 1)

            def round_qk(j, job, cast):
                act.wait_ge(s_job, job)
                dst = (Q["h"][:, 0:HALF], Q["h"][:, HALF:T], K["h"][:, 0:HALF], K["h"][:, HALF:T], K["h"][:, T:NK])[j]
                src = shared[(job_parity[0] + j) % 2]
                nc.scalar.copy(dst, src[:, 0:SP] if j == 4 else src).then_inc(s_cast, 1)

            job_parity = [0]
            for j in range(5):
                round_qk(j, j + 1, j)
            job_parity[0] = 5 + 3

            def turn(b, i, g, nb):
                for s in range(STEPS):
                    m = P if s % KT < TB else S
                    act.wait_ge(s_score, 36 * g + s + 1 + 1)
                    act.wait_ge(s_pv, 36 * g + s + 1)
                    nc.scalar.activation(PT[0:m, s % 3, :], score_banks[s % 2][0:m], ACT.Exp,
                                         scale=HD ** -0.5).then_inc(s_exp, 1)
                    if nb is not None and QK_AT <= s < QK_AT + 5:
                        if s == QK_AT:
                            act.wait_ge(s_stack[1], 96 * g + 96)
                        round_qk(s - QK_AT, jobs_before(g) + 3 + s - QK_AT + 1, 0)
                a = 8 if nb is not None else 3
                for j in range(2):
                    act.wait_ge(s_job, jobs_before(g) + a + j + 1)
                    nc.scalar.copy(ATT["h"][:, HALF * j:HALF * j + HALF], bank(a + j)).then_inc(s_cast, 1)

            turns(act, turn)

            def transposed_hi(z):
                for k, (c, b, h) in enumerate(TJOBS):
                    act.wait_ge(s_tj, (0, 20, 28)[z] + k + 1)
                    nc.scalar.copy(XT["h"][:, c, b, PAD + HALF * h:PAD + HALF * h + HALF], tbank[k % 2]).then_inc(s_thi, 1)

            transposed_hi(0)
            act.wait_ge(s_rexp_in, 1)
            nc.scalar.activation(rw[:, 1, :], rw[:, 0, :], ACT.Exp).then_inc(s_rexp, 1)
            act.wait_ge(s_in1, 16 * 4)

            def expert(e):
                act.wait_ge(s_b1e, 16 * e + 16)
                for u in range(GR * FC):
                    n = GR * FC * e + u
                    act.wait_ge(s_up, n + 1)
                    act.wait_ge(s_down, n + 1)
                    nc.scalar.activation(hs["h"][:, u % 3], hidden_banks[u % 2], ACT.Relu,
                                         bias=b1e[:, u % FC:u % FC + 1]).then_inc(s_hhi, 1)

            with act.Fori(0, E0) as e:
                expert(e)

            transposed_hi(1)
            for n in range(B * H1):
                for a in range(2):
                    k = 2 * n + a
                    act.wait_ge(s_sc1, k + 1)
                    if k >= 3:
                        act.wait_ge(s_pv1, k - 2)
                    nc.scalar.activation(PT1[0:S, k % 3, :], score1[k % 2], ACT.Exp, scale=D1 ** -0.5).then_inc(s_ex1, 1)

            transposed_hi(2)
            act.wait_ge(s_route, 2)
            nc.scalar.activation(logits[:], tbank[0][:, 0:NT * E1].rearrange("p (t e) -> p t e", t=NT), ACT.Exp,
                                 scale=-1.0).then_inc(s_rexp, 1)
            for n in range(GR * EM):
                act.wait_ge(s_gu, 2 * n + 2)
                if n >= 2:
                    act.wait_ge(s_gated, n - 1)
                nc.scalar.activation(silu[:, n % 2], gate_banks[n % 2], ACT.Silu).then_inc(s_silu, 1)
                act.wait_ge(s_gated, n + 1)
                if n >= 3:
                    act.wait_ge(s_dn1h, 2 * n - 4)
                nc.scalar.copy(gs["h"][:, n % 3], gated[:, n % 2]).then_inc(s_ghi, 1)

        @block.vector
        def _(dve):
            dve.sem_inc(s_jobfree, 2)
            dve.sem_inc(s_mxfree, 1)
            dve.sem_inc(s_score, 1)
            dve.sem_inc(s_exp, 2)
            dve.sem_inc(s_pv, 3)
            dve.sem_inc(s_norm, 1)
            for h in range(2):
                nc.vector.memset(KB[h][HD:HD + 1, :].bitcast(F32), 1.0).then_inc(s_const, 1)
            dve.wait_ge(s_in, 16 * 7)
            dve.wait_ge(s_const, 7)
            normalise(dve, C, C, B, s_lnc)
            normalise(dve, X, Y, NT)
            normalise(dve, Y, Y, NT, s_ln)
            for k, (b, c, h) in enumerate(LATJOBS):
                dve.wait_ge(s_lat_full, k + 1)
                dve.wait_ge(s_lat_hi, k + 1)
                if k >= 1:
                    dve.wait_ge(s_lat_lo, k)
                n = HALF if h < 2 else SP
                w = 2 if h < 2 else 0
                nc.vector.tensor_scalar(latf[:, 0:n], shared[k % 2][:, 0:n], lnp[:, w, c:c + 1],
                                        lnp[:, w + 1, c:c + 1], ALU.mult, ALU.add).then_inc(s_lat_f, 1)

            def rest_qk(j, cast, bk):
                dve.wait_ge(s_cast, cast)
                which, cols = (("q", slice(0, HALF)), ("q", slice(HALF, T)), ("k", slice(0, HALF)),
                               ("k", slice(HALF, T)), ("k", slice(T, NK)))[j]
                part = Q if which == "q" else K
                n = cols.stop - cols.start
                nc.vector.tensor_tensor(part["l"][:, cols], bk[:, 0:n], part["h"][:, cols].bitcast(F32),
                                        ALU.subtract).then_inc(s_jobfree, 1)

            def max_tile(t, n):
                dve.wait_ge(s_mx, n + 1)
                r = nc.vector.reduce_max(mxs[:, t:t + 1], max_banks, AX.X)
                if t % 4 == 3:
                    r = nc.vector.reduce_max(mcs[:, t - 3:t + 1],
                                             small_bank[:, 0:4 * SP].rearrange("p (t s) -> p t s", t=4), AX.X)
                r.then_inc(s_mxfree, 1)

            def max_join(n):
                dve.wait_ge(s_mxfree, n + 1)
                nc.vector.tensor_tensor(maxs[:], mxs[:], mcs[:], ALU.max).then_inc(s_max, 1)

            def max_rows(h, k):
                dve.wait_ge(s_maxT, k + 1)
                nc.vector.tensor_scalar(maxT[h][:], small_bank[0:TB, 0:P], -1.0, None, ALU.mult).then_inc(s_maxrow, 1)

            for j in range(5):
                rest_qk(j, j + 1, shared[j % 2])
            for t in range(TB):
                max_tile(t, t)
            max_join(TB)
            max_rows(0, 0)

            def values(g, b):
                for j in range(3):
                    dve.wait_ge(s_job, jobs_before(g) + j + 1)
                    if j < 2:
                        nc.vector.tensor_copy(V[:, 4 * j:4 * j + 4, :, 0:HD],
                                              bank(j).rearrange("p (k h d) -> p k h d", k=4, h=2)).then_inc(s_jobfree, 1)
                    else:
                        nc.vector.tensor_copy(V[0:S, TB, :, 0:HD],
                                              bank(j)[0:S, 0:P].rearrange("p (h d) -> p h d", h=2)).then_inc(s_jobfree, 1)

            def unit_done(g, u):
                dve.wait_ge(s_pv, 36 * g + KT * (u + 1) + 3)
                nc.vector.reciprocal(rsum[:], pv_bank[:, :, HD]).then_inc(s_rec, 1)
                dve.wait_ge(s_rec, 4 * g + u + 1)
                h, half = u // 2, u % 2
                nc.vector.tensor_tensor(AT[:, 4 * half:4 * half + 4, HD * h:HD * h + HD], pv_bank[:, :, 0:HD],
                                        rsum[:].unsqueeze(2).to_broadcast([P, 4, HD]), ALU.mult).then_inc(s_norm, 1)

            def turn(b, i, g, nb):
                values(g, b)
                for s in range(STEPS):
                    if s % KT == 0 and s > 0:
                        unit_done(g, s // KT - 1)
                    if M1_AT <= s < M1_AT + TB:
                        max_tile(s - M1_AT, 16 * g + 8 + s - M1_AT)
                    if s == M1_MAX:
                        max_join(16 * g + 16)
                    if s == M1_T:
                        max_rows(1, 2 * g + 1)
                    if nb is not None:
                        if QK_AT <= s < QK_AT + 5:
                            j = s - QK_AT
                            if j == 0:
                                dve.wait_ge(s_stack[1], 96 * g + 96)
                            rest_qk(j, 5 + CASTS * g + j + 1, bank(3 + j))
                        if M0_AT <= s < M0_AT + TB:
                            max_tile(s - M0_AT, 16 * g + 16 + s - M0_AT)
                        if s == M0_MAX:
                            max_join(16 * g + 24)
                        if s == M0_T:
                            max_rows(0, 2 * g + 2)
                unit_done(g, 3)
                a = 8 if nb is not None else 3
                for j in range(2):
                    dve.wait_ge(s_cast, 5 + CASTS * g + (5 if nb is not None else 0) + j + 1)
                    nc.vector.tensor_tensor(ATT["l"][:, HALF * j:HALF * j + HALF], bank(a + j),
                                            ATT["h"][:, HALF * j:HALF * j + HALF].bitcast(F32), ALU.subtract) \
                        .then_inc(s_jobfree, 1)
                for j in range(4):
                    dve.wait_ge(s_job, jobs_before(g) + a + 2 + j + 1)
                    xt = X[:, TB * b + 2 * j:TB * b + 2 * j + 2, :]
                    nc.vector.tensor_tensor(xt, xt, bank(a + 2 + j).rearrange("p (t d) -> p t d", t=2), ALU.add) \
                        .then_inc(s_jobfree, 1)

            turns(dve, turn)
            for se, v in ((s_hf, 2), (s_hlo, 2), (s_down, 3), (s_accfree, 2)):
                dve.sem_inc(se, v)

            def transposed_lo(z):
                for k, (c, b, h) in enumerate(TJOBS):
                    dve.wait_ge(s_thi, XJ * z + k + 1)
                    cols = slice(PAD + HALF * h, PAD + HALF * h + HALF)
                    nc.vector.tensor_tensor(XT["l"][:, c, b, cols], tbank[k % 2], XT["h"][:, c, b, cols].bitcast(F32),
                                            ALU.subtract).then_inc(s_tfree, 1)

            def over_experts(v):
                return v.unsqueeze(2).to_broadcast([P, NT, E0])

            def over_tokens(v):
                return v.unsqueeze(1).to_broadcast([P, NT, E0])

            def top_two(src):
                for t in range(NT):
                    ins = nc.vector.max(top[:, t, :], src[:, t, :])
                link(dve, ins)
                for t in range(NT):
                    ins = nc.vector.max_index(topi[:, t, :], top[:, t, :], src[:, t, :])
                link(dve, ins)
                link(dve, nc.vector.tensor_copy(topf[:], topi[:, :, 0:2]))
                for k in range(2):
                    ins = nc.vector.tensor_tensor(oh[:, k], over_tokens(iota8[:]), over_experts(topf[:, :, k]), ALU.is_equal)
                link(dve, ins)

            dve.wait_ge(s_in1, 16 * 4)
            normalise(dve, X, Y, NT, s_xn)
            nc.vector.tensor_copy(wrs["h"][:], wr_raw[:]).then_inc(s_wr, 1)
            dve.wait_ge(s_wr, 1)
            nc.vector.tensor_tensor(wrs["l"][:], wr_raw[:], wrs["h"][:].bitcast(F32), ALU.subtract).then_inc(s_wr, 1)
            transposed_lo(0)
            dve.wait_ge(s_route, 1)
            dve.wait_ge(s_const, 10)
            router = tbank[0][:, 0:NT * E0].rearrange("p (t e) -> p t e", t=NT)
            link(dve, nc.vector.tensor_tensor(logits[:], router, over_tokens(rb[:, 0, :]), ALU.add))
            top_two(logits)
            nc.vector.tensor_tensor(rw[:, 0, :], top[:, :, 1], top[:, :, 0], ALU.subtract).then_inc(s_rexp_in, 1)
            dve.wait_ge(s_rexp, 1)
            link(dve, nc.vector.tensor_scalar(rw[:, 2, :], rw[:, 1, :], 1.0, None, ALU.add))
            link(dve, nc.vector.reciprocal(rw[:, 2, :], rw[:, 2, :]))
            link(dve, nc.vector.tensor_tensor(rw[:, 3, :], rw[:, 1, :], rw[:, 2, :], ALU.mult))
            for k in range(2):
                ins = nc.vector.tensor_tensor(oh[:, k], oh[:, k], over_experts(rw[:, 2 + k, :]), ALU.mult)
            link(dve, ins)
            nc.vector.tensor_tensor(R[:], oh[:, 0], oh[:, 1], ALU.add).then_inc(s_R, 1)
            for j in range(4):
                dve.wait_ge(s_tj, XJ + j + 1)
                nc.vector.tensor_copy(RT[:, 4 * j:4 * j + 4, :],
                                      tbank[j % 2][0:E0].rearrange("p (t q) -> p t q", t=4)).then_inc(s_RT, 1)
            for j in range(8):
                dve.wait_ge(s_tj, XJ + 4 + j + 1)
                yt = Y[:, 2 * j:2 * j + 2, :]
                ins = nc.vector.tensor_tensor(yt, yt, tbank[j % 2].rearrange("p (t d) -> p t d", t=2), ALU.add)
                ins.then_inc(s_RT, 1)
            dve.wait_ge(s_RT, 12)

            def expert(e):
                for u in range(GR * FC):
                    n = GR * FC * e + u
                    dve.wait_ge(s_hhi, n + 1)
                    dve.wait_ge(s_hlo, n + 1)
                    nc.vector.tensor_scalar(hf[:, u % 2], hidden_banks[u % 2], b1e[:, u % FC:u % FC + 1], 0.0,
                                            ALU.add, ALU.max).then_inc(s_hf, 1)
                    if u % FC == 0 and u > 0:
                        add_group(e, u // FC - 1)
                add_group(e, GR - 1)

            def add_group(e, g):
                dve.wait_ge(s_down, GR * FC * e + FC * (g + 1) + 3)
                for t in range(4):
                    yt = Y[:, 4 * g + t, :]
                    ins = nc.vector.scalar_tensor_tensor(out=yt, in0=acc_banks[g % 2][:, t * D:t * D + D],
                                                         scalar=R[:, 4 * g + t, bass.ds(e, 1)], in1=yt,
                                                         op0=ALU.mult, op1=ALU.add)
                ins.then_inc(s_accfree, 1)

            with dve.Fori(0, E0) as e:
                expert(e)
            dve.wait_ge(s_accfree, GR * E0 + 2)
            normalise(dve, Y, Y, NT)
            link(dve, nc.vector.tensor_tensor(Y[:], Y[:], gbs[:, 0:1, :].to_broadcast([P, NT, D]), ALU.mult))
            link(dve, nc.vector.tensor_tensor(Y[:], Y[:], gbs[:, 1:2, :].to_broadcast([P, NT, D]), ALU.add))
            link(dve, nc.vector.tensor_tensor(X[:], X[:], Y[:], ALU.add))

            normalise(dve, X, Y, NT, s_xn)
            transposed_lo(1)
            nc.vector.memset(KS[32:64, :, :].bitcast(F32), 1.0).then_inc(s_ones, 1)
            nc.vector.memset(ones_row[:].bitcast(F32), 1.0).then_inc(s_ones, 1)
            nc.vector.tensor_copy(ident_r[:], ident[:]).then_inc(s_ones, 1)
            dve.wait_ge(s_const, 14)
            nc.vector.tensor_copy(mask[:], mask_f[:]).then_inc(s_ones, 1)
            dve.wait_ge(s_in2, 16 * 5)
            nc.vector.tensor_copy(bvo["h"][:], bvo_raw[:]).then_inc(s_ones, 1)
            dve.wait_ge(s_ones, 5)
            nc.vector.tensor_tensor(bvo["l"][:], bvo_raw[:], bvo["h"][:].bitcast(F32), ALU.subtract).then_inc(s_ones, 1)
            a1 = [0]

            def job(n=1):
                a1[0] += n
                dve.wait_ge(s_a1, a1[0])
                return tbank[(a1[0] - 1) % 2]

            def split_bank(src, hi, lo):
                link(dve, nc.vector.tensor_copy(hi, src))
                nc.vector.tensor_tensor(lo, src, hi.bitcast(F32), ALU.subtract).then_inc(s_a1e, 1)

            for c in range(NC):
                bk = job()[:, 0:B * SP].rearrange("p (b s) -> p b s", b=B)
                split_bank(bk, CT["h"][:, c], CT["l"][:, c])
            for c in range(NC):
                bk = job()
                link(dve, nc.vector.tensor_scalar(kf[:, c, :], bk[:, 0:B * SP], bqk[:, 1, c:c + 1], None, ALU.add))
                split_bank(kf[:, c, :], K1["h"][:, c, :], K1["l"][:, c, :])
            for b in range(B):
                bk = job()
                nc.vector.tensor_copy(V1[0:S, b, :, 0:D1], bk[0:S, 0:D].rearrange("p (h d) -> p h d", h=H1)).then_inc(s_a1e, 1)
            for b in range(B):
                for j in range(4):
                    bk = job()
                    n = 4 * b + j
                    if n >= 1:
                        dve.wait_ge(s_q1s, 2 * n)
                    nc.vector.tensor_scalar(qf[:], bk, bqk[:, 0, j // 2:j // 2 + 1], None, ALU.add).then_inc(s_q1f, 1)
                for n in range(b * H1, b * H1 + H1):
                    def max1(n):
                        dve.wait_ge(s_mx1, n + 1)
                        for a in range(2):
                            ins = nc.vector.reduce_max(m8[:, n % 2, 4 * a:4 * a + 4],
                                                       ps[:, a, 0:4 * SP].rearrange("p (t s) -> p t s", t=4), AX.X)
                        ins.then_inc(s_m8, 1)
                        dve.wait_ge(s_m8t, n + 1)
                        if n >= 2:
                            dve.wait_ge(s_row1[(n - 2) % 4], 16 * ((n - 2) // 4 + 1))
                        nc.vector.tensor_scalar(m8T[:, n % 2, :], ps[0:TB, 2, 0:P], -1.0, None, ALU.mult).then_inc(s_m8T, 1)

                    def norm1(n):
                        h = n % H1
                        dve.wait_ge(s_pv1, 2 * n + 2)
                        link(dve, nc.vector.reciprocal(rs8[:], pv1[:, :, D1]))
                        nc.vector.tensor_tensor(Y[:, TB * b:TB * b + TB, D1 * h:D1 * h + D1], pv1[:, :, 0:D1],
                                                rs8[:].unsqueeze(2).to_broadcast([P, TB, D1]), ALU.mult).then_inc(s_nm1, 1)

                    if n == b * H1:
                        max1(n)
                        max1(n + 1)
                    if n + 2 < b * H1 + H1:
                        max1(n + 2)
                    norm1(n)
            for g in range(GR):
                for c in range(NC):
                    bk = job()
                    split_bank(bk, A1T["h"][:, c, :], A1T["l"][:, c, :])
                for j in range(2):
                    bk = job()
                    xt = X[:, 4 * g + 2 * j:4 * g + 2 * j + 2, :]
                    nc.vector.tensor_tensor(xt, xt, bk.rearrange("p (t d) -> p t d", t=2), ALU.add).then_inc(s_a1e, 1)
            dve.wait_ge(s_a1e, a1[0] - 8)

            normalise(dve, X, Y, NT, s_xn)
            transposed_lo(2)
            link(dve, nc.vector.memset(ones_f[:], 1.0))
            dve.wait_ge(s_in3, 16 * 4)
            link(dve, nc.vector.tensor_copy(cwh[:], cw[:, 0, :]))
            link(dve, nc.vector.tensor_tensor(cw[:, 1, :], cw[:, 0, :], cwh[:].bitcast(F32), ALU.subtract))
            for k in range(TAPS * NC):
                for i, u in enumerate("hl"):
                    src = cwh[:, k:k + 1].bitcast(F32) if u == "h" else cw[:, 1, k:k + 1]
                    ins = nc.vector.tensor_scalar(diag[u][:, k, :], ident[:], src, None, ALU.mult)
            ins.then_inc(s_w3d, 1)
            dve.wait_ge(s_rexp, 2)
            link(dve, nc.vector.tensor_scalar(logits[:], logits[:], 1.0, None, ALU.add))
            link(dve, nc.vector.reciprocal(logits[:], logits[:]))
            link(dve, nc.vector.tensor_tensor(R[:], logits[:], over_tokens(rb[:, 1, :]), ALU.add))
            top_two(R)
            link(dve, nc.vector.tensor_tensor(oh[:, 0], oh[:, 0], oh[:, 1], ALU.add))
            link(dve, nc.vector.tensor_tensor(oh[:, 0], oh[:, 0], logits[:], ALU.mult))
            link(dve, nc.vector.reduce_sum(rw[:, 0, :], oh[:, 0], AX.X))
            link(dve, nc.vector.tensor_scalar(rw[:, 0, :], rw[:, 0, :], 1e-9, None, ALU.add))
            link(dve, nc.vector.reciprocal(rw[:, 0, :], rw[:, 0, :]))
            link(dve, nc.vector.tensor_tensor(R[:], oh[:, 0], over_experts(rw[:, 0, :]), ALU.mult))
            link(dve, nc.vector.tensor_tensor(rw[:, 1, :], R[:, :, EM], R[:, :, EM + 2], ALU.add))

            def own_terms(g):
                ys, xs = Y[:, 4 * g:4 * g + 4, :], X[:, 4 * g:4 * g + 4, :]
                link(dve, nc.vector.tensor_scalar(reluY[:], ys, 0.0, None, ALU.max))
                for t in range(4):
                    ins = nc.vector.scalar_tensor_tensor(out=xs[:, t, :], in0=ys[:, t, :], scalar=rw[:, 1, 4 * g + t:4 * g + t + 1],
                                                         in1=xs[:, t, :], op0=ALU.mult, op1=ALU.add)
                link(dve, ins)
                for t in range(4):
                    ins = nc.vector.scalar_tensor_tensor(out=xs[:, t, :], in0=reluY[:, t, :],
                                                         scalar=R[:, 4 * g + t, E1 - 1:E1],
                                                         in1=xs[:, t, :], op0=ALU.mult, op1=ALU.add)
                link(dve, ins)
                for j in range(2):
                    dve.wait_ge(s_conv, 2 * g + j + 1)
                    x2 = xs[:, 2 * j:2 * j + 2, :]
                    ins = nc.vector.tensor_tensor(x2, x2, ps[:, 7, :].rearrange("p (t d) -> p t d", t=2), ALU.add)
                    ins.then_inc(s_convfree, 1)
                dve.wait_ge(s_convfree, 2 * g + 2)

            def gate(n):
                dve.wait_ge(s_silu, n + 1)
                if n >= 2:
                    dve.wait_ge(s_glo, n - 1)
                nc.vector.tensor_tensor(gated[:, n % 2], silu[:, n % 2], up_banks[n % 2], ALU.mult).then_inc(s_gated, 1)

            def add1(n):
                g, e = divmod(n, EM)
                for t in range(4):
                    if t % 2 == 0:
                        dve.wait_ge(s_dn1h, 2 * n + t // 2 + 1)
                    xt = X[:, 4 * g + t, :]
                    ins = nc.vector.scalar_tensor_tensor(out=xt, in0=down_banks[t // 2][:, t % 2 * D:t % 2 * D + D],
                                                         scalar=R[:, 4 * g + t, e:e + 1], in1=xt, op0=ALU.mult, op1=ALU.add)
                    ins.then_inc(s_acc1, 1)
                dve.wait_ge(s_acc1, 4 * n + 4)

            for n in range(GR * EM):
                gate(n)
                if n % EM == 0:
                    own_terms(n // EM)
                if n >= 1:
                    add1(n - 1)
            add1(GR * EM - 1)

        @block.tensor
        def _(pe):
            pe.wait_ge(s_const, 7)
            pe.wait_ge(s_lnc, 1)
            pe.wait_ge(s_ln, 1)
            for k, (b, c, h) in enumerate(LATJOBS):
                if k >= 2:
                    pe.wait_ge(s_lat_f, k - 1)
                if h < 2:
                    for t in range(4):
                        mm = nc.tensor.transpose(shared[k % 2][:, t * P:t * P + P],
                                                 Y[:, b * TB + 4 * h + t, c * P:c * P + P], ident[:])
                else:
                    mm = nc.tensor.transpose(shared[k % 2][:, 0:SP], C[0:SP, b, c * P:c * P + P], ident[0:SP, 0:SP])
                mm.then_inc(s_lat_full, 1)

            def product(o, pairs, **kw):
                n = len(pairs)
                for k, (l, r) in enumerate(pairs):
                    mm = nc.tensor.matmul(o, l, r, start=(k == 0), stop=(k == n - 1), **kw)
                return mm

            def project_qk(j, nb, job, bk):
                pe.wait_ge(s_jobfree, job + 1)
                cols = (slice(0, HALF), slice(HALF, T), slice(0, HALF), slice(HALF, T), slice(T, NK))[j]
                product(bk[:, 0:cols.stop - cols.start],
                        [(wqk[u][:, c, j // 2 if j < 4 else 1, :], lat[v][:, nb, c, cols])
                         for c in range(NC) for u, v in RANDL]).then_inc(s_job, 1)

            def max_tile(h, t, n):
                pe.wait_ge(s_mxfree, n + 1)
                r = slice(HD * h, HD * h + HD)
                q = Q["h"][r, t * P:t * P + P]
                for a in range(2):
                    nc.tensor.matmul(max_banks[:, a * HALF:a * HALF + HALF], q, K["h"][r, a * HALF:a * HALF + HALF],
                                     start=True, stop=True)
                nc.tensor.matmul(small_bank[:, t % 4 * SP:t % 4 * SP + SP], q, K["h"][r, T:NK],
                                 start=True, stop=True).then_inc(s_mx, 1)

            def max_turn(k):
                pe.wait_ge(s_max, k + 1)
                nc.tensor.transpose(small_bank[0:TB, 0:P], maxs[:], ident[:]).then_inc(s_maxT, 1)

            pe.wait_ge(s_lat_lo, len(LATJOBS))
            pe.wait_ge(s_wqk, 2)
            for j in range(5):
                project_qk(j, 0, j, shared[j % 2])
            pe.wait_ge(s_jobfree, 5 + 2)
            for t in range(TB):
                max_tile(0, t, t)
            max_turn(0)

            def values(g, b):
                pe.wait_ge(s_wv, 2 * g + 2)
                for j in range(3):
                    pe.wait_ge(s_jobfree, jobs_before(g) + j + 1)
                    for k in range(4 * j, min(4 * j + 4, KT)):
                        m = P if k < TB else S
                        mm = product(bank(j)[0:m, (k % 4) * P:(k % 4) * P + P],
                                     [(lat[u][:, b, c, k * P:k * P + m], wv[v][:, c, :])
                                      for c in range(NC) for u, v in RANDL])
                    mm.then_inc(s_job, 1)

            def scores(g, s):
                h, half, kt = s // (2 * KT), s // KT % 2, s % KT
                m = P if kt < TB else S
                pe.wait_ge(s_exp, 36 * g + s + 1)
                if s % (2 * KT) == 0:
                    pe.wait_ge(s_stack[h], 96 * g + 96)
                    pe.wait_ge(s_row[h], 16 * g + 16)
                o = score_banks[s % 2][0:m]
                q, k = slice(HALF * half, HALF * half + HALF), slice(kt * P, kt * P + m)
                nc.tensor.matmul(o, KA[h][:, k], QA[h][:, q], start=True, stop=False)
                nc.tensor.matmul(o, KB[h][0:HD + 1, k], QB[h][0:HD + 1, q], start=False, stop=True) \
                    .then_inc(s_score, 1)

            def attend(g, s):
                h, kt = s // (2 * KT), s % KT
                m = P if kt < TB else S
                pe.wait_ge(s_exp, 36 * g + s + 1 + 2)
                if kt == 0:
                    pe.wait_ge(s_norm, 4 * g + s // KT + 1)
                for q in range(4):
                    mm = nc.tensor.matmul(pv_bank[:, q, :], PT[0:m, s % 3, q * P:q * P + P], V[0:m, kt, h, :],
                                          start=(kt == 0 and q == 0), stop=(kt == KT - 1), skip_group_check=True)
                mm.then_inc(s_pv, 1)

            def turn(b, i, g, nb):
                values(g, b)
                for s in range(STEPS):
                    scores(g, s)
                    if s == 1:
                        pe.wait_ge(s_jobfree, jobs_before(g) + 3 + 2)
                    if s >= 1:
                        attend(g, s - 1)
                    if M1_AT <= s < M1_AT + TB:
                        if s == M1_AT:
                            pe.wait_ge(s_maxrow, 2 * g + 1)
                        max_tile(1, s - M1_AT, 16 * g + 8 + s - M1_AT)
                    if s == M1_T:
                        max_turn(2 * g + 1)
                    if nb is not None:
                        if QK_AT <= s < QK_AT + 5:
                            if s == QK_AT:
                                pe.wait_ge(s_wqk, 2 * g + 4)
                            project_qk(s - QK_AT, nb, jobs_before(g) + 3 + s - QK_AT, bank(3 + s - QK_AT))
                        if M0_AT <= s < M0_AT + TB:
                            if s == M0_AT:
                                pe.wait_ge(s_jobfree, jobs_before(g) + 8 + 2)
                                pe.wait_ge(s_maxrow, 2 * g + 2)
                            max_tile(0, s - M0_AT, 16 * g + 16 + s - M0_AT)
                        if s == M0_T:
                            max_turn(2 * g + 2)
                attend(g, STEPS - 1)
                a = 8 if nb is not None else 3
                pe.wait_ge(s_norm, 4 * g + 5)
                for j in range(2):
                    pe.wait_ge(s_jobfree, jobs_before(g) + a + j + 1)
                    for t in range(4):
                        mm = nc.tensor.transpose(bank(a + j)[:, t * P:t * P + P], AT[:, 4 * j + t, :], ident[:])
                    mm.then_inc(s_job, 1)
                pe.wait_ge(s_wo, 2 * g + 2)
                for j in range(4):
                    if j % 2 == 0:
                        pe.wait_ge(s_jobfree, jobs_before(g) + a + j // 2 + 1 + 2)
                    pe.wait_ge(s_jobfree, jobs_before(g) + a + 2 + j + 1)
                    for t in range(2):
                        q = slice((2 * j + t) * P, (2 * j + t + 1) * P)
                        mm = product(bank(a + 2 + j)[:, t * D:t * D + D],
                                     [(ATT[u][:, q], wo[v][:]) for u, v in RANDL])
                    mm.then_inc(s_job, 1)

            turns(pe, turn)

            def transposes(z):
                pe.wait_ge(s_xn, z + 1)
                for k, (c, b, h) in enumerate(TJOBS):
                    if z == 0 and k < 2:
                        pe.wait_ge(s_jobfree, ATT0_JOBS + 2)
                    if k >= 2:
                        pe.wait_ge(s_tfree, 8 * z + k - 1)
                    for t in range(4):
                        mm = nc.tensor.transpose(tbank[k % 2][:, t * P:t * P + P],
                                                 Y[:, b * TB + 4 * h + t, c * P:c * P + P], ident[:])
                    mm.then_inc(s_tj, 1)

            def tokens(u, c, t):
                return XT[u][:, c, t // TB, PAD + t % TB * P:PAD + t % TB * P + P]

            def group(u, c, g):
                return XT[u][:, c, g // 2, PAD + HALF * (g % 2):PAD + HALF * (g % 2) + HALF]

            def route(z, layer):
                pe.wait_ge(s_tfree, 8 * z + 8)
                pe.wait_ge(s_wr, 2)
                for t in range(NT):
                    mm = product(tbank[0][:, t * E0:t * E0 + E0],
                                 [(tokens(u, c, t), wrs[v][:, layer, c, :]) for c in range(NC) for u, v in RANDL])
                mm.then_inc(s_route, 1)

            transposes(0)
            route(0, 0)
            pe.wait_ge(s_R, 1)
            for j in range(4):
                if j >= 2:
                    pe.wait_ge(s_RT, j - 1)
                for t in range(4):
                    mm = nc.tensor.transpose(tbank[j % 2][0:E0, t * P:t * P + P], R[:, 4 * j + t, :], ident[:])
                mm.then_inc(s_tj, 1)
            for j in range(8):
                pe.wait_ge(s_RT, 4 if j < 1 else 4 + j - 1)
                for t in range(2):
                    mm = nc.tensor.matmul(tbank[j % 2][:, t * D:t * D + D], RT[:, 2 * j + t, :], b2s[:],
                                          start=True, stop=True)
                mm.then_inc(s_tj, 1)

            def up(e, u):
                n = GR * FC * e + u
                g, f = divmod(u, FC)
                pe.wait_ge(s_hf, n + 1)
                if g == 0:
                    pe.wait_ge(s_w1, 2 * FC * e + 2 * f + 2)
                product(hidden_banks[u % 2], [(w1s[a][:, f, c * P:c * P + P], group(b, c, g))
                                              for c in range(NC) for a, b in RANDL]).then_inc(s_up, 1)

            def down(e, u):
                n = GR * FC * e + u
                g, f = divmod(u, FC)
                if f == 0:
                    pe.wait_ge(s_accfree, GR * e + g + 1)
                if g == 0:
                    pe.wait_ge(s_w2, 2 * FC * e + 2 * f + 2)
                pe.wait_ge(s_hlo, n + 1 + 2)
                for t in range(4):
                    o = acc_banks[g % 2][:, t * D:t * D + D]
                    for k, (a, b) in enumerate(RANDL):
                        mm = nc.tensor.matmul(o, hs[a][:, u % 3, t * P:t * P + P], w2s[b][:, f, :],
                                              start=(f == 0 and k == 0 and t % 2 == 0), stop=(f == FC - 1 and k == 2),
                                              skip_group_check=True)
                mm.then_inc(s_down, 1)

            def expert(e):
                for u in range(GR * FC):
                    up(e, u)
                    if u >= 1:
                        down(e, u - 1)
                down(e, GR * FC - 1)

            with pe.Fori(0, E0) as e:
                expert(e)

            transposes(1)
            pe.wait_ge(s_tfree, 16)
            pe.wait_ge(s_ones, 6)
            pe.wait_ge(s_in2, 16 * 5)
            a1 = [0]

            def job():
                a1[0] += 1
                if a1[0] > 2:
                    need = a1[0] - 2
                    if need <= 6:
                        pe.wait_ge(s_a1e, need)
                    elif need <= 14:
                        pe.wait_ge(s_q1f, need - 6)
                    else:
                        pe.wait_ge(s_a1e, need - 8)
                return tbank[(a1[0] - 1) % 2]

            for c in range(NC):
                bk = job()
                for b in range(B):
                    mm = nc.tensor.transpose(bk[:, b * SP:b * SP + SP], C1[0:SP, b, c * P:c * P + P], ident[0:SP, 0:SP])
                mm.then_inc(s_a1, 1)
            pe.wait_ge(s_a1e, NC)
            pe.wait_ge(s_wa, 2)
            for ic in range(NC):
                product(job()[:, 0:B * SP], [(wa[u][:, 1, c, ic * P:ic * P + P], CT[v][:, c].rearrange("p b s -> p (b s)"))
                                             for c in range(NC) for u, v in RANDL]).then_inc(s_a1, 1)
            for b in range(B):
                product(job()[0:S, 0:D], [(CT[u][:, c, b, 0:S], wa[v][:, 2, c, :]) for c in range(NC) for u, v in RANDL]
                        + [(ones_row[:, 0:S], bvo[u][:, 0, :]) for u in "hl"]).then_inc(s_a1, 1)

            def max1(n):
                pe.wait_ge(s_st1[n % 4], 96 * (n // 4 + 1))
                if n >= 1:
                    pe.wait_ge(s_m8, n)
                for t in range(TB):
                    o = ps[:, t // 4, t % 4 * SP:t % 4 * SP + SP]
                    mm = nc.tensor.matmul(o, QS[0:3 * D1, n % 4, t * P:t * P + P], KS[0:3 * D1, n % 4, :],
                                          start=True, stop=(t > 0))
                    if t == 0:
                        mm = nc.tensor.matmul(o, ident_r[:], mask[:, 0, 0:SP], start=False, stop=True)
                mm.then_inc(s_mx1, 1)
                pe.wait_ge(s_m8, n + 1)
                if n >= 1:
                    pe.wait_ge(s_m8T, n)
                nc.tensor.transpose(ps[0:TB, 2, 0:P], m8[:, n % 2, :], ident[:]).then_inc(s_m8t, 1)

            def scores1(n):
                pe.wait_ge(s_row1[n % 4], 16 * (n // 4 + 1))
                for a in range(2):
                    k = 2 * n + a
                    if k >= 2:
                        pe.wait_ge(s_ex1, k - 1)
                    mm = nc.tensor.matmul(score1[k % 2], KS[0:3 * D1 + 1, n % 4, 0:S],
                                          QS[0:3 * D1 + 1, n % 4, HALF * a:HALF * a + HALF], start=True, stop=(a == 1))
                    if a == 0:
                        mm = nc.tensor.matmul(score1[k % 2][:, 0:P], ident_r[0:S, 0:S], mask[0:S, 1, :],
                                              start=False, stop=True)
                    mm.then_inc(s_sc1, 1)

            def attend1(n):
                b, h = divmod(n, H1)
                for a in range(2):
                    k = 2 * n + a
                    pe.wait_ge(s_ex1, k + 1)
                    if a == 0 and n >= 1:
                        pe.wait_ge(s_nm1, n)
                    for t in range(4):
                        mm = nc.tensor.matmul(pv1[:, 4 * a + t, :], PT1[0:S, k % 3, t * P:t * P + P], V1[0:S, b, h, :],
                                              start=True, stop=True)
                    mm.then_inc(s_pv1, 1)

            for b in range(B):
                for j in range(4):
                    ic, h = divmod(j, 2)
                    product(job(), [(wa[u][:, 0, c, ic * P:ic * P + P], group(v, c, 2 * b + h))
                                    for c in range(NC) for u, v in RANDL]).then_inc(s_a1, 1)
                last = b * H1 + H1
                max1(b * H1)
                max1(b * H1 + 1)
                for n in range(b * H1, last):
                    scores1(n)
                    if n + 2 < last:
                        max1(n + 2)
                    attend1(n)
            pe.wait_ge(s_nm1, B * H1)
            for g in range(GR):
                for c in range(NC):
                    bk = job()
                    for t in range(4):
                        mm = nc.tensor.transpose(bk[:, t * P:t * P + P], Y[:, 4 * g + t, c * P:c * P + P], ident[:])
                    mm.then_inc(s_a1, 1)
                pe.wait_ge(s_a1e, 6 + 4 * g + 2)
                for j in range(2):
                    bk = job()
                    for t in range(2):
                        q = slice((2 * j + t) * P, (2 * j + t) * P + P)
                        mm = product(bk[:, t * D:t * D + D],
                                     [(A1T[u][:, c, q], wa[v][:, 3, c, :]) for c in range(NC) for u, v in RANDL]
                                     + [(ones_row[:], bvo[u][:, 1, :]) for u in "hl"])
                    mm.then_inc(s_a1, 1)

            transposes(2)
            route(2, 1)

            def gate_up(n):
                g, e = divmod(n, EM)
                if n >= 2:
                    pe.wait_ge(s_gated, n - 1)
                for a, bk in enumerate((gate_banks[n % 2], up_banks[n % 2])):
                    product(bk, [(wgus[u][:, e, a, c, :], group(v, c, g))
                                 for c in range(NC) for u, v in RANDL]).then_inc(s_gu, 1)

            def down1(n):
                g, e = divmod(n, EM)
                pe.wait_ge(s_glo, n + 1)
                for t in range(4):
                    if n >= 1 and t % 2 == 0:
                        pe.wait_ge(s_acc1, 4 * (n - 1) + t + 2)
                    mm = product(down_banks[t // 2][:, t % 2 * D:t % 2 * D + D],
                                 [(gs[u][:, n % 3, t * P:t * P + P], wds[v][:, e, :]) for u, v in RANDL])
                    if t % 2 == 1:
                        mm.then_inc(s_dn1h, 1)
                return mm

            def conv(k):
                if k >= 1:
                    pe.wait_ge(s_convfree, k)
                for t in (2 * k, 2 * k + 1):
                    first = t % TB * P
                    for c in range(NC):
                        o = ps[:, 7, t % 2 * D + c * P:t % 2 * D + c * P + P]
                        ops = [(XT[u][:, c, t // TB, PAD - (TAPS - 1) + j + first:PAD - (TAPS - 1) + j + first + P],
                                diag[v][:, j * NC + c, :]) for j in range(TAPS) for u, v in RANDL]
                        ops.append((ones_f[:], cb[:, c * P:c * P + P]))
                        mm = product(o, ops)
                mm.then_inc(s_conv, 1)

            pe.wait_ge(s_w3, 4)
            for n in range(GR * EM):
                gate_up(n)
                if n % EM == 0:
                    if n == 0:
                        pe.wait_ge(s_w3d, 1)
                    conv(n // 2)
                if n % EM == 1:
                    conv(n // 2 + 1)
                if n >= 1:
                    down1(n - 1)
            down1(GR * EM - 1)


def kernel(**inputs):
    import numpy as np
    import concourse.bacc as bacc
    from concourse.bass_utils import run_bass_kernel_spmd

    a = {k: np.asarray(v) for k, v in inputs.items()}

    def col(v):
        return np.ascontiguousarray(v.reshape(-1, P).T)

    def pairs(w):
        return w.reshape(NC, P, PAIRS, P).transpose(2, 1, 0, 3)

    def chunks(w):
        return w.reshape(NC, P, -1).transpose(1, 0, 2)

    wkv = a["L0_xattn_Wkv"]
    arrays = {
        "x": a["x"], "ctx": a["ctx_1024"],
        "ln1w": col(a["L0_xattn_ln1_w"]), "ln1b": col(a["L0_xattn_ln1_b"]),
        "ln2w": col(a["L0_xattn_ln2_w"]), "ln2b": col(a["L0_xattn_ln2_b"]),
        "wqk0": np.stack([pairs(a["L0_xattn_Wq"]), pairs(wkv[:, :1024])], axis=3),
        "wv0": pairs(wkv[:, 1024:]),
        "wo0": a["L0_xattn_Wo"].reshape(PAIRS, P, D),
        "wr": np.stack([chunks(a["L0_ffn_Wr"].T), chunks(a["L1_ffn_Wr"])], axis=1),
        "rbias": np.stack([a["L0_ffn_br"], a["L1_ffn_router_bias"]]),
        "w1": a["L0_ffn_W1"].reshape(E0, FC, P, NC, P).transpose(0, 4, 1, 3, 2).reshape(E0, P, FC, NC * P),
        "b1": a["L0_ffn_b1"].reshape(E0, FC, P).transpose(0, 2, 1),
        "w2": a["L0_ffn_W2"].reshape(E0, D, FC, P).transpose(0, 3, 2, 1),
        "b2": a["L0_ffn_b2"],
        "gb": np.stack([a["L0_ffn_gamma"], a["L0_ffn_beta"]]),
        "watt": np.stack([chunks(a["L1_xattn_W" + k].T) for k in "qkvo"], axis=1),
        "bqk1": np.stack([col(a["L1_xattn_b" + k]) for k in "qk"], axis=1),
        "bvo1": np.stack([a["L1_xattn_b" + k] for k in "vo"])[None],
        "wgu": np.stack([a["L1_ffn_Wg"], a["L1_ffn_Wu"]]).reshape(2, EM, NC, P, P).transpose(3, 1, 0, 2, 4),
        "wd": a["L1_ffn_Wd"].transpose(1, 0, 2),
        "convw": a["L1_ffn_conv_w"].reshape(TAPS, NC, P).transpose(2, 0, 1).reshape(P, TAPS * NC),
        "convb": a["L1_ffn_conv_b"].reshape(1, D),
    }
    arrays = {k: np.ascontiguousarray(v) for k, v in arrays.items()}
    nc = bacc.Bacc("TRN2", target_bir_lowering=False, num_devices=1)
    args = [nc.dram_tensor(k, v.shape, mybir.dt.from_np(v.dtype), kind="ExternalInput").ap() for k, v in arrays.items()]
    out = nc.dram_tensor("out", (B, T, D), F32, kind="ExternalOutput").ap()
    program(nc, *args, out)
    r = run_bass_kernel_spmd(nc, [arrays], core_ids=[0])
    return r.results[0]["out"]
```

```python
from contextlib import ExitStack

import concourse.bass as bass
from concourse import mybir

P = 128
ALU = mybir.AluOpType
ACT = mybir.ActivationFunctionType
AX = mybir.AxisListType
F32 = mybir.dt.float32
F32R = mybir.dt.float32r
U32 = mybir.dt.uint32
BF16 = mybir.dt.bfloat16
F16 = mybir.dt.float16
RMAX = bass.bass_isa.ReduceOp.max

B, T, D = 2, 1024, 256
S = 77
SP = S + 1
NC = D // P
NT = B * T // P
TB = T // P
HD = 64
PAIRS = 1024 // P
KT = TB + 1
NK = T + SP
NKP = NK + 2
HALF = 512
EPS = 1e-5
STEPS = 4 * KT
RING = 6
AHEAD = 3
JOBS = 12
VJOBS = 2 * KT
AWJOBS = 6
CASTS = 7
E0, F0 = 8, 1024
FC = F0 // P
GR = B * T // HALF
E1, EM = 8, 4
TAPS = 4
PAD = 4
H1, D1 = 16, 16
HC = P // D1
K1S = 2 * H1 * B
RING1 = 4
XJ = 2 * GR
RANDL = (("h", "h"), ("h", "l"), ("l", "h"))


def program(nc, x, ctx, ln1w, ln1b, ln2w, ln2b, wqk0, wv0, wo0, wr, rbias, w1, b1, w2, b2, gb,
            watt, bqk1, bvo1, wgu, wd, convw, convb, out):
    stack = ExitStack()
    with stack:
        def sb(name, shape, dt=F32):
            return stack.enter_context(nc.sbuf_tensor(name, shape, dt))

        def sem(name):
            return stack.enter_context(nc.semaphore(name))

        ps = stack.enter_context(nc.psum_tensor("ps", [P, 8, HALF], F32))
        score_banks = [ps[:, 0, :], ps[:, 1, :]]
        max_banks = ps[:, 2:4, :].rearrange("p a n -> p (a n)")
        small_bank = ps[:, 4, :]
        shared = [ps[:, 5, :], ps[:, 6, :]]
        pv_bank = ps[:, 7, 0:4 * (HD + 1)].rearrange("p (q d) -> p q d", q=4)

        X = sb("X", [P, NT, D])
        with ExitStack() as early:
            Y = early.enter_context(nc.sbuf_tensor("Y", [P, NT, D], F32))
        wv = {k: sb("wv_" + k, [P, NC, KT * P - P], F32R) for k in "hl"}
        ident = sb("ident", [P, P])
        stats = sb("stats", [P, NT, 6])
        ln_tmp = sb("ln_tmp", [P, 6, NT])
        nhalf = sb("nhalf", [P, NT])
        zeros = sb("zeros", [P, 1])
        st0 = ExitStack()

        def sb0(name, shape, dt=F32):
            return st0.enter_context(nc.sbuf_tensor(name, shape, dt))

        C = sb0("C", [P, B, D])
        lnp = sb0("lnp", [P, 4, NC])
        lat = {k: sb0("lat_" + k, [P, B, NC, NKP], F32R) for k in "hl"}
        latf = sb0("latf", [P, HALF])
        wqk_raw = sb0("wqk_raw", [P, NC, 2, P])
        wo_raw = sb0("wo_raw", [P, D])
        wqk = {k: sb0("wqk_" + k, [P, NC, 2, P], F32R) for k in "hl"}
        wo = {k: sb0("wo_" + k, [P, D], F32R) for k in "hl"}
        Q = {k: sb0("Q_" + k, [P, T], F32R) for k in "hl"}
        K = {k: sb0("K_" + k, [P, NKP], F32R) for k in "hl"}
        QA = [sb0(f"QA{h}", [P, T], F32R) for h in range(2)]
        QB = [sb0(f"QB{h}", [P, T], F32R) for h in range(2)]
        KA = [sb0(f"KA{h}", [P, NKP], F32R) for h in range(2)]
        KB = [sb0(f"KB{h}", [P, NKP], F32R) for h in range(2)]
        V = {k: sb0("V_" + k, [P, KT, 2 * PAIRS, HD + 1], F16) for k in "hl"}
        PT = sb0("PT", [P, RING, HALF])
        PR = sb0("PR", [P, RING, HALF], F16)
        AT = sb0("AT", [P, TB, P])
        with ExitStack() as early:
            wv_raw = early.enter_context(nc.sbuf_tensor("wv_raw", [P, NC, KT * P - P], F32))
        ATT = {k: sb0("ATT_" + k, [P, T], F32R) for k in "hl"}
        bounds = sb0("bounds", [P, 2])
        bound = sb0("bound", [P, 2])
        vs = sb0("vs", [P, 4])
        rsum = sb0("rsum", [P, 4])
        mxs = sb0("mxs", [P, 3, TB])
        maxs = sb0("maxs", [P, TB])
        maxT = [sb0(f"maxT{h}", [TB, P], F32R) for h in range(2)]
        st0.close()

        XT = {k: sb("XT_" + k, [P, NC, B, PAD + T], F32R) for k in "hl"}
        wr_raw = sb("wr_raw", [P, 2, NC, E0])
        wrs = {k: sb("wr_" + k, [P, 2, NC, E0], F32R) for k in "hl"}
        rb = sb("rb", [P, 2, E0])
        iota8 = sb("iota8", [P, E0])
        logits = sb("logits", [P, NT, E0])
        top = sb("top", [P, NT, 8])
        topi = sb("topi", [P, NT, 8], U32)
        topf = sb("topf", [P, NT, 2])
        rw = sb("rw", [P, 4, NT])
        oh = sb("oh", [P, 2, NT, E0])
        R = sb("R", [P, NT, E0])
        gbs = sb("gbs", [P, 2, D])
        st1 = ExitStack()

        def sb1(name, shape, dt=F32):
            return st1.enter_context(nc.sbuf_tensor(name, shape, dt))

        RT = sb1("RT", [E0, NT, P])
        b2s = sb1("b2s", [E0, D])
        b1e = sb1("b1e", [P, 2, FC])
        w1_raw = sb1("w1_raw", [P, FC, NC * P])
        w2_raw = sb1("w2_raw", [P, FC, D])
        w1s = {k: sb1("w1_" + k, [P, 2, FC, NC * P], F32R) for k in "hl"}
        w2s = {k: sb1("w2_" + k, [P, 2, FC, D], F32R) for k in "hl"}
        hf = sb1("hf", [P, 2, HALF])
        hs = {k: sb1("h_" + k, [P, 4, HALF], F32R) for k in "hl"}
        st1.close()
        st2 = ExitStack()

        def sb2(name, shape, dt=F32):
            return st2.enter_context(nc.sbuf_tensor(name, shape, dt))

        C1 = sb2("C1", [P, B, D])
        CT = {k: sb2("CT_" + k, [P, NC, B, SP], F32R) for k in "hl"}
        wa_raw = sb2("wa_raw", [P, 4, NC, D])
        wa = {k: sb2("wa_" + k, [P, 4, NC, D], F32R) for k in "hl"}
        bqk = sb2("bqk", [P, 2, NC])
        bvo_raw = sb2("bvo_raw", [1, 2, D])
        bvo = {k: sb2("bvo_" + k, [1, 2, D], F32R) for k in "hl"}
        ones_row = sb2("ones_row", [1, P], F32R)
        ident_r = sb2("ident_r", [P, P], F32R)
        mask_f = sb2("mask_f", [P, 2, P])
        mask = sb2("mask", [P, 2, P], F32R)
        mask4 = sb2("mask4", [P, HC // 2, SP], F32R)
        hmask = sb2("hmask", [P, HC])
        sel = sb2("sel", [H1, H1, SP], F32R)
        K1 = {k: sb2("K1_" + k, [P, NC, B * SP], F32R) for k in "hl"}
        KD = {k: sb2("KD_" + k, [P, B, NC, HC, SP], F32R) for k in "hl"}
        V1f = sb2("V1f", [P, B, H1, D1])
        V1 = {k: sb2("V1_" + k, [P, B, H1, D1 + 1], F16) for k in "hl"}
        vb = sb2("vb", [P, 2])
        vs1 = sb2("vs1", [P, 3])
        Q1 = {k: sb2("Q1_" + k, [P, NC, B, T], F32R) for k in "hl"}
        m1 = sb2("m1", [P, B, TB, H1])
        NM = sb2("NM", [H1, B, T], F32R)
        PT1 = sb2("PT1", [P, RING1, HALF])
        PR1 = sb2("PR1", [P, RING1, HALF], F16)
        rs8 = sb2("rs8", [P, TB])
        A1T = {k: sb2("A1T_" + k, [P, NC, HALF], F32R) for k in "hl"}
        st2.close()
        st3 = ExitStack()

        def sb3(name, shape, dt=F32):
            return st3.enter_context(nc.sbuf_tensor(name, shape, dt))

        wgu_raw = sb3("wgu_raw", [P, EM, 2, NC, P])
        wgus = {k: sb3("wgu_" + k, [P, EM, 2, NC, P], F32R) for k in "hl"}
        wd_raw = sb3("wd_raw", [P, EM, D])
        wds = {k: sb3("wd_" + k, [P, EM, D], F32R) for k in "hl"}
        cw = sb3("cw", [P, 2, TAPS * NC])
        cwh = sb3("cwh", [P, TAPS * NC], F32R)
        diag = {k: sb3("diag_" + k, [P, TAPS * NC, P], F32R) for k in "hl"}
        cb = sb3("cb", [1, D])
        ones_f = sb3("ones_f", [1, P])
        silu = sb3("silu", [P, 2, HALF])
        gated = sb3("gated", [P, 2, HALF])
        gs = {k: sb3("g_" + k, [P, 3, HALF], F32R) for k in "hl"}
        reluY = sb3("reluY", [P, 4, D])
        st3.close()

        s_in = sem("inputs_loaded")
        s_zero = sem("context_cleared")
        s_const = sem("constants_ready")
        s_dve = sem("vector_chain")
        s_var = sem("variances_ready")
        s_rstd = sem("rstds_ready")
        s_lnc = sem("context_normalised")
        s_ln = sem("latents_normalised")
        s_lat_full = sem("latent_bank_full")
        s_lat_hi = sem("latent_hi_ready")
        s_lat_f = sem("latent_full_ready")
        s_lat_lo = sem("latent_lo_ready")
        s_wqk_raw, s_wv_raw, s_wo_raw = sem("wqk_loaded"), sem("wv_loaded"), sem("wo_loaded")
        s_wqk, s_wv, s_wo = sem("wqk_split"), sem("wv_split"), sem("wo_split")
        s_bounds, s_bound, s_vs = sem("bounds_by_partition"), sem("bounds_ready"), sem("value_scale_ready")
        s_rem_pool, s_rem_dve = sem("remainders_by_gpsimd"), sem("remainders_by_vector")
        s_job = sem("shared_bank_full")
        s_cast = sem("shared_bank_rounded")
        s_jobfree = sem("shared_bank_free")
        s_mx = sem("max_bank_full")
        s_mxfree = sem("max_bank_free")
        s_max = sem("head_max_ready")
        s_maxT = sem("head_max_transposed")
        s_maxrow = sem("head_max_row_ready")
        s_stack = [sem("stack0_loaded"), sem("stack1_loaded")]
        s_row = [sem("max_row0_loaded"), sem("max_row1_loaded")]
        s_score = sem("scores_ready")
        s_exp = sem("exp_done")
        s_pv = sem("pv_done")
        s_rec = sem("sums_inverted")
        s_norm = sem("attention_normalised")
        s_out = sem("output_written")
        s_in1 = sem("expert_inputs_loaded")
        s_xn = sem("tokens_normalised")
        s_tj = sem("transposed_bank_full")
        s_thi = sem("transposed_hi_ready")
        s_tfree = sem("transposed_bank_free")
        s_wr = sem("router_weights_split")
        s_route = sem("router_logits_ready")
        s_rexp_in = sem("router_exponents_ready")
        s_rexp = sem("router_exp_done")
        s_R = sem("routing_weights_ready")
        s_RT = sem("routing_weights_transposed")
        s_w1_raw, s_w2_raw = sem("w1_loaded"), sem("w2_loaded")
        s_w1, s_w2 = sem("w1_split"), sem("w2_split")
        s_b1e = [sem("even_expert_biases_loaded"), sem("odd_expert_biases_loaded")]
        s_up = sem("hidden_bank_full")
        s_hhi = sem("hidden_hi_ready")
        s_hf = sem("hidden_bank_free")
        s_hlo = sem("hidden_lo_ready")
        s_down = sem("hidden_used")
        s_accfree = sem("output_banks_free")
        s_in2 = sem("layer1_attention_loaded")
        s_wa = sem("layer1_weights_split")
        s_wah = sem("layer1_weights_rounded")
        s_a1 = sem("layer1_bank_full")
        s_a1h = sem("layer1_bank_rounded")
        s_a1e = sem("layer1_bank_free")
        s_kd = sem("layer1_key_blocks_hi")
        s_kdl = sem("layer1_key_blocks_lo")
        s_vb, s_vbr = sem("layer1_value_bounds"), sem("layer1_value_bound_ready")
        s_v1 = sem("layer1_values_ready")
        s_mx1 = sem("layer1_max_banks_full")
        s_m8 = sem("layer1_max_ready")
        s_sc1 = sem("layer1_scores_ready")
        s_ex1 = sem("layer1_exp_done")
        s_r1p, s_r1v = sem("layer1_remainders_by_gpsimd"), sem("layer1_remainders_by_vector")
        s_pv1 = sem("layer1_pv_done")
        s_rs1 = sem("layer1_sums_inverted")
        s_nm1 = sem("layer1_attention_normalised")
        s_in3 = sem("layer1_experts_loaded")
        s_w3 = sem("layer1_expert_weights_split")
        s_conv = sem("convolution_bank_full")
        s_convfree = sem("convolution_bank_free")
        s_gu = sem("gate_and_up_full")
        s_silu = sem("silu_ready")
        s_gated = sem("gated_ready")
        s_ghi = sem("gated_hi_ready")
        s_glo = sem("gated_lo_ready")
        s_acc1 = sem("layer1_down_added")
        s_dn1h = sem("layer1_down_half_full")
        s_w3d = sem("tap_diagonals_ready")
        s_ones = sem("layer1_constants_ready")

        def flat4(t):
            return t[:].rearrange("p a b c -> p (a b c)")

        def flat(t):
            return t[:] if len(t.shape) == 2 else t[:].rearrange(
                "p a b -> p (a b)" if len(t.shape) == 3 else "p a b c -> p (a b c)")

        chain = [0]

        def link(dve, ins):
            chain[0] += 1
            ins.then_inc(s_dve, 1)
            dve.wait_ge(s_dve, chain[0])

        lns = [0]

        def normalise(dve, src, dst, n, last=None):
            for t in range(n):
                ins = nc.vector.bn_stats(stats[:, t, :], src[:, t, :])
            link(dve, ins)
            me, mo = stats[:, 0:n, 1], stats[:, 0:n, 4]
            mean, dif, m2, var, rstd, sq = (ln_tmp[:, i, 0:n] for i in range(6))
            nc.vector.tensor_tensor(mean, me, mo, ALU.add)
            nc.vector.tensor_tensor(m2, stats[:, 0:n, 2], stats[:, 0:n, 5], ALU.add)
            link(dve, nc.vector.tensor_tensor(dif, me, mo, ALU.subtract))
            link(dve, nc.vector.tensor_tensor(sq, dif, dif, ALU.mult))
            link(dve, nc.vector.scalar_tensor_tensor(out=sq, in0=sq, scalar=D / 4.0, in1=m2,
                                                     op0=ALU.mult, op1=ALU.add))
            nc.vector.tensor_scalar(mean, mean, 0.5, None, ALU.mult)
            nc.vector.tensor_scalar(var, sq, 1.0 / D, EPS, ALU.mult, ALU.add).then_inc(s_var, 1)
            lns[0] += 1
            dve.wait_ge(s_rstd, lns[0])
            for t in range(n):
                ins = nc.vector.tensor_scalar(dst[:, t, :], src[:, t, :], mean[:, t:t + 1], rstd[:, t:t + 1],
                                              ALU.subtract, ALU.mult)
            if last is None:
                link(dve, ins)
            else:
                ins.then_inc(last, 1)

        def rstds(pool, k, n):
            pool.wait_ge(s_var, k)
            nc.gpsimd.tensor_tensor(ln_tmp[:, 4, 0:n], ln_tmp[:, 3, 0:n], nhalf[:, 0:n],
                                    ALU.pow).then_inc(s_rstd, 1)

        LATJOBS = [(b, c, h) for b in range(B) for c in range(NC) for h in range(3)]

        def jobs_before(b, i):
            return VJOBS + 5 + b * (JOBS * PAIRS + AWJOBS + VJOBS) + JOBS * i

        def casts_before(b, i):
            return VJOBS + 5 + b * (CASTS * PAIRS + 2 + VJOBS) + CASTS * i

        def bank(idx):
            return shared[(1 + idx) % 2]

        def upper(s):
            return PT[:, s % RING, :].bitcast(BF16).rearrange("p (n two) -> p n two", two=2)[:, :, 1]

        def on_vector(s):
            return s % 3 == 2

        def by_vector(s):
            return (s + 1) // 3

        def turns(eng, emit, batch=None, flush=None):
            for b in range(B):
                if batch:
                    batch(b)
                with eng.Fori(0, PAIRS - 1) as i:
                    emit(b, i, b * PAIRS + i, b)
                emit(b, PAIRS - 1, b * PAIRS + PAIRS - 1, b + 1 if b + 1 < B else None)
                if flush:
                    flush(b, jobs_before(b, PAIRS) if b + 1 < B else jobs_before(b, PAIRS - 1) + AWJOBS,
                          casts_before(b, PAIRS) if b + 1 < B else casts_before(b, PAIRS - 1) + 2)

        ATT0_JOBS = jobs_before(1, PAIRS - 1) + 2 * AWJOBS
        tbank = [ps[:, 6, :], ps[:, 7, :]]
        TJOBS = [(c, b, h) for b in range(B) for h in range(2) for c in range(NC)]

        hidden_banks = [ps[:, 0, :], ps[:, 1, :]]
        acc_banks = [ps[:, 2:4, :].rearrange("p a n -> p (a n)"), ps[:, 4:6, :].rearrange("p a n -> p (a n)")]
        score1 = [ps[0:S, 3, :], ps[0:S, 4, :]]
        pv1 = [ps[:, i, 0:TB * (D1 + 1)].rearrange("p (t d) -> p t d", t=TB) for i in (5, 2)]
        CT_JOB, K_JOB, V_JOB, Q_JOB, NM_JOB, OUT_JOB = 0, 2, 4, 6, 14, 18

        def max1_banks(i):
            a = 3 * (i % 2) if i < TB * NC else 0
            return ps[:, a:a + 2, 0:HC // 2 * SP]

        WA_ORDER = (1, 2, 0, 3)
        QJOBS = [(b, c, h) for b in range(B) for c in range(NC) for h in range(2)]
        NM_AT = (18, 19)
        CONST1 = 11

        def upper1(k):
            return PT1[:, k % RING1, :].bitcast(BF16).rearrange("p (n two) -> p n two", two=2)[:, :, 1]

        gate_banks, up_banks = [ps[:, 0, :], ps[:, 1, :]], [ps[:, 2, :], ps[:, 3, :]]
        down_banks = [ps[:, 4, :], ps[:, 5, :]]

        A_AT, WO_AT = 1, 3
        M1_AT, M1_MAX, M1_T = 1, 9, 10
        QK_AT, M0_AT, M0_MAX, M0_T = 14, 20, 28, 29
        WQK_AT, WO_SPLIT_AT = 4, 14

        UNITS = GR * FC
        UP_AHEAD = 2
        SPLIT_AFTER = {2 + k * (UNITS - 4) // (2 * FC - 1): k for k in range(2 * FC)}

        def experts(eng, emit):
            with eng.Fori(0, E0 // 2 - 1) as i:
                for k in range(2):
                    emit(2 * i + k, k, i, True)
            for k in range(2):
                emit(E0 - 2 + k, k, E0 // 2 - 1, k == 0)

        block = stack.enter_context(nc.Block())

        @block.sync
        def _(sp):
            sp.wait_ge(s_zero, 1)
            sp.dma_start(C[0:S], ctx.rearrange("b s d -> s b d")).then_inc(s_in, 16)
            sp.dma_start(C[S:SP], ctx[:, S - 1:S, :].rearrange("b s d -> s b d")).then_inc(s_in, 16)
            for i, w in enumerate((ln1w, ln1b, ln2w, ln2b)):
                sp.dma_start(lnp[:, i, :], w).then_inc(s_in, 16)
            sp.dma_start(X[:], x.rearrange("b (t p) d -> p (b t) d", p=P)).then_inc(s_in, 16)
            sp.dma_start(wqk_raw[:], wqk0[0]).then_inc(s_wqk_raw, 16)
            sp.dma_start(wv_raw[:], wv0).then_inc(s_wv_raw, 16)
            sp.dma_start(wo_raw[:], wo0[0]).then_inc(s_wo_raw, 16)

            def stack_head(h):
                r = slice(HD * h, HD * h + HD)
                for dst, src in ((QA[h][0:HD], Q["h"][r]), (QA[h][HD:P], Q["h"][r]), (QB[h][0:HD], Q["l"][r])):
                    sp.dma_start(dst.bitcast(F32), src.bitcast(F32)).then_inc(s_stack[h], 16)
                for dst, src in ((KA[h][0:HD, 0:NK], K["h"][r, 0:NK]), (KA[h][HD:P, 0:NK], K["l"][r, 0:NK]),
                                 (KB[h][0:HD, 0:NK], K["h"][r, 0:NK])):
                    sp.dma_start(dst.bitcast(F32), src.bitcast(F32)).then_inc(s_stack[h], 16)

            def max_row(h):
                sp.dma_start(QB[h][HD:HD + 1, :].bitcast(F32).rearrange("o (t p) -> o t p", t=TB), maxT[h][:].bitcast(F32)) \
                    .then_inc(s_row[h], 16)

            sp.wait_ge(s_jobfree, 2 + VJOBS + 5)
            stack_head(0)
            sp.wait_ge(s_maxrow, 1)
            max_row(0)

            def turn(b, i, g, nb):
                sp.wait_ge(s_score, STEPS * g + 1)
                stack_head(1)
                sp.wait_ge(s_wo, 2 * (g + b) + 2)
                sp.dma_start(wo_raw[:], wo0[i] if isinstance(i, int) else wo0[bass.ds(i, 1)].squeeze(0)) \
                    .then_inc(s_wo_raw, 16)
                if nb is not None:
                    nxt = (i + 1) % PAIRS if isinstance(i, int) else i + 1
                    sp.wait_ge(s_wqk, 2 * g + 2)
                    sp.dma_start(wqk_raw[:], wqk0[nxt] if isinstance(nxt, int) else wqk0[bass.ds(nxt, 1)].squeeze(0)) \
                        .then_inc(s_wqk_raw, 16)
                sp.wait_ge(s_maxrow, 2 * g + 2)
                max_row(1)
                if nb is not None:
                    sp.wait_ge(s_jobfree, jobs_before(b, i) + AWJOBS + 5 + 2)
                    stack_head(0)
                    sp.wait_ge(s_maxrow, 2 * g + 3)
                    max_row(0)

            def next_batch(b):
                if b > 0:
                    sp.wait_ge(s_wo, 2 * (PAIRS + 1) * b)
                    sp.dma_start(wo_raw[:], wo0[0]).then_inc(s_wo_raw, 16)

            turns(sp, turn, batch=next_batch)
            sp.wait_ge(s_jobfree, ATT0_JOBS + 2)
            for dst, src in ((wr_raw, wr), (rb, rbias.partition_broadcast(P)), (b2s, b2),
                             (gbs, gb.partition_broadcast(P))):
                sp.dma_start(dst[:], src).then_inc(s_in1, 16)
            for k in range(2):
                sp.dma_start(b1e[:, k], b1[k]).then_inc(s_b1e[k], 16)
            sp.dma_start(w1_raw[:], w1[0]).then_inc(s_w1_raw, 16)
            sp.dma_start(w2_raw[:], w2[0]).then_inc(s_w2_raw, 16)

            def load_expert(e):
                sp.wait_ge(s_w1, 2 * FC * e)
                sp.dma_start(w1_raw[:], w1[e] if isinstance(e, int) else w1[bass.ds(e, 1)].squeeze(0)) \
                    .then_inc(s_w1_raw, 16)
                sp.wait_ge(s_w2, 2 * FC * e)
                sp.dma_start(w2_raw[:], w2[e] if isinstance(e, int) else w2[bass.ds(e, 1)].squeeze(0)) \
                    .then_inc(s_w2_raw, 16)

            load_expert(1)
            with sp.Fori(0, E0 // 2 - 1) as i:
                for k in range(2):
                    e = 2 * i + 2 + k
                    load_expert(e)
                    sp.wait_ge(s_hf, UNITS * (e - 1) + 2)
                    sp.dma_start(b1e[:, k], b1[bass.ds(e, 1)].squeeze(0)).then_inc(s_b1e[k], 16)

            sp.wait_ge(s_accfree, GR * E0 + 2)
            sp.wait_ge(s_zero, 2)
            sp.dma_start(C1[0:S], ctx.rearrange("b s d -> s b d")).then_inc(s_in2, 16)
            sp.dma_start(C1[S:SP], ctx[:, S - 1:S, :].rearrange("b s d -> s b d")).then_inc(s_in2, 16)
            sp.dma_start(wa_raw[:], watt).then_inc(s_in2, 16)
            sp.dma_start(bqk[:], bqk1).then_inc(s_in2, 16)
            sp.dma_start(bvo_raw[:], bvo1).then_inc(s_in2, 16)

            sp.wait_ge(s_xn, 3)
            for dst, src in ((wgu_raw[:], wgu), (wd_raw[:], wd), (cw[:, 0, :], convw), (cb[:], convb)):
                sp.dma_start(dst, src).then_inc(s_in3, 16)
            for g in range(GR):
                sp.wait_ge(s_acc1, 4 * EM * (g + 1))
                sp.dma_start(out[g // 2, HALF * (g % 2):HALF * (g % 2) + HALF].rearrange("(t p) d -> p t d", p=P),
                             X[:, 4 * g:4 * g + 4, :]).then_inc(s_out, 16)
            sp.wait_ge(s_out, 16 * GR)

        @block.gpsimd
        def _(pool):
            nc.gpsimd.memset(C[:], 0.0).then_inc(s_zero, 1)
            nc.gpsimd.memset(nhalf[:], -0.5).then_inc(s_const, 1)
            nc.gpsimd.memset(ident[:], 0.0).then_inc(s_const, 1)
            nc.gpsimd.memset(zeros[:], 0.0).then_inc(s_const, 1)
            nc.gpsimd.memset(V["h"][:, :, :, HD:HD + 1], 1.0).then_inc(s_const, 1)
            nc.gpsimd.memset(V["l"][:, :, :, HD:HD + 1], 0.0).then_inc(s_const, 1)
            pool.wait_ge(s_const, 7)
            nc.gpsimd.affine_select(out=ident[:], in_=ident[:], compare_op=ALU.not_equal, fill=1.0, base=0,
                                    pattern=[[-1, P]], channel_multiplier=1).then_inc(s_const, 1)
            pool.wait_ge(s_bounds, 1)
            nc.gpsimd.partition_all_reduce(bound[:], bounds[:], P, RMAX).then_inc(s_bound, 1)
            rstds(pool, 1, B)
            rstds(pool, 2, NT)
            rstds(pool, 3, NT)

            def split(raw, parts, loaded, n, done):
                pool.wait_ge(loaded, 16 * n + 16)
                nc.gpsimd.tensor_tensor(flat(parts["h"]), flat(raw), zeros[:, 0:1].to_broadcast([P, flat(raw).shape[1]]),
                                        ALU.add).then_inc(done, 1)
                pool.wait_ge(done, 2 * n + 1)
                nc.gpsimd.tensor_tensor(flat(parts["l"]), flat(raw), flat(parts["h"]).bitcast(F32), ALU.subtract) \
                    .then_inc(done, 1)

            split(wqk_raw, wqk, s_wqk_raw, 0, s_wqk)
            split(wo_raw, wo, s_wo_raw, 0, s_wo)

            def latents_lo(k, b, c, h):
                pool.wait_ge(s_lat_f, k + 1)
                pool.wait_ge(s_lat_hi, k + 1)
                n = HALF if h < 2 else SP
                cols = slice(HALF * h, HALF * h + n)
                nc.gpsimd.tensor_tensor(lat["l"][:, b, c, cols], latf[:, 0:n],
                                        lat["h"][:, b, c, cols].bitcast(F32), ALU.subtract).then_inc(s_lat_lo, 1)

            for k, (b, c, h) in enumerate(LATJOBS):
                latents_lo(k, b, c, h)
            pool.wait_ge(s_lat_full, len(LATJOBS))
            split(wv_raw, wv, s_wv_raw, 0, s_wv)

            def turn(b, i, g, nb):
                for s in range(STEPS):
                    if not on_vector(s):
                        m = P if s % KT < TB else S
                        pool.wait_ge(s_exp, STEPS * g + s + 1 + 2)
                        nc.gpsimd.tensor_tensor(PR[0:m, s % RING, :], PT[0:m, s % RING, :], upper(s)[0:m],
                                                ALU.subtract).then_inc(s_rem_pool, 1)
                    if nb is not None and s == WQK_AT:
                        split(wqk_raw, wqk, s_wqk_raw, g + 1, s_wqk)
                    if s == WO_SPLIT_AT:
                        pool.wait_ge(s_job, jobs_before(b, i) + AWJOBS)
                        split(wo_raw, wo, s_wo_raw, g + b + 1, s_wo)

            def next_batch(b):
                if b > 0:
                    pool.wait_ge(s_job, jobs_before(b, 0) - VJOBS)
                    split(wo_raw, wo, s_wo_raw, (PAIRS + 1) * b, s_wo)

            turns(pool, turn, batch=next_batch)

            def split_part(raw, hi, lo, done, n):
                nc.gpsimd.tensor_tensor(hi, raw, zeros[:, 0:1].to_broadcast([P, raw.shape[1]]), ALU.add).then_inc(done, 1)
                pool.wait_ge(done, 2 * n + 1)
                nc.gpsimd.tensor_tensor(lo, raw, hi.bitcast(F32), ALU.subtract).then_inc(done, 1)

            pool.wait_ge(s_jobfree, ATT0_JOBS + 2)
            nc.gpsimd.iota(iota8[:], pattern=[[1, E0]], base=0, channel_multiplier=0,
                           allow_small_or_imprecise_dtypes=True).then_inc(s_const, 1)
            for k in "hl":
                nc.gpsimd.memset(XT[k][:, :, :, 0:PAD].bitcast(F32), 0.0).then_inc(s_const, 1)
            rstds(pool, 4, NT)
            for parts, raw, loaded, done in ((w1s, w1_raw, s_w1_raw, s_w1), (w2s, w2_raw, s_w2_raw, s_w2)):
                pool.wait_ge(loaded, 16)
                for f in range(FC):
                    split_part(raw[:, f], parts["h"][:, 0, f], parts["l"][:, 0, f], done, f)

            def expert(e, k, i, more):
                for u in range(UNITS):
                    n = UNITS * e + u
                    pool.wait_ge(s_hf, n + 1 + 2)
                    nc.gpsimd.tensor_tensor(hs["l"][:, u % 4], hf[:, u % 2], hs["h"][:, u % 4].bitcast(F32),
                                            ALU.subtract).then_inc(s_hlo, 1)
                    if more and u in SPLIT_AFTER:
                        next_chunk(e, 1 - k, SPLIT_AFTER[u])

            def next_chunk(e, place, j):
                parts, raw, loaded, done = ((w1s, w1_raw, s_w1_raw, s_w1), (w2s, w2_raw, s_w2_raw, s_w2))[j // FC]
                f = j % FC
                if j == 0:
                    pool.wait_ge(s_down, UNITS * e + 4)
                if f == 0:
                    pool.wait_ge(loaded, 16 * e + 32)
                split_part(raw[:, f], parts["h"][:, place, f], parts["l"][:, place, f], done, FC * e + FC + f)

            experts(pool, expert)
            pool.wait_ge(s_accfree, GR * E0 + 2)
            nc.gpsimd.memset(C1[:], 0.0).then_inc(s_zero, 1)
            nc.gpsimd.memset(V1["h"][:, :, :, D1:D1 + 1], 1.0).then_inc(s_const, 1)
            nc.gpsimd.memset(V1["l"][:, :, :, D1:D1 + 1], 0.0).then_inc(s_const, 1)
            nc.gpsimd.memset(mask_f[:], 0.0).then_inc(s_const, 1)
            nc.gpsimd.memset(hmask[:], 1.0).then_inc(s_const, 1)
            nc.gpsimd.memset(vb[:], 0.0).then_inc(s_const, 1)
            pool.wait_ge(s_const, CONST1 + 5)
            nc.gpsimd.affine_select(out=mask_f[:, 0, :], in_=mask_f[:, 0, :], compare_op=ALU.is_ge, fill=-1e30, base=0,
                                    pattern=[[-1, P]], channel_multiplier=1).then_inc(s_const, 1)
            nc.gpsimd.affine_select(out=mask_f[:, 1, :], in_=mask_f[:, 1, :], compare_op=ALU.is_ge, fill=-1e30, base=0,
                                    pattern=[[1, P]], channel_multiplier=-1).then_inc(s_const, 1)
            nc.gpsimd.affine_select(out=hmask[:], in_=hmask[:], compare_op=ALU.is_ge, fill=0.0, base=0,
                                    pattern=[[-D1, HC]], channel_multiplier=1).then_inc(s_const, 1)
            pool.wait_ge(s_const, CONST1 + 8)
            nc.gpsimd.affine_select(out=hmask[:], in_=hmask[:], compare_op=ALU.is_ge, fill=0.0, base=D1 - 1,
                                    pattern=[[D1, HC]], channel_multiplier=-1).then_inc(s_const, 1)
            rstds(pool, 5, NT)
            rstds(pool, 6, NT)
            for i, w in enumerate(WA_ORDER):
                pool.wait_ge(s_wah, i + 1)
                nc.gpsimd.tensor_tensor(flat(wa["l"][:, w]), flat(wa_raw[:, w]), flat(wa["h"][:, w]).bitcast(F32),
                                        ALU.subtract).then_inc(s_wa, 1)
            for c in range(NC):
                pool.wait_ge(s_a1e, K_JOB + c + 1)
                for b in range(B):
                    keys = K1["l"][:, c, b * SP:b * SP + SP].bitcast(F32)
                    nc.gpsimd.tensor_tensor(KD["l"][:, b, c], keys.unsqueeze(1).to_broadcast([P, HC, SP]),
                                            hmask[:].unsqueeze(2).to_broadcast([P, HC, SP]), ALU.mult).then_inc(s_kdl, 1)
            pool.wait_ge(s_vb, 1)
            nc.gpsimd.partition_all_reduce(vb[:, 1:2], vb[:, 0:1], P, RMAX).then_inc(s_vbr, 1)
            for k in range(0, K1S, 2):
                pool.wait_ge(s_ex1, k + 1)
                nc.gpsimd.tensor_tensor(PR1[0:S, k % RING1, :], PT1[0:S, k % RING1, :], upper1(k)[0:S],
                                        ALU.subtract).then_inc(s_r1p, 1)

            rstds(pool, 7, NT)
            pool.wait_ge(s_xn, 3)
            pool.wait_ge(s_in3, 16 * 4)
            split_part(wgu_raw[:].rearrange("p e a c n -> p (e a c n)"),
                       wgus["h"][:].rearrange("p e a c n -> p (e a c n)"),
                       wgus["l"][:].rearrange("p e a c n -> p (e a c n)"), s_w3, 0)
            split_part(flat(wd_raw), flat(wds["h"]), flat(wds["l"]), s_w3, 1)
            for n in range(GR * EM):
                pool.wait_ge(s_ghi, n + 1)
                nc.gpsimd.tensor_tensor(gs["l"][:, n % 3], gated[:, n % 2], gs["h"][:, n % 3].bitcast(F32),
                                        ALU.subtract).then_inc(s_glo, 1)

        @block.scalar
        def _(act):
            act.wait_ge(s_in, 16 * 7)
            for k, (b, c, h) in enumerate(LATJOBS):
                act.wait_ge(s_lat_full, k + 1)
                n = HALF if h < 2 else SP
                w = 2 if h < 2 else 0
                nc.scalar.activation(lat["h"][:, b, c, HALF * h:HALF * h + n], shared[k % 2][:, 0:n], ACT.Identity,
                                     bias=lnp[:, w + 1, c:c + 1], scale=lnp[:, w, c:c + 1]).then_inc(s_lat_hi, 1)

            def round_qk(j, job, bk):
                act.wait_ge(s_job, job + 1)
                dst = (Q["h"][:, 0:HALF], Q["h"][:, HALF:T], K["h"][:, 0:HALF], K["h"][:, HALF:T], K["h"][:, T:NK])[j]
                nc.scalar.copy(dst, bk[:, 0:SP] if j == 4 else bk).then_inc(s_cast, 1)

            def values(b, job):
                if b == 0:
                    act.wait_ge(s_vs, 1)
                for j in range(VJOBS):
                    kt, half = divmod(j, 2)
                    m = P if kt < TB else S
                    act.wait_ge(s_job, job + j + 1)
                    if b > 0 and j == 0:
                        act.wait_ge(s_pv, STEPS * PAIRS * b + RING)
                    nc.scalar.activation(V["h"][0:m, kt, PAIRS * half:PAIRS * half + PAIRS, 0:HD],
                                         shared[(job + j) % 2][0:m].rearrange("p (h d) -> p h d", d=HD), ACT.Identity,
                                         scale=vs[0:m, 0:1]).then_inc(s_cast, 1)

            values(0, 0)
            for j in range(5):
                round_qk(j, VJOBS + j, shared[j % 2])

            def att_hi(job, j):
                act.wait_ge(s_job, job + j + 1)
                nc.scalar.copy(ATT["h"][:, HALF * j:HALF * j + HALF], bank(j)).then_inc(s_cast, 1)

            def turn(b, i, g, nb):
                for s in range(STEPS):
                    m = P if s % KT < TB else S
                    act.wait_ge(s_score, STEPS * g + s + 1)
                    act.wait_ge(s_pv, STEPS * g + s + 1)
                    nc.scalar.activation(PT[0:m, s % RING, :], score_banks[s % 2][0:m], ACT.Exp,
                                         scale=HD ** -0.5).then_inc(s_exp, 1)
                    at = s - AHEAD
                    if A_AT <= at < A_AT + 2:
                        att_hi(jobs_before(b, i), at - A_AT)
                    if nb is not None and QK_AT <= at < QK_AT + 5:
                        if at == QK_AT:
                            act.wait_ge(s_stack[1], 96 * g + 96)
                        j = at - QK_AT
                        round_qk(j, jobs_before(b, i) + AWJOBS + j, bank(AWJOBS + j))

            def next_batch(b):
                if b > 0:
                    values(b, jobs_before(b, 0) - VJOBS)

            def flush(b, job, cast):
                for j in range(2):
                    act.wait_ge(s_job, job + j + 1)
                    nc.scalar.copy(ATT["h"][:, HALF * j:HALF * j + HALF], shared[(job + j) % 2]).then_inc(s_cast, 1)

            turns(act, turn, next_batch, flush)

            def transposed_hi(z):
                for k, (c, b, h) in enumerate(TJOBS):
                    act.wait_ge(s_tj, (0, 20, 28)[z] + k + 1)
                    nc.scalar.copy(XT["h"][:, c, b, PAD + HALF * h:PAD + HALF * h + HALF], tbank[k % 2]).then_inc(s_thi, 1)

            transposed_hi(0)
            act.wait_ge(s_rexp_in, 1)
            nc.scalar.activation(rw[:, 1, :], rw[:, 0, :], ACT.Exp).then_inc(s_rexp, 1)
            act.wait_ge(s_in1, 16 * 4)

            def expert(e, k, i, more):
                act.wait_ge(s_b1e[k], 16 * i + 16)
                for u in range(UNITS):
                    n = UNITS * e + u
                    act.wait_ge(s_up, n + 1)
                    act.wait_ge(s_down, n + 1)
                    nc.scalar.activation(hs["h"][:, u % 4], hidden_banks[u % 2], ACT.Relu,
                                         bias=b1e[:, k, u % FC:u % FC + 1]).then_inc(s_hhi, 1)

            experts(act, expert)

            act.wait_ge(s_in2, 16 * 5)
            for w in WA_ORDER:
                nc.scalar.copy(wa["h"][:, w], wa_raw[:, w]).then_inc(s_wah, 1)
            transposed_hi(1)

            def round_job(j, dst, src, bias=None):
                act.wait_ge(s_a1, j + 1)
                ins = nc.scalar.copy(dst, src) if bias is None else \
                    nc.scalar.activation(dst, src, ACT.Identity, bias=bias)
                ins.then_inc(s_a1h, 1)

            for c in range(NC):
                j = CT_JOB + c
                round_job(j, CT["h"][:, c], tbank[j % 2][:, 0:B * SP].rearrange("p (b s) -> p b s", b=B))
            for c in range(NC):
                j = K_JOB + c
                round_job(j, K1["h"][:, c], tbank[j % 2][:, 0:B * SP], bqk[:, 1, c:c + 1])
            for i, (b, c, h) in enumerate(QJOBS):
                j = Q_JOB + i
                round_job(j, Q1["h"][:, c, b, HALF * h:HALF * h + HALF], tbank[j % 2], bqk[:, 0, c:c + 1])
            for k in range(K1S):
                act.wait_ge(s_sc1, k + 1)
                if k >= RING1:
                    act.wait_ge(s_pv1, k - RING1 + 1)
                nc.scalar.activation(PT1[0:S, k % RING1, :], score1[k % 2], ACT.Exp, scale=D1 ** -0.5).then_inc(s_ex1, 1)
            for g in range(GR):
                for c in range(NC):
                    j = OUT_JOB + 4 * g + c
                    round_job(j, A1T["h"][:, c, :], tbank[j % 2])

            transposed_hi(2)
            act.wait_ge(s_route, 2)
            nc.scalar.activation(logits[:], tbank[0][:, 0:NT * E1].rearrange("p (t e) -> p t e", t=NT), ACT.Exp,
                                 scale=-1.0).then_inc(s_rexp, 1)
            for n in range(GR * EM):
                act.wait_ge(s_gu, 2 * n + 2)
                if n >= 2:
                    act.wait_ge(s_gated, n - 1)
                nc.scalar.activation(silu[:, n % 2], gate_banks[n % 2], ACT.Silu).then_inc(s_silu, 1)
                act.wait_ge(s_gated, n + 1)
                if n >= 3:
                    act.wait_ge(s_dn1h, 2 * n - 4)
                nc.scalar.copy(gs["h"][:, n % 3], gated[:, n % 2]).then_inc(s_ghi, 1)

        @block.vector
        def _(dve):
            dve.sem_inc(s_jobfree, 2)
            dve.sem_inc(s_mxfree, 2)
            dve.sem_inc(s_exp, 2)
            dve.sem_inc(s_pv, RING)
            dve.sem_inc(s_norm, 1)
            for h in range(2):
                nc.vector.memset(KB[h][HD:HD + 1, :].bitcast(F32), 1.0).then_inc(s_const, 1)
            dve.wait_ge(s_in, 16 * 7)
            dve.wait_ge(s_const, 8)
            dve.wait_ge(s_wv_raw, 16)
            nc.vector.tensor_reduce(bounds[:, 0:1], lnp[:].rearrange("p a c -> p (a c)"), AX.X, ALU.max,
                                    apply_absolute_value=True)
            nc.vector.tensor_reduce(bounds[:, 1:2], flat(wv_raw), AX.X, ALU.max,
                                    apply_absolute_value=True).then_inc(s_bounds, 1)
            dve.wait_ge(s_bound, 1)
            link(dve, nc.vector.tensor_tensor(vs[:, 2:3], bound[:, 0:1], bound[:, 1:2], ALU.mult))
            link(dve, nc.vector.tensor_scalar(vs[:, 2:3], vs[:, 2:3], D * (D ** 0.5 + 1) * 1.1, 1e-30, ALU.mult, ALU.max))
            link(dve, nc.vector.tensor_scalar(vs[:, 3:4].bitcast(U32), vs[:, 2:3].bitcast(U32), 0x7F800000, None,
                                              ALU.bitwise_and))
            link(dve, nc.vector.reciprocal(vs[:, 0:1], vs[:, 3:4]))
            nc.vector.tensor_scalar(vs[:, 0:1], vs[:, 0:1], 16384.0, None, ALU.mult).then_inc(s_vs, 1)
            nc.vector.tensor_scalar(vs[:, 1:2], vs[:, 3:4], 1.0 / 16384.0, None, ALU.mult)
            normalise(dve, C, C, B, s_lnc)
            normalise(dve, X, Y, NT)
            normalise(dve, Y, Y, NT, s_ln)
            for k, (b, c, h) in enumerate(LATJOBS):
                dve.wait_ge(s_lat_full, k + 1)
                dve.wait_ge(s_lat_hi, k + 1)
                if k >= 1:
                    dve.wait_ge(s_lat_lo, k)
                n = HALF if h < 2 else SP
                w = 2 if h < 2 else 0
                nc.vector.tensor_scalar(latf[:, 0:n], shared[k % 2][:, 0:n], lnp[:, w, c:c + 1],
                                        lnp[:, w + 1, c:c + 1], ALU.mult, ALU.add).then_inc(s_lat_f, 1)

            def rest_qk(j, cast, bk):
                dve.wait_ge(s_cast, cast)
                which, cols = (("q", slice(0, HALF)), ("q", slice(HALF, T)), ("k", slice(0, HALF)),
                               ("k", slice(HALF, T)), ("k", slice(T, NK)))[j]
                part = Q if which == "q" else K
                n = cols.stop - cols.start
                nc.vector.tensor_tensor(part["l"][:, cols], bk[:, 0:n], part["h"][:, cols].bitcast(F32),
                                        ALU.subtract).then_inc(s_jobfree, 1)

            def max_tile(t, n):
                for a in range(2):
                    dve.wait_ge(s_mx, 2 * n + a + 1)
                    r = nc.vector.reduce_max(mxs[:, a, t:t + 1], max_banks[:, a * HALF:a * HALF + HALF], AX.X)
                    if a == 0:
                        r.then_inc(s_mxfree, 1)
                if t % 4 == 3:
                    r = nc.vector.reduce_max(mxs[:, 2, t - 3:t + 1],
                                             small_bank[:, 0:4 * SP].rearrange("p (t s) -> p t s", t=4), AX.X)
                r.then_inc(s_mxfree, 1)

            def max_join(n):
                dve.wait_ge(s_mxfree, 2 * n + 2)
                nc.vector.tensor_reduce(maxs[:], mxs[:].rearrange("p a t -> p t a"), AX.X, ALU.max).then_inc(s_max, 1)

            def max_rows(h, k):
                dve.wait_ge(s_maxT, k + 1)
                nc.vector.tensor_scalar(maxT[h][:], small_bank[0:TB, 0:P], -1.0, None, ALU.mult).then_inc(s_maxrow, 1)

            def values(b, job, cast):
                for j in range(VJOBS):
                    kt, half = divmod(j, 2)
                    m = P if kt < TB else S
                    dve.wait_ge(s_cast, cast + j + 1)
                    heads = slice(PAIRS * half, PAIRS * half + PAIRS)
                    nc.vector.scalar_tensor_tensor(out=V["l"][0:m, kt, heads, 0:HD],
                                                   in0=shared[(job + j) % 2][0:m].rearrange("p (h d) -> p h d", d=HD),
                                                   scalar=vs[0:m, 0:1], in1=V["h"][0:m, kt, heads, 0:HD],
                                                   op0=ALU.mult, op1=ALU.subtract).then_inc(s_jobfree, 1)

            values(0, 0, 0)
            link(dve, nc.vector.memset(AT[:], 0.0))
            for j in range(5):
                rest_qk(j, VJOBS + j + 1, shared[j % 2])
            for t in range(TB):
                max_tile(t, t)
            max_join(TB)
            max_rows(0, 0)

            def unit_done(g, u):
                dve.wait_ge(s_pv, STEPS * g + KT * (u + 1) + RING)
                nc.vector.reciprocal(rsum[:], pv_bank[:, :, HD]).then_inc(s_rec, 1)
                dve.wait_ge(s_rec, 4 * g + u + 1)
                h, half = u // 2, u % 2
                nc.vector.scalar_tensor_tensor(out=AT[:, 4 * half:4 * half + 4, HD * h:HD * h + HD],
                                               in0=pv_bank[:, :, 0:HD], scalar=vs[:, 1:2],
                                               in1=rsum[:].unsqueeze(2).to_broadcast([P, 4, HD]),
                                               op0=ALU.mult, op1=ALU.mult).then_inc(s_norm, 1)

            def att_lo(cast, j, bk):
                dve.wait_ge(s_cast, cast + j + 1)
                nc.vector.tensor_tensor(ATT["l"][:, HALF * j:HALF * j + HALF], bk,
                                        ATT["h"][:, HALF * j:HALF * j + HALF].bitcast(F32), ALU.subtract) \
                    .then_inc(s_jobfree, 1)

            def add_out(b, job, j, bk, more=0):
                dve.wait_ge(s_job, job + 2 + j + 1)
                xt = X[:, TB * b + 2 * j:TB * b + 2 * j + 2, :]
                nc.vector.tensor_tensor(xt, xt, bk.rearrange("p (t d) -> p t d", t=2), ALU.add) \
                    .then_inc(s_jobfree, 1)

            def turn(b, i, g, nb):
                for s in range(STEPS):
                    if s % KT == 0 and s > 0:
                        unit_done(g, s // KT - 1)
                    if on_vector(s + AHEAD - 1) and s + AHEAD - 1 < STEPS:
                        r = s + AHEAD - 1
                        m = P if r % KT < TB else S
                        dve.wait_ge(s_exp, STEPS * g + r + 1 + 2)
                        nc.vector.tensor_tensor(PR[0:m, r % RING, :], PT[0:m, r % RING, :], upper(r)[0:m],
                                                ALU.subtract).then_inc(s_rem_dve, 1)
                    if A_AT < s <= A_AT + 2:
                        att_lo(casts_before(b, i), s - 1 - A_AT, bank(s - 1 - A_AT))
                    if WO_AT < s <= WO_AT + 4:
                        add_out(b, jobs_before(b, i), s - 1 - WO_AT, bank(2 + s - 1 - WO_AT))
                    if M1_AT <= s < M1_AT + TB:
                        max_tile(s - M1_AT, 16 * g + 8 + s - M1_AT)
                    if s == M1_MAX:
                        max_join(16 * g + 16)
                    if s == M1_T:
                        max_rows(1, 2 * g + 1)
                    if nb is not None:
                        if QK_AT < s <= QK_AT + 5:
                            j = s - 1 - QK_AT
                            if j == 0:
                                dve.wait_ge(s_stack[1], 96 * g + 96)
                            rest_qk(j, casts_before(b, i) + 2 + j + 1, bank(AWJOBS + j))
                        if M0_AT <= s < M0_AT + TB:
                            max_tile(s - M0_AT, 16 * g + 16 + s - M0_AT)
                        if s == M0_MAX:
                            max_join(16 * g + 24)
                        if s == M0_T:
                            max_rows(0, 2 * g + 2)
                unit_done(g, 3)
                if nb is not None:
                    dve.sem_inc(s_jobfree, 1)

            def next_batch(b):
                if b > 0:
                    link(dve, nc.vector.memset(AT[:], 0.0))
                    values(b, jobs_before(b, 0) - VJOBS, casts_before(b, 0) - VJOBS)

            def flush(b, job, cast):
                for j in range(2):
                    att_lo(cast, j, shared[(job + j) % 2])
                for j in range(4):
                    add_out(b, job, j, shared[(job + 2 + j) % 2])

            turns(dve, turn, next_batch, flush)
            for se, v in ((s_hf, 2), (s_hlo, 2), (s_down, 4), (s_accfree, 2)):
                dve.sem_inc(se, v)

            def transposed_lo(z):
                for k, (c, b, h) in enumerate(TJOBS):
                    dve.wait_ge(s_thi, XJ * z + k + 1)
                    cols = slice(PAD + HALF * h, PAD + HALF * h + HALF)
                    nc.vector.tensor_tensor(XT["l"][:, c, b, cols], tbank[k % 2], XT["h"][:, c, b, cols].bitcast(F32),
                                            ALU.subtract).then_inc(s_tfree, 1)

            def over_experts(v):
                return v.unsqueeze(2).to_broadcast([P, NT, E0])

            def over_tokens(v):
                return v.unsqueeze(1).to_broadcast([P, NT, E0])

            def top_two(src):
                for t in range(NT):
                    ins = nc.vector.max(top[:, t, :], src[:, t, :])
                link(dve, ins)
                for t in range(NT):
                    ins = nc.vector.max_index(topi[:, t, :], top[:, t, :], src[:, t, :])
                link(dve, ins)
                link(dve, nc.vector.tensor_copy(topf[:], topi[:, :, 0:2]))
                for k in range(2):
                    ins = nc.vector.tensor_tensor(oh[:, k], over_tokens(iota8[:]), over_experts(topf[:, :, k]), ALU.is_equal)
                link(dve, ins)

            dve.wait_ge(s_in1, 16 * 4)
            normalise(dve, X, Y, NT, s_xn)
            nc.vector.tensor_copy(wrs["h"][:], wr_raw[:]).then_inc(s_wr, 1)
            dve.wait_ge(s_wr, 1)
            nc.vector.tensor_tensor(wrs["l"][:], wr_raw[:], wrs["h"][:].bitcast(F32), ALU.subtract).then_inc(s_wr, 1)
            transposed_lo(0)
            dve.wait_ge(s_route, 1)
            dve.wait_ge(s_const, 11)
            router = tbank[0][:, 0:NT * E0].rearrange("p (t e) -> p t e", t=NT)
            link(dve, nc.vector.tensor_tensor(logits[:], router, over_tokens(rb[:, 0, :]), ALU.add))
            top_two(logits)
            nc.vector.tensor_tensor(rw[:, 0, :], top[:, :, 1], top[:, :, 0], ALU.subtract).then_inc(s_rexp_in, 1)
            dve.wait_ge(s_rexp, 1)
            link(dve, nc.vector.tensor_scalar(rw[:, 2, :], rw[:, 1, :], 1.0, None, ALU.add))
            link(dve, nc.vector.reciprocal(rw[:, 2, :], rw[:, 2, :]))
            link(dve, nc.vector.tensor_tensor(rw[:, 3, :], rw[:, 1, :], rw[:, 2, :], ALU.mult))
            for k in range(2):
                ins = nc.vector.tensor_tensor(oh[:, k], oh[:, k], over_experts(rw[:, 2 + k, :]), ALU.mult)
            link(dve, ins)
            nc.vector.tensor_tensor(R[:], oh[:, 0], oh[:, 1], ALU.add).then_inc(s_R, 1)
            for j in range(4):
                dve.wait_ge(s_tj, XJ + j + 1)
                nc.vector.tensor_copy(RT[:, 4 * j:4 * j + 4, :],
                                      tbank[j % 2][0:E0].rearrange("p (t q) -> p t q", t=4)).then_inc(s_RT, 1)
            for j in range(8):
                dve.wait_ge(s_tj, XJ + 4 + j + 1)
                yt = Y[:, 2 * j:2 * j + 2, :]
                ins = nc.vector.tensor_tensor(yt, yt, tbank[j % 2].rearrange("p (t d) -> p t d", t=2), ALU.add)
                ins.then_inc(s_RT, 1)
            dve.wait_ge(s_RT, 12)

            def hidden(e, k, u):
                n = UNITS * e + u
                dve.wait_ge(s_hhi, n + 1)
                dve.wait_ge(s_hlo, n + 1)
                nc.vector.tensor_scalar(hf[:, u % 2], hidden_banks[u % 2], b1e[:, k, u % FC:u % FC + 1], 0.0,
                                        ALU.add, ALU.max).then_inc(s_hf, 1)

            def expert(e, k, i, more):
                for u in range(UNITS):
                    if u + UP_AHEAD < UNITS:
                        hidden(e, k, u + UP_AHEAD)
                    elif more:
                        hidden(e + 1, 1 - k, u + UP_AHEAD - UNITS)
                    if u % FC == FC - 1:
                        add_group(e, u // FC)

            def add_group(e, g):
                dve.wait_ge(s_down, UNITS * e + FC * (g + 1) + 4)
                for t in range(4):
                    yt = Y[:, 4 * g + t, :]
                    ins = nc.vector.scalar_tensor_tensor(out=yt, in0=acc_banks[g % 2][:, t * D:t * D + D],
                                                         scalar=R[:, 4 * g + t, bass.ds(e, 1)], in1=yt,
                                                         op0=ALU.mult, op1=ALU.add)
                ins.then_inc(s_accfree, 1)

            for u in range(UP_AHEAD):
                hidden(0, 0, u)
            experts(dve, expert)
            dve.wait_ge(s_accfree, GR * E0 + 2)
            normalise(dve, Y, Y, NT)
            link(dve, nc.vector.tensor_tensor(Y[:], Y[:], gbs[:, 0:1, :].to_broadcast([P, NT, D]), ALU.mult))
            link(dve, nc.vector.tensor_tensor(Y[:], Y[:], gbs[:, 1:2, :].to_broadcast([P, NT, D]), ALU.add))
            link(dve, nc.vector.tensor_tensor(X[:], X[:], Y[:], ALU.add))

            normalise(dve, X, Y, NT, s_xn)
            transposed_lo(1)
            nc.vector.memset(ones_row[:].bitcast(F32), 1.0).then_inc(s_ones, 1)
            nc.vector.tensor_copy(ident_r[:], ident[:]).then_inc(s_ones, 1)
            nc.vector.tensor_copy(sel[:], ident[0:H1, 0:H1].unsqueeze(2).to_broadcast([H1, H1, SP])).then_inc(s_ones, 1)
            dve.wait_ge(s_const, CONST1 + 9)
            nc.vector.tensor_copy(mask[:], mask_f[:]).then_inc(s_ones, 1)
            nc.vector.tensor_copy(mask4[:], mask_f[:, 0:1, 0:SP].to_broadcast([P, HC // 2, SP])).then_inc(s_ones, 1)
            dve.wait_ge(s_in2, 16 * 5)
            nc.vector.tensor_copy(bvo["h"][:], bvo_raw[:]).then_inc(s_ones, 1)
            dve.wait_ge(s_ones, 6)
            nc.vector.tensor_tensor(bvo["l"][:], bvo_raw[:], bvo["h"][:].bitcast(F32), ALU.subtract).then_inc(s_ones, 1)

            def rest_job(k, dst, src, hi, bias=None):
                dve.wait_ge(s_a1h, k + 1)
                ins = nc.vector.tensor_tensor(dst, src, hi.bitcast(F32), ALU.subtract) if bias is None else \
                    nc.vector.scalar_tensor_tensor(out=dst, in0=src, scalar=bias, in1=hi.bitcast(F32),
                                                   op0=ALU.add, op1=ALU.subtract)
                ins.then_inc(s_a1e, 1)

            for c in range(NC):
                rest_job(c, CT["l"][:, c], tbank[(CT_JOB + c) % 2][:, 0:B * SP].rearrange("p (b s) -> p b s", b=B),
                         CT["h"][:, c])
            for c in range(NC):
                rest_job(2 + c, K1["l"][:, c], tbank[(K_JOB + c) % 2][:, 0:B * SP], K1["h"][:, c], bqk[:, 1, c:c + 1])
            for b in range(B):
                j = V_JOB + b
                dve.wait_ge(s_a1, j + 1)
                nc.vector.tensor_copy(V1f[0:S, b], tbank[j % 2][0:S, 0:D].rearrange("p (h d) -> p h d", h=H1)) \
                    .then_inc(s_a1e, 1)
            dve.wait_ge(s_a1e, V_JOB + B)
            nc.vector.tensor_reduce(vb[0:S, 0:1], V1f[0:S].rearrange("p b h d -> p (b h d)"), AX.X, ALU.max,
                                    apply_absolute_value=True).then_inc(s_vb, 1)
            for b in range(B):
                for c in range(NC):
                    keys = K1["h"][:, c, b * SP:b * SP + SP].bitcast(F32)
                    nc.vector.tensor_tensor(KD["h"][:, b, c], keys.unsqueeze(1).to_broadcast([P, HC, SP]),
                                            hmask[:].unsqueeze(2).to_broadcast([P, HC, SP]), ALU.mult).then_inc(s_kd, 1)
            for i, (b, c, h) in enumerate(QJOBS):
                cols = slice(HALF * h, HALF * h + HALF)
                rest_job(4 + i, Q1["l"][:, c, b, cols], tbank[(Q_JOB + i) % 2], Q1["h"][:, c, b, cols],
                         bqk[:, 0, c:c + 1])

            def max1(i):
                b, t, c = i // (TB * NC), i // NC % TB, i % NC
                dve.wait_ge(s_mx1, i + 1)
                nc.vector.reduce_max(m1[:, b, t, HC * c:HC * c + HC].rearrange("p (a h) -> p a h", a=2),
                                     max1_banks(i).rearrange("p a (h s) -> p a h s", s=SP), AX.X).then_inc(s_m8, 1)

            def max1_rows(b, half):
                j = NM_JOB + 2 * b + half
                dve.wait_ge(s_a1, j + 1)
                nc.vector.tensor_scalar(NM[:, b, HALF * half:HALF * half + HALF], tbank[j % 2][0:H1], -1.0, None,
                                        ALU.mult).then_inc(s_a1e, 1)

            def norm1(n):
                b, h = divmod(n, H1)
                dve.wait_ge(s_pv1, 2 * n + 2)
                nc.vector.reciprocal(rs8[:], pv1[n % 2][:, :, D1]).then_inc(s_rs1, 1)
                dve.wait_ge(s_rs1, n + 1)
                nc.vector.scalar_tensor_tensor(out=Y[:, TB * b:TB * b + TB, D1 * h:D1 * h + D1],
                                               in0=pv1[n % 2][:, :, 0:D1], scalar=vs1[:, 1:2],
                                               in1=rs8[:].unsqueeze(2).to_broadcast([P, TB, D1]),
                                               op0=ALU.mult, op1=ALU.mult).then_inc(s_nm1, 1)

            for i in range(TB * NC):
                max1(i)
            for half in range(2):
                max1_rows(0, half)
            dve.wait_ge(s_vbr, 1)
            link(dve, nc.vector.tensor_scalar(vs1[:, 2:3], vb[:, 1:2], 1e-30, None, ALU.max))
            link(dve, nc.vector.tensor_scalar(vs1[:, 2:3].bitcast(U32), vs1[:, 2:3].bitcast(U32), 0x7F800000, None,
                                              ALU.bitwise_and))
            link(dve, nc.vector.reciprocal(vs1[:, 0:1], vs1[:, 2:3]))
            link(dve, nc.vector.tensor_scalar(vs1[:, 0:1], vs1[:, 0:1], 16384.0, None, ALU.mult))
            nc.vector.tensor_scalar(vs1[:, 1:2], vs1[:, 2:3], 1.0 / 16384.0, None, ALU.mult)
            for b in range(B):
                ins = nc.vector.tensor_scalar(V1["h"][0:S, b, :, 0:D1], V1f[0:S, b], vs1[0:S, 0:1], None, ALU.mult)
            link(dve, ins)
            for b in range(B):
                nc.vector.scalar_tensor_tensor(out=V1["l"][0:S, b, :, 0:D1], in0=V1f[0:S, b], scalar=vs1[0:S, 0:1],
                                               in1=V1["h"][0:S, b, :, 0:D1], op0=ALU.mult, op1=ALU.subtract) \
                    .then_inc(s_v1, 1)
            for k in range(K1S):
                if k % 2 == 0 and k > 0:
                    norm1(k // 2 - 1)
                r = k + 1
                if r % 2 == 1 and r < K1S:
                    dve.wait_ge(s_ex1, r + 1)
                    nc.vector.tensor_tensor(PR1[0:S, r % RING1, :], PT1[0:S, r % RING1, :], upper1(r)[0:S],
                                            ALU.subtract).then_inc(s_r1v, 1)
                if k < TB * NC:
                    max1(TB * NC + k)
                if k in NM_AT:
                    max1_rows(1, k - NM_AT[0])
            norm1(K1S // 2 - 1)
            for g in range(GR):
                for c in range(NC):
                    rest_job(12 + NC * g + c, A1T["l"][:, c, :], tbank[(OUT_JOB + 4 * g + c) % 2], A1T["h"][:, c, :])
                for i in range(2):
                    j = OUT_JOB + 4 * g + 2 + i
                    dve.wait_ge(s_a1, j + 1)
                    xt = X[:, 4 * g + 2 * i:4 * g + 2 * i + 2, :]
                    nc.vector.tensor_tensor(xt, xt, tbank[j % 2].rearrange("p (t d) -> p t d", t=2), ALU.add) \
                        .then_inc(s_a1e, 1)
            dve.wait_ge(s_a1e, OUT_JOB + 4 * GR)

            normalise(dve, X, Y, NT, s_xn)
            transposed_lo(2)
            link(dve, nc.vector.memset(ones_f[:], 1.0))
            dve.wait_ge(s_in3, 16 * 4)
            link(dve, nc.vector.tensor_copy(cwh[:], cw[:, 0, :]))
            link(dve, nc.vector.tensor_tensor(cw[:, 1, :], cw[:, 0, :], cwh[:].bitcast(F32), ALU.subtract))
            for k in range(TAPS * NC):
                for i, u in enumerate("hl"):
                    src = cwh[:, k:k + 1].bitcast(F32) if u == "h" else cw[:, 1, k:k + 1]
                    ins = nc.vector.tensor_scalar(diag[u][:, k, :], ident[:], src, None, ALU.mult)
            ins.then_inc(s_w3d, 1)
            dve.wait_ge(s_rexp, 2)
            link(dve, nc.vector.tensor_scalar(logits[:], logits[:], 1.0, None, ALU.add))
            link(dve, nc.vector.reciprocal(logits[:], logits[:]))
            link(dve, nc.vector.tensor_tensor(R[:], logits[:], over_tokens(rb[:, 1, :]), ALU.add))
            top_two(R)
            link(dve, nc.vector.tensor_tensor(oh[:, 0], oh[:, 0], oh[:, 1], ALU.add))
            link(dve, nc.vector.tensor_tensor(oh[:, 0], oh[:, 0], logits[:], ALU.mult))
            link(dve, nc.vector.reduce_sum(rw[:, 0, :], oh[:, 0], AX.X))
            link(dve, nc.vector.tensor_scalar(rw[:, 0, :], rw[:, 0, :], 1e-9, None, ALU.add))
            link(dve, nc.vector.reciprocal(rw[:, 0, :], rw[:, 0, :]))
            link(dve, nc.vector.tensor_tensor(R[:], oh[:, 0], over_experts(rw[:, 0, :]), ALU.mult))
            link(dve, nc.vector.tensor_tensor(rw[:, 1, :], R[:, :, EM], R[:, :, EM + 2], ALU.add))

            def own_terms(g):
                ys, xs = Y[:, 4 * g:4 * g + 4, :], X[:, 4 * g:4 * g + 4, :]
                link(dve, nc.vector.tensor_scalar(reluY[:], ys, 0.0, None, ALU.max))
                for t in range(4):
                    ins = nc.vector.scalar_tensor_tensor(out=xs[:, t, :], in0=ys[:, t, :], scalar=rw[:, 1, 4 * g + t:4 * g + t + 1],
                                                         in1=xs[:, t, :], op0=ALU.mult, op1=ALU.add)
                link(dve, ins)
                for t in range(4):
                    ins = nc.vector.scalar_tensor_tensor(out=xs[:, t, :], in0=reluY[:, t, :],
                                                         scalar=R[:, 4 * g + t, E1 - 1:E1],
                                                         in1=xs[:, t, :], op0=ALU.mult, op1=ALU.add)
                link(dve, ins)
                for j in range(2):
                    dve.wait_ge(s_conv, 2 * g + j + 1)
                    x2 = xs[:, 2 * j:2 * j + 2, :]
                    ins = nc.vector.tensor_tensor(x2, x2, ps[:, 7, :].rearrange("p (t d) -> p t d", t=2), ALU.add)
                    ins.then_inc(s_convfree, 1)
                dve.wait_ge(s_convfree, 2 * g + 2)

            def gate(n):
                dve.wait_ge(s_silu, n + 1)
                if n >= 2:
                    dve.wait_ge(s_glo, n - 1)
                nc.vector.tensor_tensor(gated[:, n % 2], silu[:, n % 2], up_banks[n % 2], ALU.mult).then_inc(s_gated, 1)

            def add1(n):
                g, e = divmod(n, EM)
                for t in range(4):
                    if t % 2 == 0:
                        dve.wait_ge(s_dn1h, 2 * n + t // 2 + 1)
                    xt = X[:, 4 * g + t, :]
                    ins = nc.vector.scalar_tensor_tensor(out=xt, in0=down_banks[t // 2][:, t % 2 * D:t % 2 * D + D],
                                                         scalar=R[:, 4 * g + t, e:e + 1], in1=xt, op0=ALU.mult, op1=ALU.add)
                    ins.then_inc(s_acc1, 1)
                dve.wait_ge(s_acc1, 4 * n + 4)

            for n in range(GR * EM):
                gate(n)
                if n % EM == 0:
                    own_terms(n // EM)
                if n >= 1:
                    add1(n - 1)
            add1(GR * EM - 1)

        @block.tensor
        def _(pe):
            pe.wait_ge(s_const, 8)
            pe.wait_ge(s_lnc, 1)
            pe.wait_ge(s_ln, 1)
            for k, (b, c, h) in enumerate(LATJOBS):
                if k >= 2:
                    pe.wait_ge(s_lat_f, k - 1)
                if h < 2:
                    for t in range(4):
                        mm = nc.tensor.transpose(shared[k % 2][:, t * P:t * P + P],
                                                 Y[:, b * TB + 4 * h + t, c * P:c * P + P], ident[:])
                else:
                    mm = nc.tensor.transpose(shared[k % 2][:, 0:SP], C[0:SP, b, c * P:c * P + P], ident[0:SP, 0:SP])
                mm.then_inc(s_lat_full, 1)

            def product(o, pairs, **kw):
                n = len(pairs)
                for k, (l, r) in enumerate(pairs):
                    mm = nc.tensor.matmul(o, l, r, start=(k == 0), stop=(k == n - 1), **kw)
                return mm

            def project_qk(j, nb, job, bk):
                pe.wait_ge(s_jobfree, job + 1)
                cols = (slice(0, HALF), slice(HALF, T), slice(0, HALF), slice(HALF, T), slice(T, NK))[j]
                product(bk[:, 0:cols.stop - cols.start],
                        [(wqk[u][:, c, j // 2 if j < 4 else 1, :], lat[v][:, nb, c, cols])
                         for c in range(NC) for u, v in RANDL]).then_inc(s_job, 1)

            def max_part(h, t, a, n):
                pe.wait_ge(s_mxfree, 2 * n + a + 1)
                r = slice(HD * h, HD * h + HD)
                q = Q["h"][r, t * P:t * P + P]
                if a == 1:
                    nc.tensor.matmul(small_bank[:, t % 4 * SP:t % 4 * SP + SP], q, K["h"][r, T:NK],
                                     start=True, stop=True)
                nc.tensor.matmul(max_banks[:, a * HALF:a * HALF + HALF], q, K["h"][r, a * HALF:a * HALF + HALF],
                                 start=True, stop=True).then_inc(s_mx, 1)

            def max_tile(h, t, n):
                for a in range(2):
                    max_part(h, t, a, n)

            def max_turn(k):
                pe.wait_ge(s_max, k + 1)
                nc.tensor.transpose(small_bank[0:TB, 0:P], maxs[:], ident[:]).then_inc(s_maxT, 1)

            pe.wait_ge(s_lat_lo, len(LATJOBS))
            pe.wait_ge(s_wqk, 2)
            def values(b, job):
                for j in range(VJOBS):
                    kt, half = divmod(j, 2)
                    m = P if kt < TB else S
                    pe.wait_ge(s_jobfree, job + j + 1)
                    product(shared[(job + j) % 2][0:m],
                            [(lat[u][:, b, c, kt * P:kt * P + m], wv[v][:, c, HALF * half:HALF * half + HALF])
                             for c in range(NC) for u, v in RANDL]).then_inc(s_job, 1)

            pe.wait_ge(s_wv, 2)
            values(0, 0)
            for j in range(5):
                project_qk(j, 0, VJOBS + j, shared[j % 2])
            pe.wait_ge(s_jobfree, VJOBS + 5 + 2)
            for t in range(TB):
                max_tile(0, t, t)
            max_turn(0)

            def scores(g, s):
                h, half, kt = s // (2 * KT), s // KT % 2, s % KT
                m = P if kt < TB else S
                pe.wait_ge(s_exp, STEPS * g + s + 1)
                if s % (2 * KT) == 0:
                    pe.wait_ge(s_stack[h], 96 * g + 96)
                    pe.wait_ge(s_row[h], 16 * g + 16)
                o = score_banks[s % 2][0:m]
                q, k = slice(HALF * half, HALF * half + HALF), slice(kt * P, kt * P + m)
                nc.tensor.matmul(o, KA[h][:, k], QA[h][:, q], start=True, stop=False)
                nc.tensor.matmul(o, KB[h][0:HD + 1, k], QB[h][0:HD + 1, q], start=False, stop=True) \
                    .then_inc(s_score, 1)

            def attend(g, pair, s):
                h, kt = s // (2 * KT), s % KT
                m = P if kt < TB else S
                if on_vector(s):
                    pe.wait_ge(s_rem_dve, STEPS // 3 * g + by_vector(s))
                else:
                    pe.wait_ge(s_rem_pool, 2 * STEPS // 3 * g + s + 1 - by_vector(s))
                if kt == 0:
                    pe.wait_ge(s_norm, 4 * g + s // KT + 1)
                head = 2 * pair + h
                vh, vl = ((V[k][0:m, kt, head, :] if isinstance(head, int) else
                           V[k][0:m, kt, bass.ds(head, 1), :].squeeze(1)) for k in "hl")
                for q in range(4):
                    c = slice(q * P, q * P + P)
                    for k, (p, v) in enumerate(((upper(s)[0:m, c], vh), (upper(s)[0:m, c], vl),
                                                (PR[0:m, s % RING, c], vh), (PR[0:m, s % RING, c], vl))):
                        mm = nc.tensor.matmul(pv_bank[:, q, :], p, v, start=(kt == 0 and q == 0 and k == 0),
                                              stop=(kt == KT - 1 and k == 3), skip_group_check=True)
                mm.then_inc(s_pv, 1)

            def att_turn(job, j, bk):
                pe.wait_ge(s_jobfree, job + j + 1)
                for t in range(4):
                    mm = nc.tensor.transpose(bk[:, t * P:t * P + P], AT[:, 4 * j + t, :], ident[:])
                mm.then_inc(s_job, 1)

            def project_out(job, j, bk):
                if j % 2 == 0:
                    pe.wait_ge(s_jobfree, job + j // 2 + 1 + 2)
                pe.wait_ge(s_jobfree, job + 2 + j + 1)
                for t in range(2):
                    q = slice((2 * j + t) * P, (2 * j + t + 1) * P)
                    mm = product(bk[:, t * D:t * D + D], [(ATT[u][:, q], wo[v][:]) for u, v in RANDL])
                mm.then_inc(s_job, 1)

            def turn(b, i, g, nb):
                job = jobs_before(b, i)
                last = isinstance(i, int)
                for s in range(STEPS):
                    if s + AHEAD < STEPS:
                        scores(g, s + AHEAD)
                    elif not last:
                        scores(g + 1, s + AHEAD - STEPS)
                    if M1_AT <= s < M1_AT + TB:
                        if s == M1_AT:
                            pe.wait_ge(s_maxrow, 2 * g + 1)
                        max_part(1, s - M1_AT, 0, 16 * g + 8 + s - M1_AT)
                    if nb is not None and M0_AT <= s < M0_AT + TB:
                        if s == M0_AT:
                            pe.wait_ge(s_jobfree, job + AWJOBS + 5 + 2)
                            pe.wait_ge(s_maxrow, 2 * g + 2)
                        max_part(0, s - M0_AT, 0, 16 * g + 16 + s - M0_AT)
                    if A_AT <= s < A_AT + 2:
                        if s == A_AT:
                            pe.wait_ge(s_norm, 4 * g + 1)
                        att_turn(job, s - A_AT, bank(s - A_AT))
                    attend(g, i, s)
                    if WO_AT <= s < WO_AT + 4:
                        if s == WO_AT:
                            pe.wait_ge(s_wo, 2 * (g + b) + 2)
                        project_out(job, s - WO_AT, bank(2 + s - WO_AT))
                    if M1_AT <= s < M1_AT + TB:
                        max_part(1, s - M1_AT, 1, 16 * g + 8 + s - M1_AT)
                    if s == M1_T:
                        max_turn(2 * g + 1)
                    if nb is not None:
                        if QK_AT <= s < QK_AT + 5:
                            if s == QK_AT:
                                pe.wait_ge(s_wqk, 2 * g + 4)
                            j = AWJOBS + s - QK_AT
                            project_qk(s - QK_AT, nb, job + j, bank(j))
                        if M0_AT <= s < M0_AT + TB:
                            max_part(0, s - M0_AT, 1, 16 * g + 16 + s - M0_AT)
                        if s == M0_T:
                            max_turn(2 * g + 2)
                if nb is not None:
                    pe.sem_inc(s_job, 1)

            def next_batch(b):
                if b > 0:
                    values(b, jobs_before(b, 0) - VJOBS)
                for s in range(AHEAD):
                    scores(b * PAIRS, s)

            def flush(b, job, cast):
                pe.wait_ge(s_norm, 4 * PAIRS * (b + 1) + 1)
                for j in range(2):
                    att_turn(job, j, shared[(job + j) % 2])
                pe.wait_ge(s_wo, 2 * (PAIRS + 1) * (b + 1))
                for j in range(4):
                    project_out(job, j, shared[(job + 2 + j) % 2])

            turns(pe, turn, next_batch, flush)

            def transposes(z):
                pe.wait_ge(s_xn, z + 1)
                for k, (c, b, h) in enumerate(TJOBS):
                    if z == 0 and k < 2:
                        pe.wait_ge(s_jobfree, ATT0_JOBS + 2)
                    if k >= 2:
                        pe.wait_ge(s_tfree, 8 * z + k - 1)
                    for t in range(4):
                        mm = nc.tensor.transpose(tbank[k % 2][:, t * P:t * P + P],
                                                 Y[:, b * TB + 4 * h + t, c * P:c * P + P], ident[:])
                    mm.then_inc(s_tj, 1)

            def tokens(u, c, t):
                return XT[u][:, c, t // TB, PAD + t % TB * P:PAD + t % TB * P + P]

            def group(u, c, g):
                return XT[u][:, c, g // 2, PAD + HALF * (g % 2):PAD + HALF * (g % 2) + HALF]

            def route(z, layer):
                pe.wait_ge(s_tfree, 8 * z + 8)
                pe.wait_ge(s_wr, 2)
                for t in range(NT):
                    mm = product(tbank[0][:, t * E0:t * E0 + E0],
                                 [(tokens(u, c, t), wrs[v][:, layer, c, :]) for c in range(NC) for u, v in RANDL])
                mm.then_inc(s_route, 1)

            transposes(0)
            route(0, 0)
            pe.wait_ge(s_R, 1)
            for j in range(4):
                if j >= 2:
                    pe.wait_ge(s_RT, j - 1)
                for t in range(4):
                    mm = nc.tensor.transpose(tbank[j % 2][0:E0, t * P:t * P + P], R[:, 4 * j + t, :], ident[:])
                mm.then_inc(s_tj, 1)
            for j in range(8):
                pe.wait_ge(s_RT, 4 if j < 1 else 4 + j - 1)
                for t in range(2):
                    mm = nc.tensor.matmul(tbank[j % 2][:, t * D:t * D + D], RT[:, 2 * j + t, :], b2s[:],
                                          start=True, stop=True)
                mm.then_inc(s_tj, 1)

            def up(e, k, u):
                g, f = divmod(u, FC)
                pe.wait_ge(s_hf, UNITS * e + u + 1)
                if g == 0:
                    pe.wait_ge(s_w1, 2 * FC * e + 2 * f + 2)
                product(hidden_banks[u % 2], [(w1s[a][:, k, f, c * P:c * P + P], group(b, c, g))
                                              for c in range(NC) for a, b in RANDL]).then_inc(s_up, 1)

            def down(e, k, u):
                g, f = divmod(u, FC)
                if f == 0:
                    pe.wait_ge(s_accfree, GR * e + g + 1)
                if g == 0:
                    pe.wait_ge(s_w2, 2 * FC * e + 2 * f + 2)
                pe.wait_ge(s_hlo, UNITS * e + u + 1 + 2)
                for t in range(4):
                    o = acc_banks[g % 2][:, t * D:t * D + D]
                    for j, (a, b) in enumerate(RANDL):
                        mm = nc.tensor.matmul(o, hs[a][:, u % 4, t * P:t * P + P], w2s[b][:, k, f, :],
                                              start=(f == 0 and j == 0 and t % 2 == 0), stop=(f == FC - 1 and j == 2),
                                              skip_group_check=True)
                mm.then_inc(s_down, 1)

            def expert(e, k, i, more):
                for u in range(UNITS):
                    if u + UP_AHEAD < UNITS:
                        up(e, k, u + UP_AHEAD)
                    elif more:
                        up(e + 1, 1 - k, u + UP_AHEAD - UNITS)
                    down(e, k, u)

            for u in range(UP_AHEAD):
                up(0, 0, u)
            experts(pe, expert)

            transposes(1)
            pe.wait_ge(s_tfree, 16)
            pe.wait_ge(s_ones, 7)
            pe.wait_ge(s_in2, 16 * 5)

            def job(j):
                if j >= 2:
                    pe.wait_ge(s_a1e, j - 1)
                return tbank[j % 2]

            for c in range(NC):
                bk = job(CT_JOB + c)
                for b in range(B):
                    mm = nc.tensor.transpose(bk[:, b * SP:b * SP + SP], C1[0:SP, b, c * P:c * P + P], ident[0:SP, 0:SP])
                mm.then_inc(s_a1, 1)
            pe.wait_ge(s_a1e, K_JOB)
            pe.wait_ge(s_wa, 1)
            for ic in range(NC):
                product(job(K_JOB + ic)[:, 0:B * SP],
                        [(wa[u][:, 1, c, ic * P:ic * P + P], CT[v][:, c].rearrange("p b s -> p (b s)"))
                         for c in range(NC) for u, v in RANDL]).then_inc(s_a1, 1)
            pe.wait_ge(s_wa, 2)
            for b in range(B):
                product(job(V_JOB + b)[0:S, 0:D],
                        [(CT[u][:, c, b, 0:S], wa[v][:, 2, c, :]) for c in range(NC) for u, v in RANDL]
                        + [(ones_row[:, 0:S], bvo[u][:, 0, :]) for u in "hl"]).then_inc(s_a1, 1)
            pe.wait_ge(s_wa, 3)
            for i, (b, ic, h) in enumerate(QJOBS):
                product(job(Q_JOB + i), [(wa[u][:, 0, c, ic * P:ic * P + P], group(v, c, 2 * b + h))
                                         for c in range(NC) for u, v in RANDL]).then_inc(s_a1, 1)

            def max1(i):
                b, t, c = i // (TB * NC), i // NC % TB, i % NC
                if i < TB * NC and i >= 2:
                    pe.wait_ge(s_m8, i - 1)
                elif i >= TB * NC:
                    pe.wait_ge(s_m8, i)
                q = Q1["h"][:, c, b, t * P:t * P + P]
                for a in range(2):
                    o = max1_banks(i)[:, a]
                    keys = KD["h"][:, b, c, HC // 2 * a:HC // 2 * a + HC // 2].rearrange("p h s -> p (h s)")
                    mm = nc.tensor.matmul(o, q, keys, start=True, stop=(t > 0))
                    if t == 0:
                        mm = nc.tensor.matmul(o, ident_r[:], mask4[:].rearrange("p h s -> p (h s)"), start=False, stop=True)
                mm.then_inc(s_mx1, 1)

            def max1_rows(b, half):
                bk = job(NM_JOB + 2 * b + half)
                for t in range(4):
                    mm = nc.tensor.transpose(bk[0:H1, t * P:t * P + P], m1[:, b, 4 * half + t, :], ident[:])
                mm.then_inc(s_a1, 1)

            def scores1(k):
                n, a = divmod(k, 2)
                b, h = divmod(n, H1)
                c = h // HC
                if k >= 2:
                    pe.wait_ge(s_ex1, k - 1)
                o = score1[k % 2]
                q = slice(HALF * a, HALF * a + HALF)
                ops = [(KD[u][:, b, c, h % HC, 0:S], Q1[v][:, c, b, q]) for u, v in RANDL]
                ops.append((sel[:, h, 0:S], NM[:, b, q]))
                for i, (l, r) in enumerate(ops):
                    mm = nc.tensor.matmul(o, l, r, start=(i == 0), stop=(i == 3 and a == 1))
                if a == 0:
                    mm = nc.tensor.matmul(o[:, 0:P], ident_r[0:S, 0:S], mask[0:S, 1, :], start=False, stop=True)
                mm.then_inc(s_sc1, 1)

            def attend1(k):
                n, a = divmod(k, 2)
                b, h = divmod(n, H1)
                if a == 0 and n >= 2:
                    pe.wait_ge(s_nm1, n - 1)
                if k % 2 == 0:
                    pe.wait_ge(s_r1p, k // 2 + 1)
                else:
                    pe.wait_ge(s_r1v, k // 2 + 1)
                for t in range(4):
                    c = slice(t * P, t * P + P)
                    mm = product(pv1[n % 2][:, 4 * a + t, :],
                                 [(p[0:S, c], V1[v][0:S, b, h, :]) for p in (upper1(k), PR1[:, k % RING1, :]) for v in "hl"])
                mm.then_inc(s_pv1, 1)

            pe.wait_ge(s_a1e, Q_JOB + 4)
            pe.wait_ge(s_kd, B * NC)
            for i in range(TB * NC):
                max1(i)
            pe.wait_ge(s_m8, TB * NC)
            for half in range(2):
                max1_rows(0, half)
            pe.wait_ge(s_a1e, NM_JOB + 2)
            pe.wait_ge(s_kdl, B * NC)
            for k in range(AHEAD):
                scores1(k)
            pe.wait_ge(s_v1, B)
            for k in range(K1S):
                if k + AHEAD == K1S // 2:
                    pe.wait_ge(s_a1e, NM_JOB + 4)
                if k + AHEAD < K1S:
                    scores1(k + AHEAD)
                if k < TB * NC:
                    max1(TB * NC + k)
                attend1(k)
                if k in NM_AT:
                    pe.wait_ge(s_m8, 2 * TB * NC)
                    max1_rows(1, k - NM_AT[0])
            pe.wait_ge(s_nm1, B * H1)
            pe.wait_ge(s_wa, 4)
            for g in range(GR):
                for c in range(NC):
                    bk = job(OUT_JOB + 4 * g + c)
                    for t in range(4):
                        mm = nc.tensor.transpose(bk[:, t * P:t * P + P], Y[:, 4 * g + t, c * P:c * P + P], ident[:])
                    mm.then_inc(s_a1, 1)
                pe.wait_ge(s_a1e, OUT_JOB + 4 * g + 2)
                for j in range(2):
                    bk = job(OUT_JOB + 4 * g + 2 + j)
                    for t in range(2):
                        q = slice((2 * j + t) * P, (2 * j + t) * P + P)
                        mm = product(bk[:, t * D:t * D + D],
                                     [(A1T[u][:, c, q], wa[v][:, 3, c, :]) for c in range(NC) for u, v in RANDL]
                                     + [(ones_row[:], bvo[u][:, 1, :]) for u in "hl"])
                    mm.then_inc(s_a1, 1)

            transposes(2)
            route(2, 1)

            def gate_up(n):
                g, e = divmod(n, EM)
                if n >= 2:
                    pe.wait_ge(s_gated, n - 1)
                for a, bk in enumerate((gate_banks[n % 2], up_banks[n % 2])):
                    product(bk, [(wgus[u][:, e, a, c, :], group(v, c, g))
                                 for c in range(NC) for u, v in RANDL]).then_inc(s_gu, 1)

            def down1(n):
                g, e = divmod(n, EM)
                pe.wait_ge(s_glo, n + 1)
                for t in range(4):
                    if n >= 1 and t % 2 == 0:
                        pe.wait_ge(s_acc1, 4 * (n - 1) + t + 2)
                    mm = product(down_banks[t // 2][:, t % 2 * D:t % 2 * D + D],
                                 [(gs[u][:, n % 3, t * P:t * P + P], wds[v][:, e, :]) for u, v in RANDL])
                    if t % 2 == 1:
                        mm.then_inc(s_dn1h, 1)
                return mm

            def conv(k):
                if k >= 1:
                    pe.wait_ge(s_convfree, k)
                for t in (2 * k, 2 * k + 1):
                    first = t % TB * P
                    for c in range(NC):
                        o = ps[:, 7, t % 2 * D + c * P:t % 2 * D + c * P + P]
                        ops = [(XT[u][:, c, t // TB, PAD - (TAPS - 1) + j + first:PAD - (TAPS - 1) + j + first + P],
                                diag[v][:, j * NC + c, :]) for j in range(TAPS) for u, v in RANDL]
                        ops.append((ones_f[:], cb[:, c * P:c * P + P]))
                        mm = product(o, ops)
                mm.then_inc(s_conv, 1)

            pe.wait_ge(s_w3, 4)
            for n in range(GR * EM):
                gate_up(n)
                if n % EM == 0:
                    if n == 0:
                        pe.wait_ge(s_w3d, 1)
                    conv(n // 2)
                if n % EM == 1:
                    conv(n // 2 + 1)
                if n >= 1:
                    down1(n - 1)
            down1(GR * EM - 1)


def kernel(**inputs):
    import numpy as np
    import concourse.bacc as bacc
    from concourse.bass_utils import run_bass_kernel_spmd

    a = {k: np.asarray(v) for k, v in inputs.items()}

    def col(v):
        return np.ascontiguousarray(v.reshape(-1, P).T)

    def pairs(w):
        return w.reshape(NC, P, PAIRS, P).transpose(2, 1, 0, 3)

    def chunks(w):
        return w.reshape(NC, P, -1).transpose(1, 0, 2)

    wkv = a["L0_xattn_Wkv"]
    arrays = {
        "x": a["x"], "ctx": a["ctx_1024"],
        "ln1w": col(a["L0_xattn_ln1_w"]), "ln1b": col(a["L0_xattn_ln1_b"]),
        "ln2w": col(a["L0_xattn_ln2_w"]), "ln2b": col(a["L0_xattn_ln2_b"]),
        "wqk0": np.stack([pairs(a["L0_xattn_Wq"]), pairs(wkv[:, :1024])], axis=3),
        "wv0": chunks(wkv[:, 1024:]),
        "wo0": a["L0_xattn_Wo"].reshape(PAIRS, P, D),
        "wr": np.stack([chunks(a["L0_ffn_Wr"].T), chunks(a["L1_ffn_Wr"])], axis=1),
        "rbias": np.stack([a["L0_ffn_br"], a["L1_ffn_router_bias"]]),
        "w1": a["L0_ffn_W1"].reshape(E0, FC, P, NC, P).transpose(0, 4, 1, 3, 2).reshape(E0, P, FC, NC * P),
        "b1": a["L0_ffn_b1"].reshape(E0, FC, P).transpose(0, 2, 1),
        "w2": a["L0_ffn_W2"].reshape(E0, D, FC, P).transpose(0, 3, 2, 1),
        "b2": a["L0_ffn_b2"],
        "gb": np.stack([a["L0_ffn_gamma"], a["L0_ffn_beta"]]),
        "watt": np.stack([chunks(a["L1_xattn_W" + k].T) for k in "qkvo"], axis=1),
        "bqk1": np.stack([col(a["L1_xattn_b" + k]) for k in "qk"], axis=1),
        "bvo1": np.stack([a["L1_xattn_b" + k] for k in "vo"])[None],
        "wgu": np.stack([a["L1_ffn_Wg"], a["L1_ffn_Wu"]]).reshape(2, EM, NC, P, P).transpose(3, 1, 0, 2, 4),
        "wd": a["L1_ffn_Wd"].transpose(1, 0, 2),
        "convw": a["L1_ffn_conv_w"].reshape(TAPS, NC, P).transpose(2, 0, 1).reshape(P, TAPS * NC),
        "convb": a["L1_ffn_conv_b"].reshape(1, D),
    }
    arrays = {k: np.ascontiguousarray(v) for k, v in arrays.items()}
    nc = bacc.Bacc("TRN2", target_bir_lowering=False, num_devices=1)
    args = [nc.dram_tensor(k, v.shape, mybir.dt.from_np(v.dtype), kind="ExternalInput").ap() for k, v in arrays.items()]
    out = nc.dram_tensor("out", (B, T, D), F32, kind="ExternalOutput").ap()
    program(nc, *args, out)
    r = run_bass_kernel_spmd(nc, [arrays], core_ids=[0])
    return r.results[0]["out"]
```

```python
from contextlib import ExitStack

import concourse.bass as bass
from concourse import mybir

P = 128
ALU = mybir.AluOpType
ACT = mybir.ActivationFunctionType
AX = mybir.AxisListType
F32 = mybir.dt.float32
F32R = mybir.dt.float32r
U32 = mybir.dt.uint32
BF16 = mybir.dt.bfloat16
F16 = mybir.dt.float16
RMAX = bass.bass_isa.ReduceOp.max

B, T, D = 2, 1024, 256
S = 77
SP = S + 1
NC = D // P
NT = B * T // P
TB = T // P
HD = 64
PAIRS = 1024 // P
KT = TB + 1
NK = T + SP
NKP = NK + 2
HALF = 512
EPS = 1e-5
STEPS = 4 * KT
RING = 6
AHEAD = 3
JOBS = 12
AWJOBS = 6
VJOBS = 2 * KT
CASTS = 7
WQK0_AT = 5
BOUND_AT = 9
QK0_AT = 9
MAX0_T = 2 * TB
E0, F0 = 8, 1024
FC = F0 // P
GR = B * T // HALF
E1, EM = 8, 4
TAPS = 4
PAD = 4
H1, D1 = 16, 16
HC = P // D1
K1S = 2 * H1 * B
RING1 = 4
XJ = 2 * GR
RANDL = (("h", "h"), ("h", "l"), ("l", "h"))


def program(nc, x, ctx, ln1w, ln1b, ln2w, ln2b, wqk0, wv0, wo0, wr, rbias, w1, b1, w2, b2, gb,
            watt, bqk1, bvo1, wgu, wd, convw, convb, out):
    stack = ExitStack()
    with stack:
        def sb(name, shape, dt=F32):
            return stack.enter_context(nc.sbuf_tensor(name, shape, dt))

        def sem(name):
            return stack.enter_context(nc.semaphore(name))

        ps = stack.enter_context(nc.psum_tensor("ps", [P, 8, HALF], F32))
        score_banks = [ps[:, 0, :], ps[:, 1, :]]
        max_banks = ps[:, 2:4, :].rearrange("p a n -> p (a n)")
        small_bank = ps[:, 4, :]
        shared = [ps[:, 5, :], ps[:, 6, :]]
        pv_bank = ps[:, 7, 0:4 * (HD + 1)].rearrange("p (q d) -> p q d", q=4)

        X = sb("X", [P, NT, D])
        with ExitStack() as early:
            Y = early.enter_context(nc.sbuf_tensor("Y", [P, NT, D], F32))
        wv = {k: sb("wv_" + k, [P, NC, KT * P - P], F32R) for k in "hl"}
        ident = sb("ident", [P, P])
        stats = sb("stats", [P, NT, 6])
        ln_tmp = sb("ln_tmp", [P, 6, NT])
        nhalf = sb("nhalf", [P, NT])
        zeros = sb("zeros", [P, 1])
        st0 = ExitStack()

        def sb0(name, shape, dt=F32):
            return st0.enter_context(nc.sbuf_tensor(name, shape, dt))

        C = sb0("C", [P, B, D])
        lnp = sb0("lnp", [P, 4, NC])
        lat = {k: sb0("lat_" + k, [P, B, NC, NKP], F32R) for k in "hl"}
        latf = sb0("latf", [P, 2, HALF])
        wqk_raw = sb0("wqk_raw", [P, NC, 2, P])
        wo_raw = sb0("wo_raw", [P, D])
        wqk = {k: sb0("wqk_" + k, [P, NC, 2, P], F32R) for k in "hl"}
        wo = {k: sb0("wo_" + k, [P, D], F32R) for k in "hl"}
        Q = {k: sb0("Q_" + k, [P, T], F32R) for k in "hl"}
        K = {k: sb0("K_" + k, [P, NKP], F32R) for k in "hl"}
        QA = [sb0(f"QA{h}", [P, T], F32R) for h in range(2)]
        QB = [sb0(f"QB{h}", [P, T], F32R) for h in range(2)]
        KA = [sb0(f"KA{h}", [P, NKP], F32R) for h in range(2)]
        KB = [sb0(f"KB{h}", [P, NKP], F32R) for h in range(2)]
        V = {k: sb0("V_" + k, [P, KT, 2 * PAIRS, HD + 1], F16) for k in "hl"}
        PT = sb0("PT", [P, RING, HALF])
        PR = sb0("PR", [P, RING, HALF], F16)
        AT = sb0("AT", [P, TB, P])
        with ExitStack() as early:
            wv_raw = early.enter_context(nc.sbuf_tensor("wv_raw", [P, NC, KT * P - P], F32))
        ATT = {k: sb0("ATT_" + k, [P, T], F32R) for k in "hl"}
        bounds = sb0("bounds", [P, 2])
        bound = sb0("bound", [P, 2])
        vs = sb0("vs", [P, 4])
        PVS = sb0("PVS", [P, 2, 4, HD + 1])
        rsum = sb0("rsum", [P, 4])
        mxs = sb0("mxs", [P, 3, TB])
        maxs = sb0("maxs", [P, TB])
        maxT = [sb0(f"maxT{h}", [TB, P], F32R) for h in range(2)]
        st0.close()

        XT = {k: sb("XT_" + k, [P, NC, B, PAD + T], F32R) for k in "hl"}
        wr_raw = sb("wr_raw", [P, 2, NC, E0])
        wrs = {k: sb("wr_" + k, [P, 2, NC, E0], F32R) for k in "hl"}
        rb = sb("rb", [P, 2, E0])
        iota8 = sb("iota8", [P, E0])
        logits = sb("logits", [P, NT, E0])
        top = sb("top", [P, NT, 8])
        topi = sb("topi", [P, NT, 8], U32)
        topf = sb("topf", [P, NT, 2])
        rw = sb("rw", [P, 4, NT])
        oh = sb("oh", [P, 2, NT, E0])
        R = sb("R", [P, NT, E0])
        gbs = sb("gbs", [P, 2, D])
        C1 = sb("C1", [P, B, D])
        CT = {k: sb("CT_" + k, [P, NC, B, SP], F32R) for k in "hl"}
        with ExitStack() as early:
            LT0 = early.enter_context(nc.sbuf_tensor("LT0", [E0, GR, HALF], F32))
        with ExitStack() as early:
            RT = early.enter_context(nc.sbuf_tensor("RT", [E0, NT, P], F32))
        wa = {k: sb("wa_" + k, [P, 4, NC, D], F32R) for k in "lh"}
        bqk = sb("bqk", [P, 2, NC])
        bvo_raw = sb("bvo_raw", [1, 2, D])
        bvo = {k: sb("bvo_" + k, [1, 2, D], F32R) for k in "hl"}
        ones_row = sb("ones_row", [1, P], F32R)
        ident_r = sb("ident_r", [P, P], F32R)
        K1 = {k: sb("K1_" + k, [P, NC, B * SP], F32R) for k in "hl"}
        V1f = sb("V1f", [P, B, H1, D1])
        st1 = ExitStack()

        def sb1(name, shape, dt=F32):
            return st1.enter_context(nc.sbuf_tensor(name, shape, dt))

        b2s = sb1("b2s", [E0, D])
        b1e = sb1("b1e", [P, 2, FC])
        w1_raw = sb1("w1_raw", [P, FC, NC * P])
        wa_raw = w1_raw[:].rearrange("p (w c) d -> p w c d", w=4)
        w2_raw = sb1("w2_raw", [P, FC, D])
        w1s = {k: sb1("w1_" + k, [P, 2, FC, NC * P], F32R) for k in "hl"}
        w2s = {k: sb1("w2_" + k, [P, 2, FC, D], F32R) for k in "hl"}
        hf = sb1("hf", [P, 2, HALF])
        hs = {k: sb1("h_" + k, [P, 4, HALF], F32R) for k in "hl"}
        st1.close()
        st2 = ExitStack()

        def sb2(name, shape, dt=F32):
            return st2.enter_context(nc.sbuf_tensor(name, shape, dt))

        mask_f = sb2("mask_f", [P, 2, P])
        mask = sb2("mask", [P, 2, P], F32R)
        mask4 = sb2("mask4", [P, HC // 2, SP], F32R)
        hmask = sb2("hmask", [P, HC])
        sel = sb2("sel", [H1, H1, SP], F32R)
        KD = {k: sb2("KD_" + k, [P, B, NC, HC, SP], F32R) for k in "hl"}
        V1 = {k: sb2("V1_" + k, [P, B, H1, D1 + 1], F16) for k in "hl"}
        vb = sb2("vb", [P, 2])
        vs1 = sb2("vs1", [P, 3])
        Q1 = {k: sb2("Q1_" + k, [P, NC, B, T], F32R) for k in "hl"}
        m1 = sb2("m1", [P, B, TB, H1])
        NM = sb2("NM", [H1, B, T], F32R)
        PT1 = sb2("PT1", [P, RING1, HALF])
        PR1 = sb2("PR1", [P, RING1, HALF], F16)
        rs8 = sb2("rs8", [P, TB])
        A1T = {k: sb2("A1T_" + k, [P, NC, HALF], F32R) for k in "hl"}
        st2.close()
        st3 = ExitStack()

        def sb3(name, shape, dt=F32):
            return st3.enter_context(nc.sbuf_tensor(name, shape, dt))

        LT1 = sb3("LT1", [E1, GR, HALF])
        wgu_raw = sb3("wgu_raw", [P, EM, 2, NC, P])
        wgus = {k: sb3("wgu_" + k, [P, EM, 2, NC, P], F32R) for k in "hl"}
        wd_raw = sb3("wd_raw", [P, EM, D])
        wds = {k: sb3("wd_" + k, [P, EM, D], F32R) for k in "hl"}
        cw = sb3("cw", [P, 2, TAPS * NC])
        cwh = sb3("cwh", [P, TAPS * NC], F32R)
        diag = {k: sb3("diag_" + k, [P, TAPS * NC, P], F32R) for k in "hl"}
        cb = sb3("cb", [P, NC])
        convT = sb3("convT", [P, 2, HALF])
        silu = sb3("silu", [P, 2, HALF])
        gated = sb3("gated", [P, 2, HALF])
        gs = {k: sb3("g_" + k, [P, 3, HALF], F32R) for k in "hl"}
        reluY = sb3("reluY", [P, 4, D])
        st3.close()

        s_in = sem("inputs_loaded")
        s_x = [sem(f"tokens{g}_loaded") for g in range(GR)]
        s_zero = sem("context_cleared")
        s_const = sem("constants_ready")
        s_dve = sem("vector_chain")
        s_var = sem("variances_ready")
        s_rstd = sem("rstds_ready")
        s_lnc = sem("context_normalised")
        s_ln = sem("latents_normalised")
        s_lat_full = sem("latent_bank_full")
        s_lat_hi = sem("latent_hi_ready")
        s_lat_f = sem("latent_full_ready")
        s_lat_lo = sem("latent_lo_ready")
        s_wqk_raw, s_wv_raw, s_wo_raw = sem("wqk_loaded"), sem("wv_loaded"), sem("wo_loaded")
        s_wvh = sem("wv_rounded")
        s_wqk, s_wv, s_wo = sem("wqk_split"), sem("wv_split"), sem("wo_split")
        s_bounds, s_bound, s_vs = sem("bounds_by_partition"), sem("bounds_ready"), sem("value_scale_ready")
        s_rem_pool, s_rem_dve = sem("remainders_by_gpsimd"), sem("remainders_by_vector")
        s_job = sem("shared_bank_full")
        s_cast = sem("shared_bank_rounded")
        s_jobfree = sem("shared_bank_free")
        s_mx = sem("max_bank_full")
        s_mxfree = sem("max_bank_free")
        s_max = sem("head_max_ready")
        s_maxT = sem("head_max_transposed")
        s_maxrow = sem("head_max_row_ready")
        s_stack = [sem("stack0_loaded"), sem("stack1_loaded")]
        s_row = [sem("max_row0_loaded"), sem("max_row1_loaded")]
        s_score = sem("scores_ready")
        s_exp = sem("exp_done")
        s_pv = sem("pv_done")
        s_rec = sem("sums_inverted")
        s_pvc = sem("pv_bank_copied")
        s_norm = sem("attention_normalised")
        s_out = sem("output_written")
        s_in1 = sem("expert_inputs_loaded")
        s_xn = sem("tokens_normalised")
        s_tj = sem("transposed_bank_full")
        s_thi = sem("transposed_hi_ready")
        s_tfree = sem("transposed_bank_free")
        s_wr = sem("router_weights_split")
        s_rt = sem("router_bank_full")
        s_lt = sem("router_bank_copied")
        s_route = sem("router_logits_ready")
        s_bt = sem("routing_bank_full")
        s_rexp_in = sem("router_exponents_ready")
        s_rexp = sem("router_exp_done")
        s_R = sem("routing_weights_ready")
        s_RT = sem("routing_weights_transposed")
        s_w1_raw, s_w2_raw = sem("w1_loaded"), sem("w2_loaded")
        s_w1, s_w2 = sem("w1_split"), sem("w2_split")
        s_w0h = sem("first_expert_weights_rounded")
        s_b1e = [sem("even_expert_biases_loaded"), sem("odd_expert_biases_loaded")]
        s_up = sem("hidden_bank_full")
        s_hhi = sem("hidden_hi_ready")
        s_hf = sem("hidden_bank_free")
        s_hlo = sem("hidden_lo_ready")
        s_down = sem("hidden_used")
        s_accfree = sem("output_banks_free")
        s_in2 = sem("layer1_attention_loaded")
        s_wa = sem("layer1_weights_split")
        s_wa_in = sem("layer1_attention_weights_loaded")
        s_wah = sem("layer1_weights_rounded")
        s_a1 = sem("layer1_bank_full")
        s_a1h = sem("layer1_bank_rounded")
        s_a1e = sem("layer1_bank_free")
        s_kd = sem("layer1_key_blocks_hi")
        s_kdl = sem("layer1_key_blocks_lo")
        s_vb, s_vbr = sem("layer1_value_bounds"), sem("layer1_value_bound_ready")
        s_v1 = sem("layer1_values_ready")
        s_mx1 = sem("layer1_max_banks_full")
        s_m8 = sem("layer1_max_ready")
        s_sc1 = sem("layer1_scores_ready")
        s_ex1 = sem("layer1_exp_done")
        s_r1p, s_r1v = sem("layer1_remainders_by_gpsimd"), sem("layer1_remainders_by_vector")
        s_pv1 = sem("layer1_pv_done")
        s_rs1 = sem("layer1_sums_inverted")
        s_nm1 = sem("layer1_attention_normalised")
        s_in3 = sem("layer1_experts_loaded")
        s_w3 = sem("layer1_expert_weights_split")
        s_conv = sem("convolution_bank_full")
        s_convc = sem("convolution_copied")
        s_convt = sem("convolution_transposed")
        s_convfree = sem("convolution_bank_free")
        s_gu = sem("gate_and_up_full")
        s_silu = sem("silu_ready")
        s_gated = sem("gated_ready")
        s_ghi = sem("gated_hi_ready")
        s_glo = sem("gated_lo_ready")
        s_acc1 = sem("layer1_down_added")
        s_dn1h = sem("layer1_down_half_full")
        s_w3d = sem("tap_diagonals_ready")
        s_ones = sem("layer1_constants_ready")

        def flat4(t):
            return t[:].rearrange("p a b c -> p (a b c)")

        def flat(t):
            return t[:] if len(t.shape) == 2 else t[:].rearrange(
                "p a b -> p (a b)" if len(t.shape) == 3 else "p a b c -> p (a b c)")

        chain = [0]

        def link(dve, ins):
            chain[0] += 1
            ins.then_inc(s_dve, 1)
            dve.wait_ge(s_dve, chain[0])

        lns = [0]

        def ln_sums(dve, src, t0, n):
            for t in range(t0, t0 + n):
                ins = nc.vector.bn_stats(stats[:, t, :], src[:, t, :])
            link(dve, ins)
            st = stats[:, t0:t0 + n]
            me, mo = st[:, :, 1], st[:, :, 4]
            mean, dif, m2, var, rstd, sq = (ln_tmp[:, i, t0:t0 + n] for i in range(6))
            nc.vector.tensor_tensor(mean, me, mo, ALU.add)
            nc.vector.tensor_tensor(m2, st[:, :, 2], st[:, :, 5], ALU.add)
            link(dve, nc.vector.tensor_tensor(dif, me, mo, ALU.subtract))
            link(dve, nc.vector.tensor_tensor(sq, dif, dif, ALU.mult))
            link(dve, nc.vector.scalar_tensor_tensor(out=sq, in0=sq, scalar=D / 4.0, in1=m2,
                                                     op0=ALU.mult, op1=ALU.add))
            nc.vector.tensor_scalar(mean, mean, 0.5, None, ALU.mult)
            nc.vector.tensor_scalar(var, sq, 1.0 / D, EPS, ALU.mult, ALU.add).then_inc(s_var, 1)

        def ln_apply(dve, src, dst, t0, n, last=None):
            lns[0] += 1
            dve.wait_ge(s_rstd, lns[0])
            for t in range(t0, t0 + n):
                ins = nc.vector.tensor_scalar(dst[:, t, :], src[:, t, :], ln_tmp[:, 0, t:t + 1], ln_tmp[:, 4, t:t + 1],
                                              ALU.subtract, ALU.mult)
            if last is None:
                link(dve, ins)
            else:
                ins.then_inc(last, 1)

        def normalise(dve, src, dst, t0, n, last=None):
            ln_sums(dve, src, t0, n)
            ln_apply(dve, src, dst, t0, n, last)

        powers = [0]

        def rstds(pool, t0=None):
            powers[0] += 1
            cols = slice(0, B) if t0 is None else slice(t0, t0 + 4)
            pool.wait_ge(s_var, powers[0])
            nc.gpsimd.tensor_tensor(ln_tmp[:, 4, cols], ln_tmp[:, 3, cols], nhalf[:, cols],
                                    ALU.pow).then_inc(s_rstd, 1)

        LATJOBS = [(b, c, 2) for b in range(B) for c in range(NC)] + \
                  [(b, c, h) for b in range(B) for h in range(2) for c in range(NC)]

        def jobs_before(b, i):
            return VJOBS + 5 + b * (JOBS * PAIRS + AWJOBS + VJOBS) + JOBS * i

        def casts_before(b, i):
            return VJOBS + 5 + b * (CASTS * PAIRS + 2 + VJOBS) + CASTS * i

        def first_qk_bank(j):
            return max_banks[:, j % 2 * HALF:j % 2 * HALF + HALF]

        def bank(idx):
            return shared[(1 + idx) % 2]

        def upper(s):
            return PT[:, s % RING, :].bitcast(BF16).rearrange("p (n two) -> p n two", two=2)[:, :, 1]

        VECTOR_STEPS = (2, 11, 13, 15, 17, 19, 29, 31, 33, 35)

        def on_vector(s):
            return s in VECTOR_STEPS

        def by_vector(s):
            return sum(v <= s for v in VECTOR_STEPS)

        def turns(eng, emit, batch=None, flush=None):
            for b in range(B):
                if batch:
                    batch(b)
                with eng.Fori(0, PAIRS - 1) as i:
                    emit(b, i, b * PAIRS + i, b)
                emit(b, PAIRS - 1, b * PAIRS + PAIRS - 1, b + 1 if b + 1 < B else None)
                if flush:
                    flush(b, jobs_before(b, PAIRS) if b + 1 < B else jobs_before(b, PAIRS - 1) + AWJOBS,
                          casts_before(b, PAIRS) if b + 1 < B else casts_before(b, PAIRS - 1) + 2)

        ATT0_JOBS = jobs_before(1, PAIRS - 1) + 2 * AWJOBS
        def t_banks(z, g):
            return [ps[:, 0, :], ps[:, 1, :]] if z == 2 else [ps[:, 2, :], ps[:, 5, :]] if z == 1 and g >= 2 else tbank

        tbank = [ps[:, 6, :], ps[:, 7, :]]
        TJOBS = [(c, b, h) for b in range(B) for h in range(2) for c in range(NC)]

        hidden_banks = [ps[:, 0, :], ps[:, 1, :]]
        acc_banks = [ps[:, 2:4, :].rearrange("p a n -> p (a n)"), ps[:, 4:6, :].rearrange("p a n -> p (a n)")]
        score1 = [ps[0:S, 3, :], ps[0:S, 4, :]]
        pv1 = [ps[:, i, 0:TB * (D1 + 1)].rearrange("p (t d) -> p t d", t=TB) for i in (5, 2)]
        CT_JOB, K_JOB, V_JOB, Q_JOB, NM_JOB, OUT_JOB = 0, 2, 4, 6, 14, 18

        def max1_banks(i):
            a = 3 * (i % 2) if i < TB * NC else 0
            return ps[:, a:a + 2, 0:HC // 2 * SP]

        WA_ORDER = (1, 2, 0, 3)
        QJOBS = [(b, c, h) for b in range(B) for c in range(NC) for h in range(2)]
        NM_AT = (18, 19)
        T3_AFTER, Q_AFTER = 5, {9: 4, 11: 5, 13: 6, 15: 7}
        OUT_T, OUT_P, OUT_LN, OUT_XT = {36: 0, 43: 1}, {39: 0, 46: 1}, {42: 0, 49: 1}, {50: 0, 56: 1}
        CONST1 = 11

        def upper1(k):
            return PT1[:, k % RING1, :].bitcast(BF16).rearrange("p (n two) -> p n two", two=2)[:, :, 1]

        gate_banks, up_banks = [ps[:, 0, :], ps[:, 1, :]], [ps[:, 2, :], ps[:, 3, :]]
        down_banks = [ps[:, 4, :], ps[:, 5, :]]

        A_AT, WO_AT = 1, 3
        M1_AT, M1_MAX, M1_T = 1, 9, 12
        QK_AT, M0_AT, M0_MAX, M0_T = 13, 19, 27, 29
        WQK_AT, WO_SPLIT_AT = 9, 16

        UNITS = GR * FC
        UP_AHEAD = 2
        SPLIT_AFTER = {2 + k * (UNITS - 4) // (2 * FC - 1): k for k in range(2 * FC)}

        TAIL_POWERS = {FC * (g + 1) + p: 4 * g for g in range(GR - 1) for p in (2, 6)}
        TAIL_T = {FC * (g + 2): g for g in range(GR - 2)}
        WA_AT = (1, 3, 5, 7)
        KV_AT = {2: 0, 3: 1, 6: 2, 7: 3, 10: 4, 11: 5}
        B2_UNITS = 12

        def experts(eng, emit):
            with eng.Fori(0, E0 // 2 - 1) as i:
                for k in range(2):
                    emit(2 * i + k, k, i, True)
            for k in range(2):
                emit(E0 - 2 + k, k, E0 // 2 - 1, k == 0)

        EARLY_LN = {20: 0, 24: 1}

        block = stack.enter_context(nc.Block())

        @block.sync
        def _(sp):
            sp.wait_ge(s_zero, 1)
            sp.dma_start(C[0:S], ctx.rearrange("b s d -> s b d")).then_inc(s_in, 16)
            sp.dma_start(C[S:SP], ctx[:, S - 1:S, :].rearrange("b s d -> s b d")).then_inc(s_in, 16)
            for i, w in enumerate((ln1w, ln1b, ln2w, ln2b)):
                sp.dma_start(lnp[:, i, :], w).then_inc(s_in, 16)
            for g in range(GR):
                sp.dma_start(X[:, 4 * g:4 * g + 4, :], x[g // 2, HALF * (g % 2):HALF * (g % 2) + HALF]
                             .rearrange("(t p) d -> p t d", p=P)).then_inc(s_x[g], 16)
            sp.dma_start(wqk_raw[:], wqk0[0]).then_inc(s_wqk_raw, 16)
            sp.dma_start(wv_raw[:], wv0).then_inc(s_wv_raw, 16)
            sp.dma_start(wo_raw[:], wo0[0]).then_inc(s_wo_raw, 16)

            def stack_head(h):
                r = slice(HD * h, HD * h + HD)
                for dst, src in ((QA[h][0:HD], Q["h"][r]), (QA[h][HD:P], Q["h"][r]), (QB[h][0:HD], Q["l"][r])):
                    sp.dma_start(dst.bitcast(F32), src.bitcast(F32)).then_inc(s_stack[h], 16)
                for dst, src in ((KA[h][0:HD, 0:NK], K["h"][r, 0:NK]), (KA[h][HD:P, 0:NK], K["l"][r, 0:NK]),
                                 (KB[h][0:HD, 0:NK], K["h"][r, 0:NK])):
                    sp.dma_start(dst.bitcast(F32), src.bitcast(F32)).then_inc(s_stack[h], 16)

            def max_row(h):
                sp.dma_start(QB[h][HD:HD + 1, :].bitcast(F32).rearrange("o (t p) -> o t p", t=TB), maxT[h][:].bitcast(F32)) \
                    .then_inc(s_row[h], 16)

            sp.wait_ge(s_jobfree, 2 + 5)
            stack_head(0)
            sp.wait_ge(s_maxrow, 1)
            max_row(0)

            def turn(b, i, g, nb):
                sp.wait_ge(s_score, STEPS * g + 1)
                stack_head(1)
                sp.wait_ge(s_wo, 2 * (g + b) + 2)
                sp.dma_start(wo_raw[:], wo0[i] if isinstance(i, int) else wo0[bass.ds(i, 1)].squeeze(0)) \
                    .then_inc(s_wo_raw, 16)
                if nb is not None:
                    nxt = (i + 1) % PAIRS if isinstance(i, int) else i + 1
                    sp.wait_ge(s_wqk, 2 * g + 2)
                    sp.dma_start(wqk_raw[:], wqk0[nxt] if isinstance(nxt, int) else wqk0[bass.ds(nxt, 1)].squeeze(0)) \
                        .then_inc(s_wqk_raw, 16)
                sp.wait_ge(s_maxrow, 2 * g + 2)
                max_row(1)
                if nb is not None:
                    sp.wait_ge(s_jobfree, jobs_before(b, i) + AWJOBS + 5 + 2)
                    stack_head(0)
                    sp.wait_ge(s_maxrow, 2 * g + 3)
                    max_row(0)

            def next_batch(b):
                if b > 0:
                    sp.wait_ge(s_wo, 2 * (PAIRS + 1) * b)
                    sp.dma_start(wo_raw[:], wo0[0]).then_inc(s_wo_raw, 16)

            turns(sp, turn, batch=next_batch)
            sp.wait_ge(s_jobfree, ATT0_JOBS + 2)
            for dst, src in ((wr_raw, wr), (rb, rbias.partition_broadcast(P)), (b2s, b2),
                             (gbs, gb.partition_broadcast(P))):
                sp.dma_start(dst[:], src).then_inc(s_in1, 16)
            for k in range(2):
                sp.dma_start(b1e[:, k], b1[k]).then_inc(s_b1e[k], 16)
            sp.dma_start(w1_raw[:], w1[0]).then_inc(s_w1_raw, 16)
            sp.dma_start(w2_raw[:], w2[0]).then_inc(s_w2_raw, 16)

            def load_expert(e):
                sp.wait_ge(s_w1, 2 * FC * e)
                sp.dma_start(w1_raw[:], w1[e] if isinstance(e, int) else w1[bass.ds(e, 1)].squeeze(0)) \
                    .then_inc(s_w1_raw, 16)
                sp.wait_ge(s_w2, 2 * FC * e)
                sp.dma_start(w2_raw[:], w2[e] if isinstance(e, int) else w2[bass.ds(e, 1)].squeeze(0)) \
                    .then_inc(s_w2_raw, 16)

            sp.wait_ge(s_zero, 2)
            sp.dma_start(C1[0:S], ctx.rearrange("b s d -> s b d")).then_inc(s_in2, 16)
            sp.dma_start(C1[S:SP], ctx[:, S - 1:S, :].rearrange("b s d -> s b d")).then_inc(s_in2, 16)
            sp.dma_start(bqk[:], bqk1).then_inc(s_in2, 16)
            sp.dma_start(bvo_raw[:], bvo1).then_inc(s_in2, 16)

            load_expert(1)
            with sp.Fori(0, E0 // 2 - 1) as i:
                for k in range(2):
                    e = 2 * i + 2 + k
                    load_expert(e)
                    sp.wait_ge(s_hf, UNITS * (e - 1) + 2)
                    sp.dma_start(b1e[:, k], b1[bass.ds(e, 1)].squeeze(0)).then_inc(s_b1e[k], 16)

            sp.wait_ge(s_w1, 2 * FC * E0)
            sp.dma_start(wa_raw, watt).then_inc(s_wa_in, 16)

            sp.wait_ge(s_a1e, OUT_JOB + 4 * GR)
            for dst, src in ((wgu_raw[:], wgu), (wd_raw[:], wd), (cw[:, 0, :], convw), (cb[:], convb)):
                sp.dma_start(dst, src).then_inc(s_in3, 16)
            for g in range(GR):
                sp.wait_ge(s_acc1, 4 * EM * (g + 1))
                sp.dma_start(out[g // 2, HALF * (g % 2):HALF * (g % 2) + HALF].rearrange("(t p) d -> p t d", p=P),
                             X[:, 4 * g:4 * g + 4, :]).then_inc(s_out, 16)
            sp.wait_ge(s_out, 16 * GR)

        @block.gpsimd
        def _(pool):
            nc.gpsimd.memset(C[:], 0.0).then_inc(s_zero, 1)
            nc.gpsimd.memset(nhalf[:], -0.5).then_inc(s_const, 1)
            nc.gpsimd.memset(ident[:], 0.0).then_inc(s_const, 1)
            nc.gpsimd.memset(zeros[:], 0.0).then_inc(s_const, 1)
            nc.gpsimd.memset(V["h"][:, :, :, HD:HD + 1], 1.0).then_inc(s_const, 1)
            nc.gpsimd.memset(V["l"][:, :, :, HD:HD + 1], 0.0).then_inc(s_const, 1)
            pool.wait_ge(s_const, 7)
            nc.gpsimd.affine_select(out=ident[:], in_=ident[:], compare_op=ALU.not_equal, fill=1.0, base=0,
                                    pattern=[[-1, P]], channel_multiplier=1).then_inc(s_const, 1)
            rstds(pool)
            for g in (0, 1, 0, 1):
                rstds(pool, 4 * g)

            def split(raw, parts, loaded, n, done):
                pool.wait_ge(loaded, 16 * n + 16)
                nc.gpsimd.tensor_tensor(flat(parts["h"]), flat(raw), zeros[:, 0:1].to_broadcast([P, flat(raw).shape[1]]),
                                        ALU.add).then_inc(done, 1)
                pool.wait_ge(done, 2 * n + 1)
                nc.gpsimd.tensor_tensor(flat(parts["l"]), flat(raw), flat(parts["h"]).bitcast(F32), ALU.subtract) \
                    .then_inc(done, 1)

            def latents_lo(k, b, c, h):
                pool.wait_ge(s_lat_f, k + 1)
                pool.wait_ge(s_lat_hi, k + 1)
                n = HALF if h < 2 else SP
                cols = slice(HALF * h, HALF * h + n)
                nc.gpsimd.tensor_tensor(lat["l"][:, b, c, cols], latf[:, k % 2, 0:n],
                                        lat["h"][:, b, c, cols].bitcast(F32), ALU.subtract).then_inc(s_lat_lo, 1)

            for k, (b, c, h) in enumerate(LATJOBS):
                if k == 4:
                    rstds(pool, 8)
                    rstds(pool, 12)
                if k in (5, 6):
                    rstds(pool, 4 * (k - 3))
                latents_lo(k, b, c, h)
            pool.wait_ge(s_wvh, 1)
            nc.gpsimd.tensor_tensor(wv["l"][:, 0], wv_raw[:, 0], wv["h"][:, 0].bitcast(F32), ALU.subtract).then_inc(s_wv, 1)
            pool.wait_ge(s_bounds, 1)
            nc.gpsimd.partition_all_reduce(bound[:], bounds[:], P, RMAX).then_inc(s_bound, 1)
            split(wo_raw, wo, s_wo_raw, 0, s_wo)

            def turn(b, i, g, nb):
                for s in range(STEPS):
                    if not on_vector(s):
                        m = P if s % KT < TB else S
                        pool.wait_ge(s_exp, STEPS * g + s + 1 + 2)
                        nc.gpsimd.tensor_tensor(PR[0:m, s % RING, :], PT[0:m, s % RING, :], upper(s)[0:m],
                                                ALU.subtract).then_inc(s_rem_pool, 1)
                    if isinstance(i, int) and b + 1 == B and s - AHEAD + 1 in EARLY_LN:
                        rstds(pool, 4 * EARLY_LN[s - AHEAD + 1])
                    if nb is not None and s == WQK_AT:
                        split(wqk_raw, wqk, s_wqk_raw, g + 1, s_wqk)
                    if s == WO_SPLIT_AT:
                        pool.wait_ge(s_job, jobs_before(b, i) + AWJOBS)
                        split(wo_raw, wo, s_wo_raw, g + b + 1, s_wo)

            def next_batch(b):
                if b > 0:
                    pool.wait_ge(s_job, jobs_before(b, 0) - VJOBS)
                    split(wo_raw, wo, s_wo_raw, (PAIRS + 1) * b, s_wo)

            turns(pool, turn, batch=next_batch)

            def split_part(raw, hi, lo, done, n):
                nc.gpsimd.tensor_tensor(hi, raw, zeros[:, 0:1].to_broadcast([P, raw.shape[1]]), ALU.add).then_inc(done, 1)
                pool.wait_ge(done, 2 * n + 1)
                nc.gpsimd.tensor_tensor(lo, raw, hi.bitcast(F32), ALU.subtract).then_inc(done, 1)

            pool.wait_ge(s_jobfree, ATT0_JOBS + 2)
            nc.gpsimd.memset(C1[:], 0.0).then_inc(s_zero, 1)
            nc.gpsimd.iota(iota8[:], pattern=[[1, E0]], base=0, channel_multiplier=0,
                           allow_small_or_imprecise_dtypes=True).then_inc(s_const, 1)
            for k in "hl":
                nc.gpsimd.memset(XT[k][:, :, :, 0:PAD].bitcast(F32), 0.0).then_inc(s_const, 1)
            for g in range(GR // 2, GR):
                rstds(pool, 4 * g)
            for f in range(FC):
                for i, (parts, raw, done) in enumerate(((w1s, w1_raw, s_w1), (w2s, w2_raw, s_w2))):
                    pool.wait_ge(s_w0h, 2 * f + i + 1)
                    nc.gpsimd.tensor_tensor(parts["l"][:, 0, f], raw[:, f], parts["h"][:, 0, f].bitcast(F32),
                                            ALU.subtract).then_inc(done, 2)

            def expert(e, k, i, more):
                for u in range(UNITS):
                    n = UNITS * e + u
                    pool.wait_ge(s_hf, n + 1 + 2)
                    nc.gpsimd.tensor_tensor(hs["l"][:, u % 4], hf[:, u % 2], hs["h"][:, u % 4].bitcast(F32),
                                            ALU.subtract).then_inc(s_hlo, 1)
                    if more and u in SPLIT_AFTER:
                        next_chunk(e, 1 - k, SPLIT_AFTER[u])
                    if not more and u in TAIL_POWERS:
                        rstds(pool, TAIL_POWERS[u])
                    if not more and u in WA_AT:
                        w = WA_ORDER[WA_AT.index(u)]
                        pool.wait_ge(s_wah, WA_AT.index(u) + 1)
                        nc.gpsimd.tensor_tensor(flat(wa["l"][:, w]), wa_raw[:, w].rearrange("p c d -> p (c d)"), flat(wa["h"][:, w]).bitcast(F32),
                                                ALU.subtract).then_inc(s_wa, 1)

            def next_chunk(e, place, j):
                parts, raw, loaded, done = ((w1s, w1_raw, s_w1_raw, s_w1), (w2s, w2_raw, s_w2_raw, s_w2))[j // FC]
                f = j % FC
                if j == 0:
                    pool.wait_ge(s_down, UNITS * e + 4)
                if f == 0:
                    pool.wait_ge(loaded, 16 * e + 32)
                split_part(raw[:, f], parts["h"][:, place, f], parts["l"][:, place, f], done, FC * e + FC + f)

            experts(pool, expert)
            pool.wait_ge(s_accfree, GR * E0 + 2)
            nc.gpsimd.memset(V1["h"][:, :, :, D1:D1 + 1], 1.0).then_inc(s_const, 1)
            nc.gpsimd.memset(V1["l"][:, :, :, D1:D1 + 1], 0.0).then_inc(s_const, 1)
            nc.gpsimd.memset(mask_f[:], 0.0).then_inc(s_const, 1)
            nc.gpsimd.memset(hmask[:], 1.0).then_inc(s_const, 1)
            nc.gpsimd.memset(vb[:], 0.0).then_inc(s_const, 1)
            pool.wait_ge(s_const, CONST1 + 5)
            nc.gpsimd.affine_select(out=mask_f[:, 0, :], in_=mask_f[:, 0, :], compare_op=ALU.is_ge, fill=-1e30, base=0,
                                    pattern=[[-1, P]], channel_multiplier=1).then_inc(s_const, 1)
            nc.gpsimd.affine_select(out=mask_f[:, 1, :], in_=mask_f[:, 1, :], compare_op=ALU.is_ge, fill=-1e30, base=0,
                                    pattern=[[1, P]], channel_multiplier=-1).then_inc(s_const, 1)
            nc.gpsimd.affine_select(out=hmask[:], in_=hmask[:], compare_op=ALU.is_ge, fill=0.0, base=0,
                                    pattern=[[-D1, HC]], channel_multiplier=1).then_inc(s_const, 1)
            pool.wait_ge(s_const, CONST1 + 8)
            nc.gpsimd.affine_select(out=hmask[:], in_=hmask[:], compare_op=ALU.is_ge, fill=0.0, base=D1 - 1,
                                    pattern=[[D1, HC]], channel_multiplier=-1).then_inc(s_const, 1)
            for k in range(2):
                rstds(pool, 4 * GR - 4)
            for c in range(NC):
                pool.wait_ge(s_a1e, K_JOB + c + 1)
                for b in range(B):
                    keys = K1["l"][:, c, b * SP:b * SP + SP].bitcast(F32)
                    nc.gpsimd.tensor_tensor(KD["l"][:, b, c], keys.unsqueeze(1).to_broadcast([P, HC, SP]),
                                            hmask[:].unsqueeze(2).to_broadcast([P, HC, SP]), ALU.mult).then_inc(s_kdl, 1)
            pool.wait_ge(s_vb, 1)
            nc.gpsimd.partition_all_reduce(vb[:, 1:2], vb[:, 0:1], P, RMAX).then_inc(s_vbr, 1)
            for k in range(0, K1S, 2):
                pool.wait_ge(s_ex1, k + 1)
                nc.gpsimd.tensor_tensor(PR1[0:S, k % RING1, :], PT1[0:S, k % RING1, :], upper1(k)[0:S],
                                        ALU.subtract).then_inc(s_r1p, 1)
                for at in (k - 4, k - 3):
                    if at in OUT_LN:
                        rstds(pool, 4 * OUT_LN[at])

            for g in range(GR // 2, GR):
                rstds(pool, 4 * g)
            pool.wait_ge(s_in3, 16 * 4)
            split_part(wgu_raw[:].rearrange("p e a c n -> p (e a c n)"),
                       wgus["h"][:].rearrange("p e a c n -> p (e a c n)"),
                       wgus["l"][:].rearrange("p e a c n -> p (e a c n)"), s_w3, 0)
            split_part(flat(wd_raw), flat(wds["h"]), flat(wds["l"]), s_w3, 1)
            for n in range(GR * EM):
                pool.wait_ge(s_ghi, n + 1)
                nc.gpsimd.tensor_tensor(gs["l"][:, n % 3], gated[:, n % 2], gs["h"][:, n % 3].bitcast(F32),
                                        ALU.subtract).then_inc(s_glo, 1)

        @block.scalar
        def _(act):
            def round_qk(j, job, bk):
                act.wait_ge(s_job, job + 1)
                dst = (Q["h"][:, 0:HALF], Q["h"][:, HALF:T], K["h"][:, 0:HALF], K["h"][:, HALF:T], K["h"][:, T:NK])[j]
                nc.scalar.copy(dst, bk[:, 0:SP] if j == 4 else bk).then_inc(s_cast, 1)

            act.wait_ge(s_in, 16 * 6)
            for k, (b, c, h) in enumerate(LATJOBS):
                act.wait_ge(s_lat_full, k + 1)
                n = HALF if h < 2 else SP
                w = 2 if h < 2 else 0
                nc.scalar.activation(lat["h"][:, b, c, HALF * h:HALF * h + n], shared[k % 2][:, 0:n], ACT.Identity,
                                     bias=lnp[:, w + 1, c:c + 1], scale=lnp[:, w, c:c + 1]).then_inc(s_lat_hi, 1)
                if k == WQK0_AT:
                    act.wait_ge(s_wqk_raw, 16)
                    nc.scalar.copy(flat(wqk["h"]), flat(wqk_raw)).then_inc(s_wqk, 1)
                if k >= QK0_AT:
                    round_qk(k - QK0_AT, k - QK0_AT, first_qk_bank(k - QK0_AT))

            act.wait_ge(s_wv_raw, 16)
            for c in range(NC):
                nc.scalar.copy(wv["h"][:, c], wv_raw[:, c]).then_inc(s_wvh, 1)

            def values(b, job):
                if b == 0:
                    act.wait_ge(s_vs, 1)
                for j in range(VJOBS):
                    kt, half = divmod(j, 2)
                    m = P if kt < TB else S
                    act.wait_ge(s_job, job + j + 1)
                    if b > 0 and j == 0:
                        act.wait_ge(s_pv, STEPS * PAIRS * b + RING)
                    nc.scalar.activation(V["h"][0:m, kt, PAIRS * half:PAIRS * half + PAIRS, 0:HD],
                                         shared[(job + j) % 2][0:m].rearrange("p (h d) -> p h d", d=HD), ACT.Identity,
                                         scale=vs[0:m, 0:1]).then_inc(s_cast, 1)

            for j in range(len(LATJOBS) - QK0_AT, 5):
                round_qk(j, j, first_qk_bank(j))
            values(0, 5)

            def att_hi(job, j):
                act.wait_ge(s_job, job + j + 1)
                nc.scalar.copy(ATT["h"][:, HALF * j:HALF * j + HALF], bank(j)).then_inc(s_cast, 1)

            def turn(b, i, g, nb):
                for s in range(STEPS):
                    m = P if s % KT < TB else S
                    act.wait_ge(s_score, STEPS * g + s + 1)
                    act.wait_ge(s_pv, STEPS * g + s + 1)
                    nc.scalar.activation(PT[0:m, s % RING, :], score_banks[s % 2][0:m], ACT.Exp,
                                         scale=HD ** -0.5).then_inc(s_exp, 1)
                    at = s - AHEAD
                    if at >= 0 and at % KT == KT - 1:
                        u = at // KT
                        act.wait_ge(s_pv, STEPS * g + at + 1 + RING)
                        act.wait_ge(s_norm, 4 * g + u + 1)
                        nc.scalar.copy(PVS[:, u % 2], pv_bank).then_inc(s_pvc, 1)
                    if A_AT <= at < A_AT + 2:
                        att_hi(jobs_before(b, i), at - A_AT)
                    if nb is not None and QK_AT <= at < QK_AT + 5:
                        if at == QK_AT:
                            act.wait_ge(s_stack[1], 96 * g + 96)
                        j = at - QK_AT
                        round_qk(j, jobs_before(b, i) + AWJOBS + j, bank(AWJOBS + j))

            def next_batch(b):
                if b > 0:
                    values(b, jobs_before(b, 0) - VJOBS)

            def flush(b, job, cast):
                for j in range(2):
                    act.wait_ge(s_job, job + j + 1)
                    nc.scalar.copy(ATT["h"][:, HALF * j:HALF * j + HALF], shared[(job + j) % 2]).then_inc(s_cast, 1)

            turns(act, turn, next_batch, flush)

            def group_hi(z, g):
                for k in (2 * g, 2 * g + 1):
                    c, b, h = TJOBS[k]
                    act.wait_ge(s_tj, XJ * z + k + 1)
                    nc.scalar.copy(XT["h"][:, c, b, PAD + HALF * h:PAD + HALF * h + HALF], t_banks(z, g)[k % 2]) \
                        .then_inc(s_thi, 1)

            def copy_logits(layer, LT):
                for g in range(GR):
                    act.wait_ge(s_rt, GR * layer + g + 1)
                    nc.scalar.copy(LT[:, g, :], tbank[g % 2][0:E0]).then_inc(s_lt, 1)

            for g in range(GR):
                group_hi(0, g)
                for f in {GR - 2: range(FC // 4), GR - 1: range(FC // 4, FC)}.get(g, ()):
                    for parts, raw, loaded in ((w1s, w1_raw, s_w1_raw), (w2s, w2_raw, s_w2_raw)):
                        act.wait_ge(loaded, 16)
                        nc.scalar.copy(parts["h"][:, 0, f], raw[:, f]).then_inc(s_w0h, 1)
            copy_logits(0, LT0)
            act.wait_ge(s_rexp_in, 1)
            nc.scalar.activation(rw[:, 1, :], rw[:, 0, :], ACT.Exp).then_inc(s_rexp, 1)
            act.wait_ge(s_in1, 16 * 4)

            def round_job(j, dst, src, bias=None):
                act.wait_ge(s_a1, j + 1)
                ins = nc.scalar.copy(dst, src) if bias is None else \
                    nc.scalar.activation(dst, src, ACT.Identity, bias=bias)
                ins.then_inc(s_a1h, 1)

            def round_kv(j):
                c = j % NC
                if j < K_JOB:
                    round_job(j, CT["h"][:, c], tbank[j % 2][:, 0:B * SP].rearrange("p (b s) -> p b s", b=B))
                elif j < V_JOB:
                    round_job(j, K1["h"][:, c], tbank[j % 2][:, 0:B * SP], bqk[:, 1, c:c + 1])

            def expert(e, k, i, more):
                act.wait_ge(s_b1e[k], 16 * i + 16)
                for u in range(UNITS):
                    n = UNITS * e + u
                    act.wait_ge(s_up, n + 1)
                    act.wait_ge(s_down, n + 1)
                    nc.scalar.activation(hs["h"][:, u % 4], hidden_banks[u % 2], ACT.Relu,
                                         bias=b1e[:, k, u % FC:u % FC + 1]).then_inc(s_hhi, 1)
                    if not more and u < 4:
                        act.wait_ge(s_wa_in, 16)
                        w = WA_ORDER[u]
                        nc.scalar.copy(wa["h"][:, w], wa_raw[:, w]).then_inc(s_wah, 1)
                    if not more and u - UP_AHEAD in KV_AT:
                        round_kv(KV_AT[u - UP_AHEAD])
                    if not more and u - UP_AHEAD in TAIL_T:
                        group_hi(1, TAIL_T[u - UP_AHEAD])

            act.wait_ge(s_in2, 16 * 4)
            experts(act, expert)


            for i, (b, c, h) in enumerate(QJOBS):
                if i == GR:
                    for g in range(GR // 2, GR):
                        group_hi(1, g)
                j = Q_JOB + i
                round_job(j, Q1["h"][:, c, b, HALF * h:HALF * h + HALF], tbank[j % 2], bqk[:, 0, c:c + 1])

            def round_out(g):
                for c in range(NC):
                    j = OUT_JOB + 4 * g + c
                    round_job(j, A1T["h"][:, c, :], tbank[j % 2])

            for k in range(K1S):
                act.wait_ge(s_sc1, k + 1)
                if k >= RING1:
                    act.wait_ge(s_pv1, k - RING1 + 1)
                nc.scalar.activation(PT1[0:S, k % RING1, :], score1[k % 2], ACT.Exp, scale=D1 ** -0.5).then_inc(s_ex1, 1)
                at = k - AHEAD
                if at in OUT_T:
                    round_out(OUT_T[at])
                if at in OUT_XT:
                    group_hi(2, OUT_XT[at])
            for g in range(GR // 2, GR):
                round_out(g)
            group_hi(2, GR // 2)

            group_hi(2, GR - 1)
            copy_logits(1, LT1)
            act.wait_ge(s_route, 2)
            nc.scalar.activation(logits[:], tbank[0][:, 0:NT * E1].rearrange("p (t e) -> p t e", t=NT), ACT.Exp,
                                 scale=-1.0).then_inc(s_rexp, 1)
            for n in range(GR * EM):
                act.wait_ge(s_gu, 2 * n + 2)
                if n >= 2:
                    act.wait_ge(s_gated, n - 1)
                nc.scalar.activation(silu[:, n % 2], gate_banks[n % 2], ACT.Silu).then_inc(s_silu, 1)
                act.wait_ge(s_gated, n + 1)
                if n >= 3:
                    act.wait_ge(s_dn1h, 2 * n - 4)
                nc.scalar.copy(gs["h"][:, n % 3], gated[:, n % 2]).then_inc(s_ghi, 1)
                g, e = divmod(n, EM)
                if e < NC:
                    i = NC * g + e
                    act.wait_ge(s_conv, i + 1)
                    if i >= 2:
                        act.wait_ge(s_convt, i - 1)
                    nc.scalar.activation(convT[:, i % 2], ps[:, 7, :], ACT.Identity, bias=cb[:, e:e + 1]).then_inc(s_convc, 1)

        @block.vector
        def _(dve):
            dve.sem_inc(s_jobfree, 2)
            dve.sem_inc(s_mxfree, 2)
            dve.sem_inc(s_exp, 2)
            dve.sem_inc(s_pv, RING)
            dve.sem_inc(s_pvc, 1)
            dve.sem_inc(s_norm, 2)
            for h in range(2):
                nc.vector.memset(KB[h][HD:HD + 1, :].bitcast(F32), 1.0).then_inc(s_const, 1)
            dve.wait_ge(s_in, 16 * 6)
            dve.wait_ge(s_const, 8)
            normalise(dve, C, C, 0, B, s_lnc)

            def first_sums(g):
                dve.wait_ge(s_x[g], 16)
                ln_sums(dve, X, 4 * g, 4)

            def second_sums(g):
                ln_apply(dve, X, Y, 4 * g, 4)
                ln_sums(dve, Y, 4 * g, 4)

            def second_apply(g):
                ln_apply(dve, Y, Y, 4 * g, 4, s_ln)

            def rest_qk(j, cast, bk):
                dve.wait_ge(s_cast, cast)
                which, cols = (("q", slice(0, HALF)), ("q", slice(HALF, T)), ("k", slice(0, HALF)),
                               ("k", slice(HALF, T)), ("k", slice(T, NK)))[j]
                part = Q if which == "q" else K
                n = cols.stop - cols.start
                nc.vector.tensor_tensor(part["l"][:, cols], bk[:, 0:n], part["h"][:, cols].bitcast(F32),
                                        ALU.subtract).then_inc(s_jobfree, 1)

            for step in (first_sums, second_sums, second_apply):
                for g in range(2):
                    step(g)
            for k, (b, c, h) in enumerate(LATJOBS):
                if k == 4:
                    first_sums(2)
                    first_sums(3)
                if k in (5, 6):
                    second_sums(k - 3)
                if k in (7, 8):
                    second_apply(k - 5)
                dve.wait_ge(s_lat_full, k + 1)
                dve.wait_ge(s_lat_hi, k + 1)
                if k >= 2:
                    dve.wait_ge(s_lat_lo, k - 1)
                n = HALF if h < 2 else SP
                w = 2 if h < 2 else 0
                nc.vector.tensor_scalar(latf[:, k % 2, 0:n], shared[k % 2][:, 0:n], lnp[:, w, c:c + 1],
                                        lnp[:, w + 1, c:c + 1], ALU.mult, ALU.add).then_inc(s_lat_f, 1)
                if k == WQK0_AT:
                    dve.wait_ge(s_wqk, 1)
                    nc.vector.tensor_tensor(flat(wqk["l"]), flat(wqk_raw), flat(wqk["h"]).bitcast(F32),
                                            ALU.subtract).then_inc(s_wqk, 1)
                if k == BOUND_AT:
                    dve.wait_ge(s_wv_raw, 16)
                    nc.vector.tensor_reduce(bounds[:, 0:1], lnp[:].rearrange("p a c -> p (a c)"), AX.X, ALU.max,
                                            apply_absolute_value=True)
                    nc.vector.tensor_reduce(bounds[:, 1:2], flat(wv_raw), AX.X, ALU.max,
                                            apply_absolute_value=True).then_inc(s_bounds, 1)
                if k >= QK0_AT:
                    rest_qk(k - QK0_AT, k - QK0_AT + 1, first_qk_bank(k - QK0_AT))
            dve.wait_ge(s_wvh, 2)
            nc.vector.tensor_tensor(wv["l"][:, 1], wv_raw[:, 1], wv["h"][:, 1].bitcast(F32), ALU.subtract).then_inc(s_wv, 1)
            for j in range(len(LATJOBS) - QK0_AT, 5):
                rest_qk(j, j + 1, first_qk_bank(j))
            dve.wait_ge(s_bound, 1)
            link(dve, nc.vector.tensor_tensor(vs[:, 2:3], bound[:, 0:1], bound[:, 1:2], ALU.mult))
            link(dve, nc.vector.tensor_scalar(vs[:, 2:3], vs[:, 2:3], D * (D ** 0.5 + 1) * 1.1, 1e-30, ALU.mult, ALU.max))
            link(dve, nc.vector.tensor_scalar(vs[:, 3:4].bitcast(U32), vs[:, 2:3].bitcast(U32), 0x7F800000, None,
                                              ALU.bitwise_and))
            link(dve, nc.vector.reciprocal(vs[:, 0:1], vs[:, 3:4]))
            nc.vector.tensor_scalar(vs[:, 0:1], vs[:, 0:1], 16384.0, None, ALU.mult).then_inc(s_vs, 1)
            nc.vector.tensor_scalar(vs[:, 1:2], vs[:, 3:4], 1.0 / 16384.0, None, ALU.mult)

            def max_tile(t, n):
                for a in range(2):
                    dve.wait_ge(s_mx, 2 * n + a + 1)
                    r = nc.vector.reduce_max(mxs[:, a, t:t + 1], max_banks[:, a * HALF:a * HALF + HALF], AX.X)
                    if a == 0:
                        r.then_inc(s_mxfree, 1)
                if t % 4 == 3:
                    r = nc.vector.reduce_max(mxs[:, 2, t - 3:t + 1],
                                             small_bank[:, 0:4 * SP].rearrange("p (t s) -> p t s", t=4), AX.X)
                r.then_inc(s_mxfree, 1)

            def max_join(n):
                dve.wait_ge(s_mxfree, 2 * n + 2)
                nc.vector.tensor_reduce(maxs[:], mxs[:].rearrange("p a t -> p t a"), AX.X, ALU.max).then_inc(s_max, 1)

            def max_rows(h, k):
                dve.wait_ge(s_maxT, k + 1)
                nc.vector.tensor_scalar(maxT[h][:], small_bank[0:TB, 0:P], -1.0, None, ALU.mult).then_inc(s_maxrow, 1)

            def values(b, job, cast):
                for j in range(VJOBS):
                    kt, half = divmod(j, 2)
                    m = P if kt < TB else S
                    dve.wait_ge(s_cast, cast + j + 1)
                    heads = slice(PAIRS * half, PAIRS * half + PAIRS)
                    nc.vector.scalar_tensor_tensor(out=V["l"][0:m, kt, heads, 0:HD],
                                                   in0=shared[(job + j) % 2][0:m].rearrange("p (h d) -> p h d", d=HD),
                                                   scalar=vs[0:m, 0:1], in1=V["h"][0:m, kt, heads, 0:HD],
                                                   op0=ALU.mult, op1=ALU.subtract).then_inc(s_jobfree, 1)
                    if b == 0 and half == 0 and kt < TB:
                        max_tile(kt, kt)
                    if b == 0 and j == 2 * TB - 2:
                        max_join(TB)
                    if b == 0 and j == MAX0_T:
                        max_rows(0, 0)

            link(dve, nc.vector.memset(AT[:], 0.0))
            values(0, 5, 5)

            def unit_done(g, u):
                if u == 3:
                    dve.wait_ge(s_pv, STEPS * g + KT * (u + 1) + RING)
                    nc.vector.tensor_copy(PVS[:, u % 2], pv_bank).then_inc(s_pvc, 1)
                dve.wait_ge(s_pvc, 4 * g + u + 1 + 1)
                dve.wait_ge(s_norm, 4 * g + u + 2)
                nc.vector.reciprocal(rsum[:], PVS[:, u % 2, :, HD]).then_inc(s_rec, 1)
                dve.wait_ge(s_rec, 4 * g + u + 1)
                h, half = u // 2, u % 2
                nc.vector.scalar_tensor_tensor(out=AT[:, 4 * half:4 * half + 4, HD * h:HD * h + HD],
                                               in0=PVS[:, u % 2, :, 0:HD], scalar=vs[:, 1:2],
                                               in1=rsum[:].unsqueeze(2).to_broadcast([P, 4, HD]),
                                               op0=ALU.mult, op1=ALU.mult).then_inc(s_norm, 1)

            def att_lo(cast, j, bk):
                dve.wait_ge(s_cast, cast + j + 1)
                nc.vector.tensor_tensor(ATT["l"][:, HALF * j:HALF * j + HALF], bk,
                                        ATT["h"][:, HALF * j:HALF * j + HALF].bitcast(F32), ALU.subtract) \
                    .then_inc(s_jobfree, 1)

            def add_out(b, job, j, bk, more=0):
                dve.wait_ge(s_job, job + 2 + j + 1)
                xt = X[:, TB * b + 2 * j:TB * b + 2 * j + 2, :]
                nc.vector.tensor_tensor(xt, xt, bk.rearrange("p (t d) -> p t d", t=2), ALU.add) \
                    .then_inc(s_jobfree, 1)

            def turn(b, i, g, nb):
                for s in range(STEPS):
                    if s % KT == 1 and s > 1:
                        unit_done(g, s // KT - 1)
                    if on_vector(s + AHEAD - 1) and s + AHEAD - 1 < STEPS:
                        r = s + AHEAD - 1
                        m = P if r % KT < TB else S
                        dve.wait_ge(s_exp, STEPS * g + r + 1 + 2)
                        nc.vector.tensor_tensor(PR[0:m, r % RING, :], PT[0:m, r % RING, :], upper(r)[0:m],
                                                ALU.subtract).then_inc(s_rem_dve, 1)
                    if A_AT < s <= A_AT + 2:
                        att_lo(casts_before(b, i), s - 1 - A_AT, bank(s - 1 - A_AT))
                    if WO_AT < s <= WO_AT + 4:
                        add_out(b, jobs_before(b, i), s - 1 - WO_AT, bank(2 + s - 1 - WO_AT))
                    if M1_AT <= s < M1_AT + TB:
                        max_tile(s - M1_AT, 16 * g + 8 + s - M1_AT)
                    if s == M1_MAX:
                        max_join(16 * g + 16)
                    if s == M1_T:
                        max_rows(1, 2 * g + 1)
                    if nb is not None:
                        if QK_AT < s <= QK_AT + 5:
                            j = s - 1 - QK_AT
                            if j == 0:
                                dve.wait_ge(s_stack[1], 96 * g + 96)
                            rest_qk(j, casts_before(b, i) + 2 + j + 1, bank(AWJOBS + j))
                        if M0_AT <= s < M0_AT + TB:
                            max_tile(s - M0_AT, 16 * g + 16 + s - M0_AT)
                        if s == M0_MAX:
                            max_join(16 * g + 24)
                        if s == M0_T:
                            max_rows(0, 2 * g + 2)
                    if isinstance(i, int) and b + 1 == B and s in EARLY_LN:
                        normalise(dve, X, Y, 4 * EARLY_LN[s], 4, s_xn)
                unit_done(g, 3)
                if nb is not None:
                    dve.sem_inc(s_jobfree, 1)

            def next_batch(b):
                if b > 0:
                    link(dve, nc.vector.memset(AT[:], 0.0))
                    values(b, jobs_before(b, 0) - VJOBS, casts_before(b, 0) - VJOBS)

            def flush(b, job, cast):
                for j in range(2):
                    att_lo(cast, j, shared[(job + j) % 2])
                for j in range(4):
                    add_out(b, job, j, shared[(job + 2 + j) % 2])

            turns(dve, turn, next_batch, flush)
            for se, v in ((s_hf, 2), (s_hlo, 2), (s_down, 4), (s_accfree, 2)):
                dve.sem_inc(se, v)

            def group_lo(z, g):
                for k in (2 * g, 2 * g + 1):
                    c, b, h = TJOBS[k]
                    dve.wait_ge(s_thi, XJ * z + k + 1)
                    cols = slice(PAD + HALF * h, PAD + HALF * h + HALF)
                    nc.vector.tensor_tensor(XT["l"][:, c, b, cols], t_banks(z, g)[k % 2], XT["h"][:, c, b, cols].bitcast(F32),
                                            ALU.subtract).then_inc(s_tfree, 1)

            def over_experts(v):
                return v.unsqueeze(2).to_broadcast([P, NT, E0])

            def over_tokens(v):
                return v.unsqueeze(1).to_broadcast([P, NT, E0])

            def top_two(src):
                for t in range(NT):
                    ins = nc.vector.max(top[:, t, :], src[:, t, :])
                link(dve, ins)
                for t in range(NT):
                    ins = nc.vector.max_index(topi[:, t, :], top[:, t, :], src[:, t, :])
                link(dve, ins)
                link(dve, nc.vector.tensor_copy(topf[:], topi[:, :, 0:2]))
                for k in range(2):
                    ins = nc.vector.tensor_tensor(oh[:, k], over_tokens(iota8[:]), over_experts(topf[:, :, k]), ALU.is_equal)
                link(dve, ins)

            dve.wait_ge(s_jobfree, ATT0_JOBS + 2)
            for g in range(GR // 2):
                group_lo(0, g)
                normalise(dve, X, Y, 4 * (g + GR // 2), 4, s_xn)
            for g in range(GR // 2, GR):
                group_lo(0, g)
            dve.wait_ge(s_in1, 16 * 4)
            nc.vector.tensor_copy(wrs["h"][:], wr_raw[:]).then_inc(s_wr, 1)
            dve.wait_ge(s_wr, 1)
            nc.vector.tensor_tensor(wrs["l"][:], wr_raw[:], wrs["h"][:].bitcast(F32), ALU.subtract).then_inc(s_wr, 1)
            dve.wait_ge(s_route, 1)
            dve.wait_ge(s_const, 11)
            router = tbank[0][:, 0:NT * E0].rearrange("p (t e) -> p t e", t=NT)
            link(dve, nc.vector.tensor_tensor(logits[:], router, over_tokens(rb[:, 0, :]), ALU.add))
            top_two(logits)
            nc.vector.tensor_tensor(rw[:, 0, :], top[:, :, 1], top[:, :, 0], ALU.subtract).then_inc(s_rexp_in, 1)
            dve.wait_ge(s_rexp, 1)
            link(dve, nc.vector.tensor_scalar(rw[:, 2, :], rw[:, 1, :], 1.0, None, ALU.add))
            link(dve, nc.vector.reciprocal(rw[:, 2, :], rw[:, 2, :]))
            link(dve, nc.vector.tensor_tensor(rw[:, 3, :], rw[:, 1, :], rw[:, 2, :], ALU.mult))
            for k in range(2):
                ins = nc.vector.tensor_tensor(oh[:, k], oh[:, k], over_experts(rw[:, 2 + k, :]), ALU.mult)
            link(dve, ins)
            nc.vector.tensor_tensor(R[:], oh[:, 0], oh[:, 1], ALU.add).then_inc(s_R, 1)
            def hidden(e, k, u):
                n = UNITS * e + u
                dve.wait_ge(s_hhi, n + 1)
                dve.wait_ge(s_hlo, n + 1)
                nc.vector.tensor_scalar(hf[:, u % 2], hidden_banks[u % 2], b1e[:, k, u % FC:u % FC + 1], 0.0,
                                        ALU.add, ALU.max).then_inc(s_hf, 1)

            def routed_b2(j):
                dve.wait_ge(s_bt, j + 1)
                if j < 4:
                    nc.vector.tensor_copy(RT[:, 4 * j:4 * j + 4, :],
                                          tbank[j % 2][0:E0].rearrange("p (t q) -> p t q", t=4)).then_inc(s_RT, 1)
                else:
                    yt = Y[:, 2 * (j - 4):2 * (j - 4) + 2, :]
                    nc.vector.tensor_tensor(yt, yt, tbank[j % 2].rearrange("p (t d) -> p t d", t=2), ALU.add) \
                        .then_inc(s_RT, 1)

            def finish_group(g, part):
                ys, xs = Y[:, 4 * g:4 * g + 4, :], X[:, 4 * g:4 * g + 4, :]
                if part == 0:
                    dve.wait_ge(s_accfree, GR * (E0 - 1) + g + 1 + 2)
                    ln_sums(dve, Y, 4 * g, 4)
                if part == 2:
                    ln_apply(dve, Y, Y, 4 * g, 4)
                if part == 3:
                    link(dve, nc.vector.tensor_tensor(ys, ys, gbs[:, 0:1, :].to_broadcast([P, 4, D]), ALU.mult))
                    link(dve, nc.vector.tensor_tensor(ys, ys, gbs[:, 1:2, :].to_broadcast([P, 4, D]), ALU.add))
                if part == 4:
                    link(dve, nc.vector.tensor_tensor(xs, xs, ys, ALU.add))
                    ln_sums(dve, X, 4 * g, 4)
                if part == 6:
                    ln_apply(dve, X, Y, 4 * g, 4, s_xn)

            def rest_job(k, dst, src, hi, bias=None):
                dve.wait_ge(s_a1h, k + 1)
                ins = nc.vector.tensor_tensor(dst, src, hi.bitcast(F32), ALU.subtract) if bias is None else \
                    nc.vector.scalar_tensor_tensor(out=dst, in0=src, scalar=bias, in1=hi.bitcast(F32),
                                                   op0=ALU.add, op1=ALU.subtract)
                ins.then_inc(s_a1e, 1)

            def rest_kv(j):
                c = j % NC
                if j < K_JOB:
                    rest_job(j, CT["l"][:, c], tbank[j % 2][:, 0:B * SP].rearrange("p (b s) -> p b s", b=B),
                             CT["h"][:, c])
                elif j < V_JOB:
                    rest_job(j, K1["l"][:, c], tbank[j % 2][:, 0:B * SP], K1["h"][:, c], bqk[:, 1, c:c + 1])
                else:
                    dve.wait_ge(s_a1, j + 1)
                    nc.vector.tensor_copy(V1f[0:S, j - V_JOB], tbank[j % 2][0:S, 0:D].rearrange("p (h d) -> p h d", h=H1)) \
                        .then_inc(s_a1e, 1)

            def constants1():
                nc.vector.memset(ones_row[:].bitcast(F32), 1.0).then_inc(s_ones, 1)
                nc.vector.tensor_copy(ident_r[:], ident[:]).then_inc(s_ones, 1)
                dve.wait_ge(s_in2, 16 * 4)
                nc.vector.tensor_copy(bvo["h"][:], bvo_raw[:]).then_inc(s_ones, 1)
                dve.wait_ge(s_ones, 3)
                nc.vector.tensor_tensor(bvo["l"][:], bvo_raw[:], bvo["h"][:].bitcast(F32), ALU.subtract).then_inc(s_ones, 1)

            def expert(e, k, i, more):
                routing = isinstance(e, int) and more
                for u in range(UNITS):
                    if u + UP_AHEAD < UNITS:
                        hidden(e, k, u + UP_AHEAD)
                    elif more:
                        hidden(e + 1, 1 - k, u + UP_AHEAD - UNITS)
                    if not more and u in TAIL_T:
                        group_lo(1, TAIL_T[u])
                    if not more and u == 0:
                        constants1()
                    if not more and u in KV_AT:
                        rest_kv(KV_AT[u])
                    if routing and u < B2_UNITS:
                        routed_b2(u)
                    if not more and u >= FC:
                        finish_group(u // FC - 1, u % FC)
                    if u % FC == FC - 1:
                        if routing:
                            dve.wait_ge(s_RT, 8 if u < B2_UNITS else B2_UNITS)
                        add_group(e, u // FC)

            def add_group(e, g):
                dve.wait_ge(s_down, UNITS * e + FC * (g + 1) + 4)
                for t in range(4):
                    yt = Y[:, 4 * g + t, :]
                    ins = nc.vector.scalar_tensor_tensor(out=yt, in0=acc_banks[g % 2][:, t * D:t * D + D],
                                                         scalar=R[:, 4 * g + t, bass.ds(e, 1)], in1=yt,
                                                         op0=ALU.mult, op1=ALU.add)
                ins.then_inc(s_accfree, 1)

            for u in range(UP_AHEAD):
                hidden(0, 0, u)
            experts(dve, expert)
            def max1(i):
                b, t, c = i // (TB * NC), i // NC % TB, i % NC
                dve.wait_ge(s_mx1, i + 1)
                nc.vector.reduce_max(m1[:, b, t, HC * c:HC * c + HC].rearrange("p (a h) -> p a h", a=2),
                                     max1_banks(i).rearrange("p a (h s) -> p a h s", s=SP), AX.X).then_inc(s_m8, 1)

            def max1_rows(b, half):
                j = NM_JOB + 2 * b + half
                dve.wait_ge(s_a1, j + 1)
                nc.vector.tensor_scalar(NM[:, b, HALF * half:HALF * half + HALF], tbank[j % 2][0:H1], -1.0, None,
                                        ALU.mult).then_inc(s_a1e, 1)

            def norm1(n):
                b, h = divmod(n, H1)
                dve.wait_ge(s_pv1, 2 * n + 2)
                nc.vector.reciprocal(rs8[:], pv1[n % 2][:, :, D1]).then_inc(s_rs1, 1)
                dve.wait_ge(s_rs1, n + 1)
                nc.vector.scalar_tensor_tensor(out=Y[:, TB * b:TB * b + TB, D1 * h:D1 * h + D1],
                                               in0=pv1[n % 2][:, :, 0:D1], scalar=vs1[:, 1:2],
                                               in1=rs8[:].unsqueeze(2).to_broadcast([P, TB, D1]),
                                               op0=ALU.mult, op1=ALU.mult).then_inc(s_nm1, 1)

            def rest_out(g):
                for c in range(NC):
                    rest_job(12 + NC * g + c, A1T["l"][:, c, :], tbank[(OUT_JOB + 4 * g + c) % 2], A1T["h"][:, c, :])

            def add_out1(g, i):
                j = OUT_JOB + 4 * g + 2 + i
                dve.wait_ge(s_a1, j + 1)
                xt = X[:, 4 * g + 2 * i:4 * g + 2 * i + 2, :]
                nc.vector.tensor_tensor(xt, xt, tbank[j % 2].rearrange("p (t d) -> p t d", t=2), ALU.add) \
                    .then_inc(s_a1e, 1)

            def rest_q(i):
                b, c, h = QJOBS[i]
                cols = slice(HALF * h, HALF * h + HALF)
                rest_job(4 + i, Q1["l"][:, c, b, cols], tbank[(Q_JOB + i) % 2], Q1["h"][:, c, b, cols],
                         bqk[:, 0, c:c + 1])

            def key_blocks(b):
                for c in range(NC):
                    keys = K1["h"][:, c, b * SP:b * SP + SP].bitcast(F32)
                    nc.vector.tensor_tensor(KD["h"][:, b, c], keys.unsqueeze(1).to_broadcast([P, HC, SP]),
                                            hmask[:].unsqueeze(2).to_broadcast([P, HC, SP]), ALU.mult).then_inc(s_kd, 1)

            finish_group(GR - 1, 0)
            for i in range(2):
                rest_q(i)
            finish_group(GR - 1, 2)
            for i in range(2, 4):
                rest_q(i)
            finish_group(GR - 1, 3)
            finish_group(GR - 1, 4)
            dve.wait_ge(s_const, CONST1 + 9)
            key_blocks(0)
            nc.vector.tensor_copy(sel[:], ident[0:H1, 0:H1].unsqueeze(2).to_broadcast([H1, H1, SP])).then_inc(s_ones, 1)
            nc.vector.tensor_copy(mask[:], mask_f[:]).then_inc(s_ones, 1)
            nc.vector.tensor_copy(mask4[:], mask_f[:, 0:1, 0:SP].to_broadcast([P, HC // 2, SP])).then_inc(s_ones, 1)
            finish_group(GR - 1, 6)
            group_lo(1, GR // 2)
            dve.wait_ge(s_a1e, V_JOB + B)
            nc.vector.tensor_reduce(vb[0:S, 0:1], V1f[0:S].rearrange("p b h d -> p (b h d)"), AX.X, ALU.max,
                                    apply_absolute_value=True).then_inc(s_vb, 1)
            for i in range(TB * NC):
                max1(i)
                if i == T3_AFTER:
                    group_lo(1, GR - 1)
                if i in Q_AFTER:
                    rest_q(Q_AFTER[i])
            for half in range(2):
                max1_rows(0, half)
            key_blocks(1)
            dve.wait_ge(s_vbr, 1)
            link(dve, nc.vector.tensor_scalar(vs1[:, 2:3], vb[:, 1:2], 1e-30, None, ALU.max))
            link(dve, nc.vector.tensor_scalar(vs1[:, 2:3].bitcast(U32), vs1[:, 2:3].bitcast(U32), 0x7F800000, None,
                                              ALU.bitwise_and))
            link(dve, nc.vector.reciprocal(vs1[:, 0:1], vs1[:, 2:3]))
            link(dve, nc.vector.tensor_scalar(vs1[:, 0:1], vs1[:, 0:1], 16384.0, None, ALU.mult))
            nc.vector.tensor_scalar(vs1[:, 1:2], vs1[:, 2:3], 1.0 / 16384.0, None, ALU.mult)
            for b in range(B):
                ins = nc.vector.tensor_scalar(V1["h"][0:S, b, :, 0:D1], V1f[0:S, b], vs1[0:S, 0:1], None, ALU.mult)
            link(dve, ins)
            for b in range(B):
                nc.vector.scalar_tensor_tensor(out=V1["l"][0:S, b, :, 0:D1], in0=V1f[0:S, b], scalar=vs1[0:S, 0:1],
                                               in1=V1["h"][0:S, b, :, 0:D1], op0=ALU.mult, op1=ALU.subtract) \
                    .then_inc(s_v1, 1)
            for k in range(K1S):
                if k % 2 == 0 and k > 0:
                    norm1(k // 2 - 1)
                r = k + 1
                if r % 2 == 1 and r < K1S:
                    dve.wait_ge(s_ex1, r + 1)
                    nc.vector.tensor_tensor(PR1[0:S, r % RING1, :], PT1[0:S, r % RING1, :], upper1(r)[0:S],
                                            ALU.subtract).then_inc(s_r1v, 1)
                if k < TB * NC:
                    max1(TB * NC + k)
                if k in NM_AT:
                    max1_rows(1, k - NM_AT[0])
                if k - 1 in OUT_T:
                    rest_out(OUT_T[k - 1])
                for i in range(2):
                    if k - 1 - i in OUT_P:
                        add_out1(OUT_P[k - 1 - i], i)
                if k in OUT_LN:
                    g = OUT_LN[k]
                    dve.wait_ge(s_a1e, OUT_JOB + 4 * g + 4)
                    ln_sums(dve, X, 4 * g, 4)
                if k - 3 in OUT_LN:
                    ln_apply(dve, X, Y, 4 * OUT_LN[k - 3], 4, s_xn)
                if k - 1 in OUT_XT:
                    group_lo(2, OUT_XT[k - 1])
            norm1(K1S // 2 - 1)
            for g in range(GR // 2, GR):
                rest_out(g)
                for i in range(2):
                    add_out1(g, i)
                dve.wait_ge(s_a1e, OUT_JOB + 4 * g + 4)
                normalise(dve, X, Y, 4 * g, 4, s_xn)
            group_lo(2, GR // 2)
            group_lo(2, GR - 1)

            dve.wait_ge(s_in3, 16 * 4)
            link(dve, nc.vector.tensor_copy(cwh[:], cw[:, 0, :]))
            link(dve, nc.vector.tensor_tensor(cw[:, 1, :], cw[:, 0, :], cwh[:].bitcast(F32), ALU.subtract))
            for k in range(TAPS * NC):
                for i, u in enumerate("hl"):
                    src = cwh[:, k:k + 1].bitcast(F32) if u == "h" else cw[:, 1, k:k + 1]
                    ins = nc.vector.tensor_scalar(diag[u][:, k, :], ident[:], src, None, ALU.mult)
            ins.then_inc(s_w3d, 1)
            dve.wait_ge(s_rexp, 2)
            link(dve, nc.vector.tensor_scalar(logits[:], logits[:], 1.0, None, ALU.add))
            link(dve, nc.vector.reciprocal(logits[:], logits[:]))
            link(dve, nc.vector.tensor_tensor(R[:], logits[:], over_tokens(rb[:, 1, :]), ALU.add))
            top_two(R)
            link(dve, nc.vector.tensor_tensor(oh[:, 0], oh[:, 0], oh[:, 1], ALU.add))
            link(dve, nc.vector.tensor_tensor(oh[:, 0], oh[:, 0], logits[:], ALU.mult))
            link(dve, nc.vector.reduce_sum(rw[:, 0, :], oh[:, 0], AX.X))
            link(dve, nc.vector.tensor_scalar(rw[:, 0, :], rw[:, 0, :], 1e-9, None, ALU.add))
            link(dve, nc.vector.reciprocal(rw[:, 0, :], rw[:, 0, :]))
            link(dve, nc.vector.tensor_tensor(R[:], oh[:, 0], over_experts(rw[:, 0, :]), ALU.mult))
            link(dve, nc.vector.tensor_tensor(rw[:, 1, :], R[:, :, EM], R[:, :, EM + 2], ALU.add))

            def own_terms(g):
                ys, xs = Y[:, 4 * g:4 * g + 4, :], X[:, 4 * g:4 * g + 4, :]
                link(dve, nc.vector.tensor_scalar(reluY[:], ys, 0.0, None, ALU.max))
                for t in range(4):
                    ins = nc.vector.scalar_tensor_tensor(out=xs[:, t, :], in0=ys[:, t, :], scalar=rw[:, 1, 4 * g + t:4 * g + t + 1],
                                                         in1=xs[:, t, :], op0=ALU.mult, op1=ALU.add)
                link(dve, ins)
                for t in range(4):
                    ins = nc.vector.scalar_tensor_tensor(out=xs[:, t, :], in0=reluY[:, t, :],
                                                         scalar=R[:, 4 * g + t, E1 - 1:E1],
                                                         in1=xs[:, t, :], op0=ALU.mult, op1=ALU.add)
                link(dve, ins)

            def add_conv(i):
                g, c = divmod(i, NC)
                dve.wait_ge(s_convt, i + 1)
                xs = X[:, 4 * g:4 * g + 4, c * P:c * P + P]
                nc.vector.tensor_tensor(xs, xs, ps[:, 6, :].rearrange("p (t d) -> p t d", t=4), ALU.add) \
                    .then_inc(s_convfree, 1)
                dve.wait_ge(s_convfree, i + 1)

            def gate(n):
                dve.wait_ge(s_silu, n + 1)
                if n >= 2:
                    dve.wait_ge(s_glo, n - 1)
                nc.vector.tensor_tensor(gated[:, n % 2], silu[:, n % 2], up_banks[n % 2], ALU.mult).then_inc(s_gated, 1)

            def add1(n):
                g, e = divmod(n, EM)
                for t in range(4):
                    if t % 2 == 0:
                        dve.wait_ge(s_dn1h, 2 * n + t // 2 + 1)
                    xt = X[:, 4 * g + t, :]
                    ins = nc.vector.scalar_tensor_tensor(out=xt, in0=down_banks[t // 2][:, t % 2 * D:t % 2 * D + D],
                                                         scalar=R[:, 4 * g + t, e:e + 1], in1=xt, op0=ALU.mult, op1=ALU.add)
                    ins.then_inc(s_acc1, 1)
                dve.wait_ge(s_acc1, 4 * n + 4)

            for n in range(GR * EM):
                gate(n)
                if n % EM == 0:
                    own_terms(n // EM)
                if 1 <= n % EM <= NC:
                    add_conv(NC * (n // EM) + n % EM - 1)
                if n >= 1:
                    add1(n - 1)
            add1(GR * EM - 1)

        @block.tensor
        def _(pe):
            pe.wait_ge(s_const, 8)
            pe.wait_ge(s_lnc, 1)

            def product(o, pairs, **kw):
                n = len(pairs)
                for k, (l, r) in enumerate(pairs):
                    mm = nc.tensor.matmul(o, l, r, start=(k == 0), stop=(k == n - 1), **kw)
                return mm

            def project_qk(j, nb, job, bk):
                pe.wait_ge(s_jobfree, job + 1)
                cols = (slice(0, HALF), slice(HALF, T), slice(0, HALF), slice(HALF, T), slice(T, NK))[j]
                product(bk[:, 0:cols.stop - cols.start],
                        [(wqk[u][:, c, j // 2 if j < 4 else 1, :], lat[v][:, nb, c, cols])
                         for c in range(NC) for u, v in RANDL]).then_inc(s_job, 1)

            for k, (b, c, h) in enumerate(LATJOBS):
                if h < 2:
                    pe.wait_ge(s_ln, 2 * b + h + 1)
                if k >= 2:
                    pe.wait_ge(s_lat_f, k - 1)
                if h < 2:
                    for t in range(4):
                        mm = nc.tensor.transpose(shared[k % 2][:, t * P:t * P + P],
                                                 Y[:, b * TB + 4 * h + t, c * P:c * P + P], ident[:])
                else:
                    mm = nc.tensor.transpose(shared[k % 2][:, 0:SP], C[0:SP, b, c * P:c * P + P], ident[0:SP, 0:SP])
                mm.then_inc(s_lat_full, 1)
                if k == QK0_AT:
                    pe.wait_ge(s_lat_lo, NC * (B + 2))
                    pe.wait_ge(s_wqk, 2)
                if k >= QK0_AT:
                    project_qk(k - QK0_AT, 0, k - QK0_AT, first_qk_bank(k - QK0_AT))

            def max_part(h, t, a, n):
                pe.wait_ge(s_mxfree, 2 * n + a + 1)
                r = slice(HD * h, HD * h + HD)
                q = Q["h"][r, t * P:t * P + P]
                if a == 1:
                    nc.tensor.matmul(small_bank[:, t % 4 * SP:t % 4 * SP + SP], q, K["h"][r, T:NK],
                                     start=True, stop=True)
                nc.tensor.matmul(max_banks[:, a * HALF:a * HALF + HALF], q, K["h"][r, a * HALF:a * HALF + HALF],
                                 start=True, stop=True).then_inc(s_mx, 1)

            def max_tile(h, t, n):
                for a in range(2):
                    max_part(h, t, a, n)

            def max_turn(k):
                pe.wait_ge(s_max, k + 1)
                nc.tensor.transpose(small_bank[0:TB, 0:P], maxs[:], ident[:]).then_inc(s_maxT, 1)

            def values(b, job):
                for j in range(VJOBS):
                    kt, half = divmod(j, 2)
                    m = P if kt < TB else S
                    pe.wait_ge(s_jobfree, job + j + 1)
                    product(shared[(job + j) % 2][0:m],
                            [(lat[u][:, b, c, kt * P:kt * P + m], wv[v][:, c, HALF * half:HALF * half + HALF])
                             for c in range(NC) for u, v in RANDL]).then_inc(s_job, 1)
                    if b == 0 and half == 0 and kt < TB:
                        if kt == 0:
                            pe.wait_ge(s_jobfree, 5 + 2)
                        max_tile(0, kt, kt)
                    if b == 0 and j == MAX0_T:
                        max_turn(0)

            for j in range(len(LATJOBS) - QK0_AT, 5):
                project_qk(j, 0, j, first_qk_bank(j))
            pe.wait_ge(s_lat_lo, len(LATJOBS))
            pe.wait_ge(s_wv, 2)
            values(0, 5)

            def scores(g, s):
                h, half, kt = s // (2 * KT), s // KT % 2, s % KT
                m = P if kt < TB else S
                pe.wait_ge(s_exp, STEPS * g + s + 1)
                if s % (2 * KT) == 0:
                    pe.wait_ge(s_stack[h], 96 * g + 96)
                    pe.wait_ge(s_row[h], 16 * g + 16)
                o = score_banks[s % 2][0:m]
                q, k = slice(HALF * half, HALF * half + HALF), slice(kt * P, kt * P + m)
                nc.tensor.matmul(o, KA[h][:, k], QA[h][:, q], start=True, stop=False)
                nc.tensor.matmul(o, KB[h][0:HD + 1, k], QB[h][0:HD + 1, q], start=False, stop=True) \
                    .then_inc(s_score, 1)

            def attend(g, pair, s):
                h, kt = s // (2 * KT), s % KT
                m = P if kt < TB else S
                if on_vector(s):
                    pe.wait_ge(s_rem_dve, len(VECTOR_STEPS) * g + by_vector(s))
                else:
                    pe.wait_ge(s_rem_pool, (STEPS - len(VECTOR_STEPS)) * g + s + 1 - by_vector(s))
                if kt == 0:
                    pe.wait_ge(s_pvc, 4 * g + s // KT + 1)
                head = 2 * pair + h
                vh, vl = ((V[k][0:m, kt, head, :] if isinstance(head, int) else
                           V[k][0:m, kt, bass.ds(head, 1), :].squeeze(1)) for k in "hl")
                for q in range(4):
                    c = slice(q * P, q * P + P)
                    for k, (p, v) in enumerate(((upper(s)[0:m, c], vh), (upper(s)[0:m, c], vl),
                                                (PR[0:m, s % RING, c], vh), (PR[0:m, s % RING, c], vl))):
                        mm = nc.tensor.matmul(pv_bank[:, q, :], p, v, start=(kt == 0 and q == 0 and k == 0),
                                              stop=(kt == KT - 1 and k == 3), skip_group_check=True)
                mm.then_inc(s_pv, 1)

            def att_turn(job, j, bk):
                pe.wait_ge(s_jobfree, job + j + 1)
                for t in range(4):
                    mm = nc.tensor.transpose(bk[:, t * P:t * P + P], AT[:, 4 * j + t, :], ident[:])
                mm.then_inc(s_job, 1)

            def project_out(job, j, bk):
                if j % 2 == 0:
                    pe.wait_ge(s_jobfree, job + j // 2 + 1 + 2)
                pe.wait_ge(s_jobfree, job + 2 + j + 1)
                for t in range(2):
                    q = slice((2 * j + t) * P, (2 * j + t + 1) * P)
                    mm = product(bk[:, t * D:t * D + D], [(ATT[u][:, q], wo[v][:]) for u, v in RANDL])
                mm.then_inc(s_job, 1)

            def turn(b, i, g, nb):
                job = jobs_before(b, i)
                last = isinstance(i, int)
                for s in range(STEPS):
                    if s + AHEAD < STEPS:
                        scores(g, s + AHEAD)
                    elif not last:
                        scores(g + 1, s + AHEAD - STEPS)
                    if M1_AT <= s < M1_AT + TB:
                        if s == M1_AT:
                            pe.wait_ge(s_maxrow, 2 * g + 1)
                        max_part(1, s - M1_AT, 0, 16 * g + 8 + s - M1_AT)
                    if nb is not None and M0_AT <= s < M0_AT + TB:
                        if s == M0_AT:
                            pe.wait_ge(s_jobfree, job + AWJOBS + 5 + 2)
                            pe.wait_ge(s_maxrow, 2 * g + 2)
                        max_part(0, s - M0_AT, 0, 16 * g + 16 + s - M0_AT)
                    if A_AT <= s < A_AT + 2:
                        if s == A_AT:
                            pe.wait_ge(s_norm, 4 * g + 2)
                        att_turn(job, s - A_AT, bank(s - A_AT))
                    attend(g, i, s)
                    if WO_AT <= s < WO_AT + 4:
                        if s == WO_AT:
                            pe.wait_ge(s_wo, 2 * (g + b) + 2)
                        project_out(job, s - WO_AT, bank(2 + s - WO_AT))
                    if M1_AT <= s < M1_AT + TB:
                        max_part(1, s - M1_AT, 1, 16 * g + 8 + s - M1_AT)
                    if s == M1_T:
                        max_turn(2 * g + 1)
                    if nb is not None:
                        if QK_AT <= s < QK_AT + 5:
                            if s == QK_AT:
                                pe.wait_ge(s_wqk, 2 * g + 4)
                            j = AWJOBS + s - QK_AT
                            project_qk(s - QK_AT, nb, job + j, bank(j))
                        if M0_AT <= s < M0_AT + TB:
                            max_part(0, s - M0_AT, 1, 16 * g + 16 + s - M0_AT)
                        if s == M0_T:
                            max_turn(2 * g + 2)
                if nb is not None:
                    pe.sem_inc(s_job, 1)

            def next_batch(b):
                if b > 0:
                    values(b, jobs_before(b, 0) - VJOBS)
                for s in range(AHEAD):
                    scores(b * PAIRS, s)

            def flush(b, job, cast):
                pe.wait_ge(s_norm, 4 * PAIRS * (b + 1) + 2)
                for j in range(2):
                    att_turn(job, j, shared[(job + j) % 2])
                pe.wait_ge(s_wo, 2 * (PAIRS + 1) * (b + 1))
                for j in range(4):
                    project_out(job, j, shared[(job + 2 + j) % 2])

            turns(pe, turn, next_batch, flush)

            def transposes(z, g):
                pe.wait_ge(s_xn, GR * z + g + 1)
                for k in (2 * g, 2 * g + 1):
                    c, b, h = TJOBS[k]
                    if k >= 2:
                        pe.wait_ge(s_tfree, XJ * z + k - 1)
                    if z == 1 and g >= GR // 2:
                        pe.wait_ge(s_accfree, GR * E0 + 2)
                    elif k < 2 and z == 0:
                        pe.wait_ge(s_jobfree, ATT0_JOBS + 2)
                    elif k < 2 and z == 1:
                        pe.wait_ge(s_a1e, V_JOB + B)
                    for t in range(4):
                        mm = nc.tensor.transpose(t_banks(z, g)[k % 2][:, t * P:t * P + P],
                                                 Y[:, b * TB + 4 * h + t, c * P:c * P + P], ident[:])
                    mm.then_inc(s_tj, 1)

            def group(u, c, g):
                return XT[u][:, c, g // 2, PAD + HALF * (g % 2):PAD + HALF * (g % 2) + HALF]

            def route(z, layer, LT):
                pe.wait_ge(s_tfree, XJ * z + XJ)
                pe.wait_ge(s_wr, 2)
                for g in range(GR):
                    if g >= 2:
                        pe.wait_ge(s_lt, GR * layer + g - 1)
                    product(tbank[g % 2][0:E0], [(wrs[v][:, layer, c, :], group(u, c, g))
                                                 for c in range(NC) for u, v in RANDL]).then_inc(s_rt, 1)
                pe.wait_ge(s_lt, GR * layer + GR)
                for t in range(NT):
                    mm = nc.tensor.transpose(tbank[0][:, t * E0:t * E0 + E0], LT[:, t // 4, t % 4 * P:t % 4 * P + P],
                                             ident[0:E0, 0:E0])
                mm.then_inc(s_route, 1)

            for g in range(GR):
                transposes(0, g)
            route(0, 0, LT0)

            def routed_b2(j):
                if j == 0:
                    pe.wait_ge(s_R, 1)
                else:
                    pe.wait_ge(s_RT, 4 if j == 4 else max(1, j - 1))
                if j < 4:
                    for t in range(4):
                        mm = nc.tensor.transpose(tbank[j % 2][0:E0, t * P:t * P + P], R[:, 4 * j + t, :], ident[:])
                else:
                    for t in range(2):
                        mm = nc.tensor.matmul(tbank[j % 2][:, t * D:t * D + D], RT[:, 2 * (j - 4) + t, :], b2s[:],
                                              start=True, stop=True)
                mm.then_inc(s_bt, 1)

            def up(e, k, u):
                g, f = divmod(u, FC)
                pe.wait_ge(s_hf, UNITS * e + u + 1)
                if g == 0:
                    pe.wait_ge(s_w1, 2 * FC * e + 2 * f + 2)
                product(hidden_banks[u % 2], [(w1s[a][:, k, f, c * P:c * P + P], group(b, c, g))
                                              for c in range(NC) for a, b in RANDL]).then_inc(s_up, 1)

            def down(e, k, u):
                g, f = divmod(u, FC)
                if f == 0:
                    pe.wait_ge(s_accfree, GR * e + g + 1)
                if g == 0:
                    pe.wait_ge(s_w2, 2 * FC * e + 2 * f + 2)
                pe.wait_ge(s_hlo, UNITS * e + u + 1 + 2)
                for t in range(4):
                    o = acc_banks[g % 2][:, t * D:t * D + D]
                    for j, (a, b) in enumerate(RANDL):
                        mm = nc.tensor.matmul(o, hs[a][:, u % 4, t * P:t * P + P], w2s[b][:, k, f, :],
                                              start=(f == 0 and j == 0 and t % 2 == 0), stop=(f == FC - 1 and j == 2),
                                              skip_group_check=True)
                mm.then_inc(s_down, 1)

            def job(j):
                if j >= 2:
                    pe.wait_ge(s_a1e, j - 1)
                return tbank[j % 2]

            def project_kv(j):
                if j == 0:
                    pe.wait_ge(s_RT, B2_UNITS)
                    pe.wait_ge(s_in2, 16 * 4)
                c = j % NC
                bk = job(j)
                if j < K_JOB:
                    for b in range(B):
                        mm = nc.tensor.transpose(bk[:, b * SP:b * SP + SP], C1[0:SP, b, c * P:c * P + P], ident[0:SP, 0:SP])
                elif j < V_JOB:
                    pe.wait_ge(s_a1e, K_JOB)
                    pe.wait_ge(s_wa, 1)
                    mm = product(bk[:, 0:B * SP],
                                 [(wa[u][:, 1, i, c * P:c * P + P], CT[v][:, i].rearrange("p b s -> p (b s)"))
                                  for i in range(NC) for u, v in RANDL])
                else:
                    pe.wait_ge(s_wa, 2)
                    pe.wait_ge(s_ones, 4)
                    mm = product(bk[0:S, 0:D],
                                 [(CT[u][:, i, j - V_JOB, 0:S], wa[v][:, 2, i, :]) for i in range(NC) for u, v in RANDL]
                                 + [(ones_row[:, 0:S], bvo[u][:, 0, :]) for u in "hl"])
                mm.then_inc(s_a1, 1)

            def expert(e, k, i, more):
                for u in range(UNITS):
                    if u + UP_AHEAD < UNITS:
                        up(e, k, u + UP_AHEAD)
                    elif more:
                        up(e + 1, 1 - k, u + UP_AHEAD - UNITS)
                    if not more and u in TAIL_T:
                        transposes(1, TAIL_T[u])
                    if not more and u in KV_AT:
                        project_kv(KV_AT[u])
                    if isinstance(e, int) and more and u < B2_UNITS:
                        routed_b2(u)
                    down(e, k, u)

            for u in range(UP_AHEAD):
                up(0, 0, u)
            experts(pe, expert)

            def project_q(i):
                b, ic, h = QJOBS[i]
                product(job(Q_JOB + i), [(wa[u][:, 0, c, ic * P:ic * P + P], group(v, c, 2 * b + h))
                                         for c in range(NC) for u, v in RANDL]).then_inc(s_a1, 1)

            def max1(i):
                b, t, c = i // (TB * NC), i // NC % TB, i % NC
                if i < TB * NC and i >= 2:
                    pe.wait_ge(s_m8, i - 1)
                elif i >= TB * NC:
                    pe.wait_ge(s_m8, i)
                q = Q1["h"][:, c, b, t * P:t * P + P]
                for a in range(2):
                    o = max1_banks(i)[:, a]
                    keys = KD["h"][:, b, c, HC // 2 * a:HC // 2 * a + HC // 2].rearrange("p h s -> p (h s)")
                    mm = nc.tensor.matmul(o, q, keys, start=True, stop=(t > 0))
                    if t == 0:
                        mm = nc.tensor.matmul(o, ident_r[:], mask4[:].rearrange("p h s -> p (h s)"), start=False, stop=True)
                mm.then_inc(s_mx1, 1)

            def max1_rows(b, half):
                bk = job(NM_JOB + 2 * b + half)
                for t in range(4):
                    mm = nc.tensor.transpose(bk[0:H1, t * P:t * P + P], m1[:, b, 4 * half + t, :], ident[:])
                mm.then_inc(s_a1, 1)

            def scores1(k):
                n, a = divmod(k, 2)
                b, h = divmod(n, H1)
                c = h // HC
                if k >= 2:
                    pe.wait_ge(s_ex1, k - 1)
                o = score1[k % 2]
                q = slice(HALF * a, HALF * a + HALF)
                ops = [(KD[u][:, b, c, h % HC, 0:S], Q1[v][:, c, b, q]) for u, v in RANDL]
                ops.append((sel[:, h, 0:S], NM[:, b, q]))
                for i, (l, r) in enumerate(ops):
                    mm = nc.tensor.matmul(o, l, r, start=(i == 0), stop=(i == 3 and a == 1))
                if a == 0:
                    mm = nc.tensor.matmul(o[:, 0:P], ident_r[0:S, 0:S], mask[0:S, 1, :], start=False, stop=True)
                mm.then_inc(s_sc1, 1)

            def attend1(k):
                n, a = divmod(k, 2)
                b, h = divmod(n, H1)
                if a == 0 and n >= 2:
                    pe.wait_ge(s_nm1, n - 1)
                if k % 2 == 0:
                    pe.wait_ge(s_r1p, k // 2 + 1)
                else:
                    pe.wait_ge(s_r1v, k // 2 + 1)
                for t in range(4):
                    c = slice(t * P, t * P + P)
                    mm = product(pv1[n % 2][:, 4 * a + t, :],
                                 [(p[0:S, c], V1[v][0:S, b, h, :]) for p in (upper1(k), PR1[:, k % RING1, :]) for v in "hl"])
                mm.then_inc(s_pv1, 1)

            def out_turn(g):
                pe.wait_ge(s_nm1, H1 * (g // 2 + 1))
                for c in range(NC):
                    bk = job(OUT_JOB + 4 * g + c)
                    for t in range(4):
                        mm = nc.tensor.transpose(bk[:, t * P:t * P + P], Y[:, 4 * g + t, c * P:c * P + P], ident[:])
                    mm.then_inc(s_a1, 1)

            def project_out1(g, i):
                pe.wait_ge(s_wa, 4)
                pe.wait_ge(s_a1e, OUT_JOB + 4 * g + 2)
                bk = job(OUT_JOB + 4 * g + 2 + i)
                for t in range(2):
                    q = slice((2 * i + t) * P, (2 * i + t) * P + P)
                    mm = product(bk[:, t * D:t * D + D],
                                 [(A1T[u][:, c, q], wa[v][:, 3, c, :]) for c in range(NC) for u, v in RANDL]
                                 + [(ones_row[:], bvo[u][:, 1, :]) for u in "hl"])
                mm.then_inc(s_a1, 1)

            pe.wait_ge(s_wa, 3)
            pe.wait_ge(s_tfree, XJ + 4)
            for i in range(4):
                project_q(i)
            transposes(1, GR // 2)
            pe.wait_ge(s_a1e, Q_JOB + 4)
            pe.wait_ge(s_kd, NC)
            pe.wait_ge(s_ones, 7)
            for i in range(TB * NC):
                max1(i)
                if i == T3_AFTER:
                    transposes(1, GR - 1)
                if i in Q_AFTER:
                    pe.wait_ge(s_tfree, 2 * XJ)
                    project_q(Q_AFTER[i])
            pe.wait_ge(s_m8, TB * NC)
            for half in range(2):
                max1_rows(0, half)
            pe.wait_ge(s_a1e, NM_JOB + 2)
            pe.wait_ge(s_kd, B * NC)
            pe.wait_ge(s_kdl, B * NC)
            for k in range(AHEAD):
                scores1(k)
            pe.wait_ge(s_v1, B)
            for k in range(K1S):
                if k + AHEAD == K1S // 2:
                    pe.wait_ge(s_a1e, NM_JOB + 4)
                if k + AHEAD < K1S:
                    scores1(k + AHEAD)
                if k < TB * NC:
                    max1(TB * NC + k)
                attend1(k)
                if k in NM_AT:
                    pe.wait_ge(s_m8, 2 * TB * NC)
                    max1_rows(1, k - NM_AT[0])
                if k in OUT_T:
                    out_turn(OUT_T[k])
                for i in range(2):
                    if k - i in OUT_P:
                        project_out1(OUT_P[k - i], i)
                if k in OUT_XT:
                    transposes(2, OUT_XT[k])
            for g in range(GR // 2, GR):
                out_turn(g)
                for i in range(2):
                    project_out1(g, i)
            for g in range(GR // 2, GR):
                transposes(2, g)

            pe.wait_ge(s_a1e, OUT_JOB + 4 * GR)
            route(2, 1, LT1)

            def gate_up(n):
                g, e = divmod(n, EM)
                if n >= 2:
                    pe.wait_ge(s_gated, n - 1)
                for a, bk in enumerate((gate_banks[n % 2], up_banks[n % 2])):
                    product(bk, [(wgus[u][:, e, a, c, :], group(v, c, g))
                                 for c in range(NC) for u, v in RANDL]).then_inc(s_gu, 1)

            def down1(n):
                g, e = divmod(n, EM)
                pe.wait_ge(s_glo, n + 1)
                for t in range(4):
                    if n >= 1 and t % 2 == 0:
                        pe.wait_ge(s_acc1, 4 * (n - 1) + t + 2)
                    mm = product(down_banks[t // 2][:, t % 2 * D:t % 2 * D + D],
                                 [(gs[u][:, n % 3, t * P:t * P + P], wds[v][:, e, :]) for u, v in RANDL])
                    if t % 2 == 1:
                        mm.then_inc(s_dn1h, 1)
                return mm

            def conv(i):
                g, c = divmod(i, NC)
                if i >= 1:
                    pe.wait_ge(s_convc, i)
                first = PAD - (TAPS - 1) + HALF * (g % 2)
                product(ps[:, 7, :], [(diag[v][:, j * NC + c, :], XT[u][:, c, g // 2, first + j:first + j + HALF])
                                      for j in range(TAPS) for u, v in RANDL]).then_inc(s_conv, 1)

            def conv_turn(i):
                pe.wait_ge(s_convc, i + 1)
                if i == 0:
                    pe.wait_ge(s_rexp, 2)
                else:
                    pe.wait_ge(s_convfree, i)
                for t in range(4):
                    mm = nc.tensor.transpose(ps[:, 6, t * P:t * P + P], convT[:, i % 2, t * P:t * P + P], ident[:])
                mm.then_inc(s_convt, 1)

            pe.wait_ge(s_w3, 4)
            for n in range(GR * EM):
                gate_up(n)
                g, e = divmod(n, EM)
                if n == 0:
                    pe.wait_ge(s_w3d, 1)
                if e < NC:
                    conv(NC * g + e)
                if 1 <= e <= NC:
                    conv_turn(NC * g + e - 1)
                if n >= 1:
                    down1(n - 1)
            down1(GR * EM - 1)


def kernel(**inputs):
    import numpy as np
    import concourse.bacc as bacc
    from concourse.bass_utils import run_bass_kernel_spmd

    a = {k: np.asarray(v) for k, v in inputs.items()}

    def col(v):
        return np.ascontiguousarray(v.reshape(-1, P).T)

    def pairs(w):
        return w.reshape(NC, P, PAIRS, P).transpose(2, 1, 0, 3)

    def chunks(w):
        return w.reshape(NC, P, -1).transpose(1, 0, 2)

    wkv = a["L0_xattn_Wkv"]
    arrays = {
        "x": a["x"], "ctx": a["ctx_1024"],
        "ln1w": col(a["L0_xattn_ln1_w"]), "ln1b": col(a["L0_xattn_ln1_b"]),
        "ln2w": col(a["L0_xattn_ln2_w"]), "ln2b": col(a["L0_xattn_ln2_b"]),
        "wqk0": np.stack([pairs(a["L0_xattn_Wq"]), pairs(wkv[:, :1024])], axis=3),
        "wv0": chunks(wkv[:, 1024:]),
        "wo0": a["L0_xattn_Wo"].reshape(PAIRS, P, D),
        "wr": np.stack([chunks(a["L0_ffn_Wr"].T), chunks(a["L1_ffn_Wr"])], axis=1),
        "rbias": np.stack([a["L0_ffn_br"], a["L1_ffn_router_bias"]]),
        "w1": a["L0_ffn_W1"].reshape(E0, FC, P, NC, P).transpose(0, 4, 1, 3, 2).reshape(E0, P, FC, NC * P),
        "b1": a["L0_ffn_b1"].reshape(E0, FC, P).transpose(0, 2, 1),
        "w2": a["L0_ffn_W2"].reshape(E0, D, FC, P).transpose(0, 3, 2, 1),
        "b2": a["L0_ffn_b2"],
        "gb": np.stack([a["L0_ffn_gamma"], a["L0_ffn_beta"]]),
        "watt": np.stack([chunks(a["L1_xattn_W" + k].T) for k in "qkvo"], axis=1),
        "bqk1": np.stack([col(a["L1_xattn_b" + k]) for k in "qk"], axis=1),
        "bvo1": np.stack([a["L1_xattn_b" + k] for k in "vo"])[None],
        "wgu": np.stack([a["L1_ffn_Wg"], a["L1_ffn_Wu"]]).reshape(2, EM, NC, P, P).transpose(3, 1, 0, 2, 4),
        "wd": a["L1_ffn_Wd"].transpose(1, 0, 2),
        "convw": a["L1_ffn_conv_w"].reshape(TAPS, NC, P).transpose(2, 0, 1).reshape(P, TAPS * NC),
        "convb": col(a["L1_ffn_conv_b"]),
    }
    arrays = {k: np.ascontiguousarray(v) for k, v in arrays.items()}
    nc = bacc.Bacc("TRN2", target_bir_lowering=False, num_devices=1)
    args = [nc.dram_tensor(k, v.shape, mybir.dt.from_np(v.dtype), kind="ExternalInput").ap() for k, v in arrays.items()]
    out = nc.dram_tensor("out", (B, T, D), F32, kind="ExternalOutput").ap()
    program(nc, *args, out)
    r = run_bass_kernel_spmd(nc, [arrays], core_ids=[0])
    return r.results[0]["out"]
```
